# Optimizing a Trainium2 kernel written in Bass

```python
import numpy as np
import jax
import jax.numpy as jnp

def _softmax(x, axis=-1):
    return jax.nn.softmax(x, axis=axis)

def _gelu(x):
    return jax.nn.gelu(x, approximate=True)

def _silu(x):
    return jax.nn.silu(x)

def _sigmoid(x):
    return jax.nn.sigmoid(x)

def _layernorm(x, axis=-1, eps=1e-05):
    m = jnp.mean(x, axis=axis, keepdims=True)
    v = jnp.var(x, axis=axis, keepdims=True)
    return (x - m) / jnp.sqrt(v + eps)

def _scatter_add(tgt, idx, src, axis=0):
    return tgt.at[idx].add(src)

def _segment_sum(src, seg, n):
    return jax.ops.segment_sum(src, seg, n)
kernel_name = 'mk_decoder_postln_d1_seqx_r8_c15187'

def setup_inputs(seed: int=0):
    np.random.seed(seed)
    _w = jnp.asarray

    def _rec_inputs():
        import jax
        import jax.numpy as jnp
        _rk = jax.random.key(seed)
        x = 7.22e-05 + 1 * jax.random.normal(jax.random.fold_in(_rk, 1), (16, 256, 128), jnp.float32)
        _lenS = 256 - jax.random.randint(jax.random.fold_in(_rk, 7), (16,), 0, max(1, 256 // 4) + 1, jnp.int32)
        _lenS2 = 64 - jax.random.randint(jax.random.fold_in(_rk, 8), (16,), 0, max(1, 64 // 4) + 1, jnp.int32)
        _ctx_1024P = jax.random.normal(jax.random.fold_in(_rk, 11), (16, 16, 128), jnp.float32)
        _ctx_1024c = jax.random.dirichlet(jax.random.fold_in(_rk, 511), 0.3 * jnp.ones((16,), jnp.float32), (16, 64))
        _ctx_1024t = jnp.einsum('bsk,bkd->bsd', _ctx_1024c, _ctx_1024P)
        _ctx_1024t = _ctx_1024t * jax.lax.rsqrt(jnp.mean(jnp.square(_ctx_1024t)) + 1e-12) * 0.953939
        ctx_1024 = 4.13588e-05 + 0.999923 * (_ctx_1024t + 0.3 * jax.random.normal(jax.random.fold_in(_rk, 611), (16, 64, 128), jnp.float32))
        return (x, ctx_1024)
    x, ctx_1024 = _rec_inputs()

    def _L0_attn_setup():
        import math
        import jax, jax.numpy as jnp
        import numpy as np
        HEADS = 16
        DIM_HEAD = 64
        NUM_NULL_KV = 2
        ATTN_SCALE = 8.0
        LN_EPS = 1e-05

        def _alibi_slopes(heads):
            start = 2.0 ** (-2.0 ** (-(math.log2(heads) - 3.0)))
            return np.array([start * start ** i for i in range(heads)], dtype=np.float32)

        def _l2norm(t):
            return t / jnp.maximum(jnp.linalg.norm(t, axis=-1, keepdims=True), 1e-12)
        key = jax.random.key(seed)
        ks = jax.random.split(key, 5)
        b, n, dim = (4, 256, 128)
        return {'x': jax.random.normal(ks[0], (b, n, dim), dtype=jnp.float32), 'gamma': jnp.ones((dim,), dtype=jnp.float32), 'w_q': jax.random.normal(ks[1], (dim, HEADS * DIM_HEAD), dtype=jnp.float32) * 0.02, 'w_kv': jax.random.normal(ks[2], (dim, 2 * HEADS * DIM_HEAD), dtype=jnp.float32) * 0.02, 'null_kv': jax.random.normal(ks[3], (HEADS, 2 * NUM_NULL_KV, DIM_HEAD), dtype=jnp.float32), 'q_scale': jnp.ones((DIM_HEAD,), dtype=jnp.float32), 'k_scale': jnp.ones((DIM_HEAD,), dtype=jnp.float32), 'w_out': jax.random.normal(ks[4], (HEADS * DIM_HEAD, dim), dtype=jnp.float32) * 0.02}
    _L0_attn_all = _L0_attn_setup()
    _L0_attn_in = {k: v for k, v in _L0_attn_all.items() if k in ('gamma', 'w_q', 'w_kv', 'null_kv', 'q_scale', 'k_scale', 'w_out')}
    del _L0_attn_all

    def _L0_xattn_setup():
        import jax, jax.numpy as jnp
        import numpy as np
        B, SQ, SKV, E, H = (4, 256, 256, 128, 16)
        D = E // H
        key = jax.random.key(seed)
        ks = jax.random.split(key, 8)
        s = 1.0 / np.sqrt(D)
        return {'query': jax.random.normal(ks[0], (B, SQ, E), jnp.float32), 'key_value': jax.random.normal(ks[1], (B, SKV, E), jnp.float32), 'wq': jax.random.normal(ks[2], (H, D, D), jnp.float32) * s, 'bq': jnp.zeros((H, D), jnp.float32), 'wk': jax.random.normal(ks[3], (H, D, D), jnp.float32) * s, 'bk': jnp.zeros((H, D), jnp.float32), 'wv': jax.random.normal(ks[4], (H, D, D), jnp.float32) * s, 'bv': jnp.zeros((H, D), jnp.float32), 'wo': jax.random.normal(ks[5], (E, E), jnp.float32) * (1.0 / np.sqrt(E)), 'bo': jnp.zeros((E,), jnp.float32)}
    _L0_xattn_all = _L0_xattn_setup()
    _L0_xattn_in = {k: v for k, v in _L0_xattn_all.items() if k in ('wq', 'bq', 'wk', 'bk', 'wv', 'bv', 'wo', 'bo')}
    del _L0_xattn_all

    def _L0_ffn_setup():
        import jax, jax.numpy as jnp
        import numpy as np
        NUM_GEMMS = 8
        HIDDEN = 128
        INTER = 512
        key = jax.random.key(seed)
        k_x, k_w1, k_b1, k_w2, k_b2 = jax.random.split(key, 5)
        x = jax.random.normal(k_x, (8, 256, HIDDEN), dtype=jnp.float32)
        s1 = 1.0 / np.sqrt(HIDDEN)
        s2 = 1.0 / np.sqrt(INTER)
        W1 = jax.random.uniform(k_w1, (NUM_GEMMS, INTER, HIDDEN), jnp.float32, -s1, s1)
        b1 = jax.random.uniform(k_b1, (NUM_GEMMS, INTER), jnp.float32, -s1, s1)
        W2 = jax.random.uniform(k_w2, (NUM_GEMMS, HIDDEN, INTER), jnp.float32, -s2, s2)
        b2 = jax.random.uniform(k_b2, (NUM_GEMMS, HIDDEN), jnp.float32, -s2, s2)
        return {'x': x, 'W1': W1, 'b1': b1, 'W2': W2, 'b2': b2}
    _L0_ffn_all = _L0_ffn_setup()
    _L0_ffn_in = {k: v for k, v in _L0_ffn_all.items() if k in ('W1', 'b1', 'W2', 'b2')}
    del _L0_ffn_all
    return {'x': x, 'ctx_1024': ctx_1024, 'L0_attn_gamma': _L0_attn_in['gamma'], 'L0_attn_w_q': _L0_attn_in['w_q'], 'L0_attn_w_kv': _L0_attn_in['w_kv'], 'L0_attn_null_kv': _L0_attn_in['null_kv'], 'L0_attn_q_scale': _L0_attn_in['q_scale'], 'L0_attn_k_scale': _L0_attn_in['k_scale'], 'L0_attn_w_out': _L0_attn_in['w_out'], 'L0_xattn_wq': _L0_xattn_in['wq'], 'L0_xattn_bq': _L0_xattn_in['bq'], 'L0_xattn_wk': _L0_xattn_in['wk'], 'L0_xattn_bk': _L0_xattn_in['bk'], 'L0_xattn_wv': _L0_xattn_in['wv'], 'L0_xattn_bv': _L0_xattn_in['bv'], 'L0_xattn_wo': _L0_xattn_in['wo'], 'L0_xattn_bo': _L0_xattn_in['bo'], 'L0_ffn_W1': _L0_ffn_in['W1'], 'L0_ffn_b1': _L0_ffn_in['b1'], 'L0_ffn_W2': _L0_ffn_in['W2'], 'L0_ffn_b2': _L0_ffn_in['b2']}

def reference(x, ctx_1024, L0_attn_gamma, L0_attn_w_q, L0_attn_w_kv, L0_attn_null_kv, L0_attn_q_scale, L0_attn_k_scale, L0_attn_w_out, L0_xattn_wq, L0_xattn_bq, L0_xattn_wk, L0_xattn_bk, L0_xattn_wv, L0_xattn_bv, L0_xattn_wo, L0_xattn_bo, L0_ffn_W1, L0_ffn_b1, L0_ffn_W2, L0_ffn_b2):
    import jax
    import jax.numpy as jnp

    def _L0_attn_ref(x, gamma, w_q, w_kv, null_kv, q_scale, k_scale, w_out):
        import math
        import jax, jax.numpy as jnp
        import numpy as np
        HEADS = 16
        DIM_HEAD = 64
        NUM_NULL_KV = 2
        ATTN_SCALE = 8.0
        LN_EPS = 1e-05

        def _alibi_slopes(heads):
            start = 2.0 ** (-2.0 ** (-(math.log2(heads) - 3.0)))
            return np.array([start * start ** i for i in range(heads)], dtype=np.float32)

        def _l2norm(t):
            return t / jnp.maximum(jnp.linalg.norm(t, axis=-1, keepdims=True), 1e-12)
        b, n, dim = x.shape
        mu = jnp.mean(x, axis=-1, keepdims=True)
        var = jnp.mean(jnp.square(x - mu), axis=-1, keepdims=True)
        xn = (x - mu) * jax.lax.rsqrt(var + LN_EPS) * gamma
        q = (xn @ w_q).reshape(b, n, HEADS, DIM_HEAD).transpose(0, 2, 1, 3)
        kv = xn @ w_kv
        k, v = jnp.split(kv, 2, axis=-1)
        k = k.reshape(b, n, HEADS, DIM_HEAD).transpose(0, 2, 1, 3)
        v = v.reshape(b, n, HEADS, DIM_HEAD).transpose(0, 2, 1, 3)
        nkv = null_kv.reshape(HEADS, NUM_NULL_KV, 2, DIM_HEAD)
        nk = jnp.broadcast_to(nkv[:, :, 0][None], (b, HEADS, NUM_NULL_KV, DIM_HEAD))
        nv = jnp.broadcast_to(nkv[:, :, 1][None], (b, HEADS, NUM_NULL_KV, DIM_HEAD))
        k = jnp.concatenate([nk, k], axis=2)
        v = jnp.concatenate([nv, v], axis=2)
        q = _l2norm(q) * q_scale
        k = _l2norm(k) * k_scale
        sim = jnp.einsum('bhid,bhjd->bhij', q, k) * ATTN_SCALE
        j = n + NUM_NULL_KV
        rows = jnp.arange(n)
        cols = jnp.arange(j)
        dist = -jnp.abs(cols[None, :] - (rows[:, None] + NUM_NULL_KV)).astype(sim.dtype)
        slopes = jnp.asarray(_alibi_slopes(HEADS))
        sim = sim + dist[None, None] * slopes[None, :, None, None]
        causal_mask = cols[None, :] > rows[:, None] + NUM_NULL_KV
        neg = -jnp.finfo(sim.dtype).max
        sim = jnp.where(causal_mask[None, None], neg, sim)
        attn = jax.nn.softmax(sim, axis=-1)
        out = jnp.einsum('bhij,bhjd->bhid', attn, v)
        out = out.transpose(0, 2, 1, 3).reshape(b, n, HEADS * DIM_HEAD)
        return out @ w_out

    def _L0_xattn_ref(query, key_value, wq, bq, wk, bk, wv, bv, wo, bo):
        import jax, jax.numpy as jnp
        import numpy as np
        B, SQ, SKV, E, H = (4, 256, 256, 128, 16)
        D = E // H
        b, sq, e = query.shape
        skv = key_value.shape[1]
        h, d = (wq.shape[0], wq.shape[1])
        q = query.reshape(b, sq, h, d)
        kv = key_value.reshape(b, skv, h, d)
        qh = jnp.einsum('bshd,hed->bshe', q, wq) + bq
        kh = jnp.einsum('bthd,hed->bthe', kv, wk) + bk
        vh = jnp.einsum('bthd,hed->bthe', kv, wv) + bv
        scores = jnp.einsum('bshd,bthd->bhst', qh, kh) / jnp.sqrt(jnp.asarray(d, qh.dtype))
        attn = jax.nn.softmax(scores, axis=-1)
        ctx = jnp.einsum('bhst,bthd->bshd', attn, vh)
        out = ctx.reshape(b, sq, e)
        return out @ wo.T + bo

    def _L0_ffn_ref(x, W1, b1, W2, b2):
        import jax, jax.numpy as jnp
        import numpy as np
        NUM_GEMMS = 8
        HIDDEN = 128
        INTER = 512
        orig_shape = x.shape
        token_num = int(np.prod(orig_shape[:-1]))
        m = token_num // NUM_GEMMS
        xg = x.reshape(NUM_GEMMS, m, HIDDEN)
        h1 = jnp.einsum('gmh,goh->gmo', xg, W1) + b1[:, None, :]
        h2 = jnp.einsum('gmo,gho->gmh', h1, W2) + b2[:, None, :]
        return h2.reshape(orig_shape)
    x = _layernorm(x + _L0_attn_ref(x, L0_attn_gamma, L0_attn_w_q, L0_attn_w_kv, L0_attn_null_kv, L0_attn_q_scale, L0_attn_k_scale, L0_attn_w_out), axis=-1)
    x = _layernorm(x + _L0_xattn_ref(x, ctx_1024, L0_xattn_wq, L0_xattn_bq, L0_xattn_wk, L0_xattn_bk, L0_xattn_wv, L0_xattn_bv, L0_xattn_wo, L0_xattn_bo), axis=-1)
    x = _layernorm(x + _L0_ffn_ref(x, L0_ffn_W1, L0_ffn_b1, L0_ffn_W2, L0_ffn_b2), axis=-1)
    return x

_drawn_inputs = setup_inputs


def setup_inputs(seed=0):
    import zlib

    import numpy as np

    out = dict(_drawn_inputs(seed))
    spreads = {'L0_attn_gamma': (1.0, 0.6),
     'L0_attn_q_scale': (1.0, 0.6),
     'L0_attn_k_scale': (1.0, 0.6),
     'L0_xattn_bq': (0.0, 0.1),
     'L0_xattn_bk': (0.0, 0.8),
     'L0_xattn_bv': (0.0, 0.1),
     'L0_xattn_bo': (0.0, 0.1)}
    factors = {}
    for name, (base, spread) in spreads.items():
        noise = np.random.default_rng([zlib.crc32(name.encode()), seed]).standard_normal(out[name].shape)
        drawn = base * np.exp(spread * noise) if base else spread * noise
        out[name] = jnp.asarray(drawn.astype(out[name].dtype))
    for name, factor in factors.items():
        out[name] = (out[name] * factor).astype(out[name].dtype)
    return out
```

```python
import math
from contextlib import ExitStack

import numpy as np
import concourse.bass as bass
from concourse import mybir

F32 = mybir.dt.float32
F32R = mybir.dt.float32r
ALU = mybir.AluOpType
ACT = mybir.ActivationFunctionType
AX = mybir.AxisListType

P = 128
NB, SEQ = 16, 256
NT = SEQ // P
H, DH = 16, 64
HP = H // 2
HD = H * DH
NULLS = 2
NN = H * NULLS
CTX = 64
XH, XD = 16, 8
GROUPS = 8
INTER = 512
OC = INTER // P
EPS = 1e-5
ATTN_SCALE = 8.0
SEED_SCALE = 65536.0
MASKED = 1e30

QK_CHUNKS = 8
V_CHUNKS = 8
PC = 12
TILE_PC = (4, 8)
XC = 4


def slopes():
    start = 2.0 ** (-2.0 ** (-(math.log2(H) - 3.0)))
    return np.array([start * start ** i for i in range(H)], dtype=np.float32)


class Steps:

    def __init__(self, sem):
        self.sem, self.n, self.offset = sem, 0, 0

    def mark(self, ins):
        ins.then_inc(self.sem, 1)
        self.n += 1

    def value(self):
        return self.n + self.offset

    def wait(self, eng):
        eng.wait_ge(self.sem, self.value())

    def enter_loop(self, i, per_turn):
        self.offset, self.before, self.per_turn = i * per_turn, self.n, per_turn

    def leave_loop(self, turns):
        assert self.n - self.before == self.per_turn, ("steps of a turn", self.n - self.before)
        self.n, self.offset = self.before + turns * self.per_turn, 0


def score_heads(t, c):
    n = 4 if t == 0 else 2
    return [2 * (n * (c // 2) + j) + c % 2 for j in range(n)]


def need(eng, sem, value):
    if not (isinstance(value, int) and value <= 0):
        eng.wait_ge(sem, value)


def program(nc, x, ctxT, gamma, w_q, w_kv, wqT, wvT, wout, nk, nvT, q_scale, k_scale,
            xwq, xwk, xwv, xbq, xbk, xbv, xwoT, xbo, w1b, w2T, b2, ident_in, dist_in, nullbias_in,
            hmask_in, out):
    with ExitStack() as ctx:
        def sb(name, shape, dt=F32):
            return ctx.enter_context(nc.sbuf_tensor(name, shape, dt))

        def sem(name):
            return ctx.enter_context(nc.semaphore(name))

        psS = [ctx.enter_context(nc.psum_tensor(f"psS{k}", [P, 512], F32)) for k in range(2)]
        psT = [ctx.enter_context(nc.psum_tensor(f"psT{k}", [P, 512], F32)) for k in range(2)]
        psJ = [ctx.enter_context(nc.psum_tensor(f"psJ{k}", [P, 512], F32)) for k in range(2)]
        psY = [ctx.enter_context(nc.psum_tensor(f"psY{k}", [P, 512], F32)) for k in range(2)]

        ident = sb("ident", [P, P])
        dist = sb("dist", [P, SEQ])
        alibi = sb("alibi", [P, H, SEQ])
        nullbias = sb("nullbias", [P, NT, NN])
        hmask = sb("hmask", [P, XH])
        gam = sb("gam", [P, 1])
        qks2 = sb("qks2", [P, 2])
        kscale = sb("kscale", [P, 1])
        wqk_hi = sb("wqk_hi", [P, 2 * HD], F32R)
        wqk_lo = sb("wqk_lo", [P, 2 * HD], F32R)
        wn_hi = sb("wn_hi", [P, NN], F32R)
        wn_lo = sb("wn_lo", [P, NN], F32R)
        m_hi = sb("m_hi", [P, H * P], F32R)
        m_lo = sb("m_lo", [P, H * P], F32R)
        null_v = sb("null_v", [NN, P])
        nkrow = sb("nkrow", [NN, 2 * DH])
        nksc = sb("nksc", [NN, 2 * DH])
        nksq = sb("nksq", [NN, DH])
        nkst = sb("nkst", [NN, 8])
        nkT = sb("nkT", [P, NN])
        xw = sb("xw", [P, 3, P])
        xb = sb("xb", [P, 3])
        xwo = sb("xwo", [P, P])
        bo = sb("bo", [P, P])
        kTx = sb("kTx", [P, NB * CTX])
        vTx = sb("vTx", [P, NB * CTX])
        w1s = sb("w1s", [P, OC, P + 1])
        w2s = sb("w2s", [P, OC, P])
        b2s = sb("b2s", [P, 1])
        w12raw = sb("w12raw", [P, 2, P])
        w12 = sb("w12", [P, 2, P])
        xin = sb("xin", [P, NT, P])
        xn = sb("xn", [P, NT, P])
        xnT_hi = sb("xnT_hi", [P, SEQ], F32R)
        xnT_lo = sb("xnT_lo", [P, SEQ], F32R)
        qk = [sb(f"qk{t}", [P, 2 * HD]) for t in range(NT)]
        sq = sb("sq", [P, 2 * HD])
        ssq = sb("ssq", [P, NT, 2 * H])
        lnq = sb("lnq", [P, NT, 2 * H])
        seedq = sb("seedq", [P, NT, 2 * H])
        newt = sb("newt", [P, NT, 2 * H])
        rn = sb("rn", [P, NT, 2 * H])
        nullraw = sb("nullraw", [P, NT, NN])
        nullmul = sb("nullmul", [P, NT, NN])
        nullneg = sb("nullneg", [P, NT, NN])
        nullmin = sb("nullmin", [P, NT, H])
        qT = sb("qT", [P, HP, SEQ])
        kT = sb("kT", [P, HP, SEQ])
        val = sb("val", [P, NT, H * P])
        xres = sb("xres", [P, NT, P])
        pr = [sb(f"pr{t}", [P, H, P * (t + 1)]) for t in range(NT)]
        nmin = sb("nmin", [P, NT, H])
        nulld = sb("nulld", [P, NT, NN])
        dparts = sb("dparts", [P, NT, H, 1 + NULLS])
        den = sb("den", [P, NT, H])
        rden = sb("rden", [P, NT, H])
        pnn = sb("pnn", [P, NT, NN])
        pnT = sb("pnT", [NN, NT, P])
        pT = [sb(f"pT{k}", [P, 512]) for k in range(4)]
        r1 = sb("r1", [P, NT, P])
        x1 = sb("x1", [P, NT, P])
        x1b = sb("x1b", [P, NT, P])
        x1T = sb("x1T", [P, SEQ])
        xqT = sb("xqT", [P, SEQ])
        kexp = sb("kexp", [P, XH, CTX])
        vexp = sb("vexp", [P, XH, CTX])
        xv = sb("xv", [P, XH // 2, P])
        xmax = sb("xmax", [P, NT, XH])
        xp = [sb(f"xp{t}", [P, XH, CTX]) for t in range(NT)]
        xden = sb("xden", [P, NT, XH])
        xrden = sb("xrden", [P, NT, XH])
        xpT = [sb(f"xpT{k}", [P, 512]) for k in range(2)]
        r2 = sb("r2", [P, NT, P])
        x2 = sb("x2", [P, NT, P])
        x2b = sb("x2b", [P, NT, P])
        x2T = sb("x2T", [P, SEQ])
        r3 = sb("r3", [P, NT, P])
        x3 = sb("x3", [P, NT, P])
        LN = ("ln1", "ln2", "ln3", "ln4")
        st = {n: sb(f"{n}_st", [P, NT, 6]) for n in LN}
        mv = {n: sb(f"{n}_mv", [P, NT, 2]) for n in LN}
        ve = {n: sb(f"{n}_ve", [P, NT]) for n in LN}
        lv = {n: sb(f"{n}_lv", [P, NT]) for n in LN}
        sd = {n: sb(f"{n}_sd", [P, NT]) for n in LN}
        nw = {n: sb(f"{n}_nw", [P, NT]) for n in LN}
        rs = {n: sb(f"{n}_rs", [P, NT]) for n in LN}

        wqk_raw = pr[1][:, 0:8, :].rearrange("p h k -> p (h k)")
        wqT_s = qk[0][:, 0:HD].rearrange("p (c d) -> p c d", c=HP)
        wvT_s = qk[0][:, HD:2 * HD].rearrange("p (c d) -> p c d", c=HP)
        wout_s = qk[1][:, 0:HD].rearrange("p (c d) -> p c d", c=HP)
        nvT_s = qk[1][:, HD:HD + HP * NN].rearrange("p (c n) -> p c n", c=HP)
        ctxT_s = xp[0][:].rearrange("p h k -> p (h k)")

        c_loaded = sem("c_loaded")
        h_loaded = sem("h_loaded")
        a_loaded = sem("a_loaded")
        g_loaded = sem("g_loaded")
        xin_loaded = sem("xin_loaded")
        xres_loaded = sem("xres_loaded")
        ffn_loaded = sem("ffn_loaded")
        stored = sem("stored")
        nkT_ready = sem("nkT_ready")
        wn_ready = sem("wn_ready")
        m_ready = sem("m_ready")
        nullv_ready = sem("nullv_ready")
        kvx_ready = sem("kvx_ready")
        xnT_ready = sem("xnT_ready")
        qk_ready = sem("qk_ready")
        nullraw_ready = sem("nullraw_ready")
        qkT_ready = sem("qkT_ready")
        v_ready = sem("v_ready")
        scores_ready = sem("scores_ready")
        nullT_ready = sem("nullT_ready")
        probsT_ready = sem("probsT_ready")
        pv_done = sem("pv_done")
        y_ready = sem("y_ready")
        x1T_ready = sem("x1T_ready")
        xqT_ready = sem("xqT_ready")
        xscores_ready = sem("xscores_ready")
        xv_ready = sem("xv_ready")
        w12raw_ready = sem("w12raw_ready")
        w12_ready = sem("w12_ready")
        xprobsT_ready = sem("xprobsT_ready")
        xpv_done = sem("xpv_done")
        y2_ready = sem("y2_ready")
        x2T_ready = sem("x2T_ready")
        h2_ready = sem("h2_ready")
        dve_step = sem("dve_step")
        kscale_ready = sem("kscale_ready")
        nkssq_ready = sem("nkssq_ready")
        nkrow_ready = sem("nkrow_ready")
        wsplit_ready = sem("wsplit_ready")
        wn_split = sem("wn_split")
        m_split = sem("m_split")
        nullv_copied = sem("nullv_copied")
        alibi_ready = sem("alibi_ready")
        xn_ready = sem("xn_ready")
        xnT_split = sem("xnT_split")
        ssq_ready = sem("ssq_ready")
        rn_ready = sem("rn_ready")
        qT_copied = sem("qT_copied")
        scores_masked = sem("scores_masked")
        nulld_ready = sem("nulld_ready")
        rden_ready = sem("rden_ready")
        pnn_ready = sem("pnn_ready")
        pT_copied_dve = sem("pT_copied_dve")
        y_added = sem("y_added")
        x1_ready = sem("x1_ready")
        xs_sub = sem("xs_sub")
        xrden_ready = sem("xrden_ready")
        y2_added = sem("y2_added")
        x2_ready = sem("x2_ready")
        h2_added = sem("h2_added")
        x3_ready = sem("x3_ready")
        var_ready = {n: sem(f"{n}_var_ready") for n in LN}
        act_step = sem("act_step")
        nkseed_ready = sem("nkseed_ready")
        nkT_copied = sem("nkT_copied")
        kvx_copied = sem("kvx_copied")
        seed_ready = {n: sem(f"{n}_seed_ready") for n in LN}
        qk_squared = sem("qk_squared")
        qkseed_ready = sem("qkseed_ready")
        nullraw_copied = sem("nullraw_copied")
        kT_copied = sem("kT_copied")
        v_copied = sem("v_copied")
        exp_done = sem("exp_done")
        pn_ready = sem("pn_ready")
        pnT_copied = sem("pnT_copied")
        pT_copied_act = sem("pT_copied_act")
        x1T_copied = sem("x1T_copied")
        xqT_copied = sem("xqT_copied")
        xexp_done = sem("xexp_done")
        xv_copied = sem("xv_copied")
        w12raw_copied = sem("w12raw_copied")
        w12_copied = sem("w12_copied")
        xpT_copied = sem("xpT_copied")
        x2T_copied = sem("x2T_copied")
        qk_normed = sem("qk_normed")
        probs_normed = sem("probs_normed")
        xprobs_normed = sem("xprobs_normed")
        kexp_ready = sem("kexp_ready")
        vexp_ready = sem("vexp_ready")

        x_dram = x.rearrange("b (t p) d -> p b t d", p=P)
        out_dram = out.rearrange("b (t p) d -> p b t d", p=P)
        w1_dram = w1b.rearrange("g (c p) h -> p g c h", p=P)
        w2_dram = w2T.rearrange("g (c p) h -> p g c h", p=P)

        FIRST = 3
        TURNS = (NB - 1 - FIRST) // 2

        def schedule(eng, iteration, steps=None, per_turn=0):
            for i in range(FIRST):
                iteration(i, True, i >= 1, i % 2 == 1, (i - 1) // 2)
            with eng.Fori(0, TURNS) as turn:
                if steps:
                    steps.enter_loop(turn, per_turn)
                for half in range(2):
                    iteration(2 * turn + (FIRST + half), True, True, half == 0, turn + (FIRST - 1) // 2)
            if steps:
                steps.leave_loop(TURNS)
            iteration(NB - 1, False, True, (NB - 1) % 2 == 1, (NB - 2) // 2)

        block = ctx.enter_context(nc.Block())

        @block.sync
        def _(sp):
            sp.dma_start(xin[:], x_dram[:, 0]).then_inc(xin_loaded, 16)
            sp.dma_start(ident[:], ident_in).then_inc(c_loaded, 16)
            sp.dma_start(gam[:], gamma).then_inc(c_loaded, 16)
            sp.dma_start(wqk_raw[:, 0:HD], w_q).then_inc(c_loaded, 16)
            sp.dma_start(wqk_raw[:, HD:2 * HD], w_kv[:, 0:HD]).then_inc(c_loaded, 16)
            for half in range(2):
                sp.dma_start(qks2[half * DH:(half + 1) * DH, 0:1], q_scale).then_inc(c_loaded, 16)
                sp.dma_start(qks2[half * DH:(half + 1) * DH, 1:2], k_scale).then_inc(c_loaded, 16)
            sp.dma_start(nkrow[:, 0:DH], nk).then_inc(h_loaded, 16)
            sp.dma_start(nksc[:, 0:DH], q_scale.rearrange("d a -> a d").broadcast_to([NN, DH])).then_inc(h_loaded, 16)
            sp.dma_start(nksc[:, DH:2 * DH], k_scale.rearrange("d a -> a d").broadcast_to([NN, DH])).then_inc(h_loaded, 16)
            sp.dma_start(wqT_s, wqT).then_inc(h_loaded, 16)
            sp.dma_start(wvT_s, wvT).then_inc(h_loaded, 16)
            sp.dma_start(wout_s, wout).then_inc(h_loaded, 16)
            sp.dma_start(nvT_s, nvT).then_inc(h_loaded, 16)
            sp.dma_start(dist[:], dist_in).then_inc(a_loaded, 16)
            sp.dma_start(nullbias[:], nullbias_in).then_inc(a_loaded, 16)
            sp.dma_start(xres[:], x_dram[:, 0]).then_inc(xres_loaded, 16)
            sp.dma_start(ctxT_s, ctxT).then_inc(g_loaded, 16)
            sp.dma_start(hmask[:], hmask_in).then_inc(g_loaded, 16)
            for k, (w, b) in enumerate(((xwq, xbq), (xwk, xbk), (xwv, xbv))):
                sp.dma_start(xw[:, k, :], w).then_inc(g_loaded, 16)
                sp.dma_start(xb[:, k:k + 1], b).then_inc(g_loaded, 16)
            sp.dma_start(xwo[:], xwoT).then_inc(g_loaded, 16)
            sp.dma_start(bo[:], xbo.broadcast_to([P, P])).then_inc(g_loaded, 16)

            def ffn_load(g):
                sp.dma_start(w1s[:], w1_dram[:, g]).then_inc(ffn_loaded, 16)
                sp.dma_start(w2s[:], w2_dram[:, g]).then_inc(ffn_loaded, 16)
                sp.dma_start(b2s[:], b2[g]).then_inc(ffn_loaded, 16)

            ffn_load(0)

            def iteration(i, a, c, w, g):
                if a:
                    sp.wait_ge(xn_ready, i + 1)
                    sp.dma_start(xin[:], x_dram[:, i + 1]).then_inc(xin_loaded, 16)
                if w and not (isinstance(g, int) and g + 1 >= GROUPS):
                    sp.wait_ge(w12raw_ready, g + 1)
                    sp.wait_ge(w12raw_copied, 2 * g + 2)
                    ffn_load(g + 1)
                if c:
                    sp.wait_ge(x3_ready, i)
                    sp.dma_start(out_dram[:, i - 1], x3[:]).then_inc(stored, 16)
                if a:
                    sp.wait_ge(y_added, NT * (i + 1))
                    sp.dma_start(xres[:], x_dram[:, i + 1]).then_inc(xres_loaded, 16)

            schedule(sp, iteration)
            sp.wait_ge(x3_ready, NB)
            sp.dma_start(out_dram[:, NB - 1], x3[:]).then_inc(stored, 16)
            sp.wait_ge(stored, 16 * NB)

        @block.tensor
        def _(pe):
            j_read = [None, None]

            def take(bank, read_by, value):
                if j_read[bank] is not None:
                    need(pe, *j_read[bank])
                j_read[bank] = (read_by, value)

            def split_product(dst, hi, lo, whi, wlo):
                pe.matmul(dst, hi, whi, start=True, stop=False)
                pe.matmul(dst, hi, wlo, start=False, stop=False)
                return pe.matmul(dst, lo, whi, start=False, stop=True)

            def null_keys():
                pe.wait_ge(c_loaded, 16 * 8)
                pe.wait_ge(nkrow_ready, 1)
                take(0, nkT_copied, 1)
                pe.transpose(psJ[0][:, 0:NN], nkrow[:], ident[0:NN, 0:NN]).then_inc(nkT_ready, 1)
                pe.wait_ge(h_loaded, 16 * 7)
                take(0, wn_split, 1)
                take(1, wn_split, 1)
                for h in list(range(0, H, 2)) + list(range(1, H, 2)):
                    r = slice(DH * (h % 2), DH * (h % 2) + DH)
                    mm = pe.matmul(psJ[h % 2][:, NULLS * (h // 2):NULLS * (h // 2 + 1)], wqT_s[r, h // 2, :],
                                   nkT[r, NULLS * h:NULLS * (h + 1)], start=True, stop=True)
                mm.then_inc(wn_ready, 1)

            def merged_values():
                for c in range(H // 4):
                    take(c % 2, m_split, c + 1)
                    for j, h in enumerate(score_heads(0, c)):
                        r = slice(DH * (h % 2), DH * (h % 2) + DH)
                        mm = pe.matmul(psJ[c % 2][:, P * j:P * (j + 1)], wvT_s[r, h // 2, :],
                                       wout_s[r, h // 2, :], start=True, stop=True)
                    mm.then_inc(m_ready, 1)
                take(0, nullv_copied, 1)
                for p in range(HP):
                    mm = pe.matmul(psJ[0][0:NN, 0:P], nvT_s[:, p, :], wout_s[:, p, :],
                                   start=(p == 0), stop=(p == HP - 1))
                mm.then_inc(nullv_ready, 1)

            def context_kv():
                pe.wait_ge(g_loaded, 16 * 10)
                for k in range(4):
                    take((k + 1) % 2, kvx_copied, k + 1)
                    pe.matmul(psJ[(k + 1) % 2][:], xw[:, 1 + k // 2, :], ctxT_s[:, 512 * (k % 2):512 * (k % 2) + 512],
                              start=True, stop=True).then_inc(kvx_ready, 1)

            def xn_turn(n):
                pe.wait_ge(xn_ready, n + 1)
                take(0, xnT_split, n + 1)
                for t in range(NT):
                    mm = pe.transpose(psJ[0][:, P * t:P * (t + 1)], xn[:, t, :], ident[:])
                mm.then_inc(xnT_ready, 1)

            def project_qk(n):
                pe.wait_ge(xnT_split, n + 1)
                for c in range(QK_CHUNKS):
                    t, j = c // 4, c % 4
                    take(c % 2, qk_squared, QK_CHUNKS * n + c + 1)
                    tok, col = slice(P * t, P * (t + 1)), slice(512 * j, 512 * (j + 1))
                    split_product(psJ[c % 2][:], xnT_hi[:, tok], xnT_lo[:, tok],
                                  wqk_hi[:, col], wqk_lo[:, col]).then_inc(qk_ready, 1)
                take(0, nullraw_copied, n + 1)
                for t in range(NT):
                    tok = slice(P * t, P * (t + 1))
                    mm = split_product(psJ[0][:, NN * t:NN * (t + 1)], xnT_hi[:, tok], xnT_lo[:, tok],
                                       wn_hi[:], wn_lo[:])
                mm.then_inc(nullraw_ready, 1)

            def project_v(n):
                for c in range(V_CHUNKS):
                    t, j = c // 4, c % 4
                    take(c % 2, v_copied, V_CHUNKS * n + c + 1)
                    tok, col = slice(P * t, P * (t + 1)), slice(512 * j, 512 * (j + 1))
                    split_product(psJ[c % 2][:], xnT_hi[:, tok], xnT_lo[:, tok],
                                  m_hi[:, col], m_lo[:, col]).then_inc(v_ready, 1)

            def turn_qk(n):
                for c in range(2 * NT * 2):
                    t, half, isk = c // 4, (c // 2) % 2, c % 2
                    if half == 0:
                        pe.wait_ge(qk_normed, 2 * NT * n + 2 * t + isk + 1)
                    take(isk, kT_copied if isk else qT_copied, 2 * NT * n + c // 2 + 1)
                    for j in range(4):
                        col = HD * isk + P * (4 * half + j)
                        mm = pe.transpose(psJ[isk][:, P * j:P * (j + 1)], qk[t][:, col:col + P], ident[:])
                    mm.then_inc(qkT_ready, 1)

            def scores(b, t, c):
                heads, keys = (4, P) if t == 0 else (2, SEQ)
                half = score_heads(t, c)[0] // HP
                pe.wait_ge(qT_copied, 2 * NT * b + 2 * t + half + 1)
                pe.wait_ge(kT_copied, 2 * NT * b + 2 * t + half + 1)
                before = 4 * c if t == 0 else H + 2 * c
                k = c % 2
                if t == 1 or c >= 2:
                    pe.wait_ge(scores_masked, NT * H * b + before - (heads if (t == 0 or c >= 1) else 4))
                for j, h in enumerate(score_heads(t, c)):
                    r = slice(DH * (h % 2), DH * (h % 2) + DH)
                    mm = pe.matmul(psS[k][:, keys * j:keys * (j + 1)], qT[r, h // 2, P * t:P * (t + 1)],
                                   kT[r, h // 2, 0:keys], start=True, stop=True)
                mm.then_inc(scores_ready, 1)

            def evacuated(b, c):
                if c % 2 == 0:
                    pe.wait_ge(pT_copied_dve, (PC // 2) * b + c // 2 + 1)
                else:
                    pe.wait_ge(pT_copied_act, (PC // 2) * b + c // 2 + 1)

            def turn_probs(b, t, c):
                pe.wait_ge(probs_normed, PC * b + c + 1)
                for j in range(4):
                    blk = 4 * (c - (0 if t == 0 else TILE_PC[0])) + j
                    h, kt = blk // (t + 1), blk % (t + 1)
                    mm = pe.transpose(psT[c % 2][:, P * j:P * (j + 1)], pr[t][:, h, P * kt:P * (kt + 1)], ident[:])
                mm.then_inc(probsT_ready, 1)

            def weigh_values(b, t, c):
                first = 0 if t == 0 else TILE_PC[0]
                for j in range(4):
                    blk = 4 * (c - first) + j
                    h, kt = blk // (t + 1), blk % (t + 1)
                    mm = pe.matmul(psY[t][:, 0:P], pT[c % 4][:, P * j:P * (j + 1)], val[:, kt, P * h:P * (h + 1)],
                                   start=(blk == 0), stop=False)
                mm.then_inc(pv_done, 1)

            def attend(b, t, between):
                first, last = (0, 4) if t == 0 else (4, PC)
                if t == 0:
                    pe.wait_ge(v_copied, V_CHUNKS * (b + 1))
                pe.wait_ge(pnn_ready, NT * b + t + 1)
                take(1, pnT_copied, NT * b + t + 1)
                pe.transpose(psJ[1][0:NN, 0:P], pnn[:, t, :], ident[:]).then_inc(nullT_ready, 1)
                for c in range(first, last + 2):
                    if c - 2 >= first:
                        evacuated(b, c - 2)
                    if c < last:
                        turn_probs(b, t, c)
                    if c - 2 >= first:
                        weigh_values(b, t, c - 2)
                        if c - 2 in between:
                            between[c - 2]()
                pe.wait_ge(pnT_copied, NT * b + t + 1)
                pe.matmul(psY[t][:, 0:P], pnT[:, t, :], null_v[:], start=False, stop=True).then_inc(y_ready, 1)

            def x1_turn(b):
                pe.wait_ge(x1_ready, NT * (b + 1))
                take(1, x1T_copied, b + 1)
                for t in range(NT):
                    mm = pe.transpose(psJ[1][:, P * t:P * (t + 1)], x1[:, t, :], ident[:])
                mm.then_inc(x1T_ready, 1)

            def cross_q(b):
                pe.wait_ge(x1T_copied, b + 1)
                take(0, xqT_copied, b + 1)
                pe.matmul(psJ[0][:, 0:SEQ], xw[:, 0, :], x1T[:], start=True, stop=True).then_inc(xqT_ready, 1)

            def cross_scores(b):
                pe.wait_ge(xqT_copied, b + 1)
                pe.wait_ge(kexp_ready, b + 1)
                for k in range(XC):
                    t, half = k // 2, k % 2
                    if k < 2:
                        pass
                    else:
                        pe.wait_ge(xs_sub, XC * b + k - 1)
                    pe.matmul(psS[k % 2][:], xqT[:, P * t:P * (t + 1)],
                              kexp[:, 8 * half:8 * half + 8, :].rearrange("p h k -> p (h k)"),
                              start=True, stop=True).then_inc(xscores_ready, 1)

            def cross_values(b):
                pe.wait_ge(vexp_ready, b + 1)
                for c in range(2):
                    take(c, xv_copied, 2 * b + c + 1)
                    for j in range(4):
                        p = 4 * c + j
                        mm = pe.matmul(psJ[c][:, P * j:P * (j + 1)],
                                       vexp[:, 2 * p:2 * p + 2, :].rearrange("p h k -> p (h k)"), xwo[:],
                                       start=True, stop=True)
                    mm.then_inc(xv_ready, 1)

            def merge_ffn(g):
                pe.wait_ge(ffn_loaded, 48 * (g + 1))
                take(0, w12raw_copied, 2 * g + 2)
                for c in range(OC):
                    mm = pe.matmul(psJ[0][:, 0:P + 1], w2s[:, c, :], w1s[:, c, :], start=(c == 0), stop=(c == OC - 1))
                mm.then_inc(w12raw_ready, 1)
                pe.wait_ge(w12raw_copied, 2 * g + 2)
                take(1, w12_copied, g + 1)
                for k in range(2):
                    mm = pe.transpose(psJ[1][:, P * k:P * (k + 1)], w12raw[:, k, :], ident[:])
                mm.then_inc(w12_ready, 1)

            def cross_attend(b, batch_b):
                if batch_b is not None:
                    pe.wait_ge(y_added, NT * batch_b + 1)
                pe.wait_ge(xv_copied, 2 * (b + 1))
                for k in range(XC + 2):
                    if k >= 2:
                        pe.wait_ge(xpT_copied, XC * b + k - 1)
                    if k < XC:
                        pe.wait_ge(xprobs_normed, NT * b + k // 2 + 1)
                        t, half = k // 2, k % 2
                        for j in range(4):
                            p = 4 * half + j
                            mm = pe.transpose(psT[k % 2][:, P * j:P * (j + 1)],
                                              xp[t][:, 2 * p:2 * p + 2, :].rearrange("p h k -> p (h k)"), ident[:])
                        mm.then_inc(xprobsT_ready, 1)
                    if k >= 2:
                        t, half = (k - 2) // 2, k % 2
                        for j in range(4):
                            mm = pe.matmul(psY[0][:, P * t:P * (t + 1)], xpT[k % 2][:, P * j:P * (j + 1)],
                                           xv[:, 4 * half + j, :], start=(half == 0 and j == 0),
                                           stop=(half == 1 and j == 3))
                        mm.then_inc(xpv_done, 1)

            def x2_turn(b):
                pe.wait_ge(x2_ready, b + 1)
                take(0, x2T_copied, b + 1)
                for t in range(NT):
                    mm = pe.transpose(psJ[0][:, P * t:P * (t + 1)], x2[:, t, :], ident[:])
                mm.then_inc(x2T_ready, 1)

            def feed_forward(b, g):
                pe.wait_ge(x2T_copied, b + 1)
                pe.wait_ge(w12_copied, g + 1)
                pe.wait_ge(y2_added, b + 1)
                for t in range(NT):
                    mm = pe.matmul(psY[0][:, P * t:P * (t + 1)], x2T[:, P * t:P * (t + 1)], w12[:, 0, :],
                                   start=True, stop=True)
                mm.then_inc(h2_ready, 1)

            null_keys()
            xn_turn(0)
            pe.wait_ge(wsplit_ready, 1)
            pe.wait_ge(wn_split, 1)
            merged_values()
            context_kv()
            project_qk(0)
            project_v(0)
            turn_qk(0)

            def iteration(i, a, c, w, g):
                j_read[0], j_read[1] = (qT_copied, 2 * NT * (i + 1)), (kT_copied, 2 * NT * (i + 1))
                for k in range(4):
                    scores(i, 0, k)
                for k in range(8):
                    scores(i, 1, k)
                    if k == 1:
                        if a:
                            xn_turn(i + 1)
                        if c:
                            x1_turn(i - 1)
                    if k == 4 and c:
                        cross_q(i - 1)
                if c:
                    pe.wait_ge(scores_masked, NT * H * (i + 1))
                    cross_scores(i - 1)
                if a:
                    project_qk(i + 1)
                if c:
                    cross_values(i - 1)
                    if w:
                        merge_ffn(g)
                attend(i, 0, {})
                if c:
                    cross_attend(i - 1, i)
                    y2_tail()
                between = {}
                if c:
                    between = {7: lambda: x2_turn(i - 1), 9: lambda: feed_forward(i - 1, g)}
                attend(i, 1, between)
                if a:
                    project_v(i + 1)
                    turn_qk(i + 1)

            def y2_tail():
                pass

            schedule(pe, iteration)
            j_read[0] = j_read[1] = None
            b = NB - 1
            x1_turn(b)
            cross_q(b)
            cross_scores(b)
            cross_values(b)
            cross_attend(b, None)
            x2_turn(b)
            feed_forward(b, GROUPS - 1)

        @block.vector
        def _(dve):
            steps = Steps(dve_step)

            def wait_apart(semaphore, value):
                if not isinstance(value, int):
                    value = dve.to_reg(value)
                dve.wait_ge(xin_loaded, 16)
                dve.wait_ge(semaphore, value)

            def ln_begin(name, src, tiles, count):
                for t in tiles:
                    steps.mark(dve.bn_stats(st[name][:, t, :], src[:, t, :]))
                wait_apart(dve_step, steps.value())
                for t in tiles:
                    steps.mark(dve.bn_aggr(mv[name][:, t, :], st[name][:, t, :]))
                steps.wait(dve)
                a, z = tiles[0], tiles[-1] + 1
                dve.tensor_scalar(ve[name][:, a:z], mv[name][:, a:z, 1], EPS, None, ALU.add).then_inc(var_ready[name], 1)

            def newton(y0, v, tmp, res, half):
                steps.mark(dve.tensor_tensor(tmp, y0, y0, ALU.mult))
                steps.wait(dve)
                steps.mark(dve.scalar_tensor_tensor(out=tmp, in0=tmp, scalar=-half, in1=v, op0=ALU.mult, op1=ALU.mult))
                steps.wait(dve)
                return dve.scalar_tensor_tensor(out=res, in0=tmp, scalar=1.5, in1=y0, op0=ALU.add, op1=ALU.mult)

            def ln_end(name, src, dst, tiles, count):
                dve.wait_ge(seed_ready[name], count)
                a, z = tiles[0], tiles[-1] + 1
                steps.mark(newton(sd[name][:, a:z], ve[name][:, a:z], nw[name][:, a:z], rs[name][:, a:z], 0.5))
                steps.wait(dve)
                for t in tiles:
                    last = dve.tensor_scalar(dst[:, t, :], src[:, t, :], mv[name][:, t, 0:1], rs[name][:, t:t + 1],
                                             ALU.subtract, ALU.mult)
                    if t != tiles[-1]:
                        steps.mark(last)
                return last

            def scale_rows():
                dve.wait_ge(c_loaded, 16 * 8)
                dve.scalar_tensor_tensor(out=kscale[:], in0=qks2[:, 0:1], scalar=-ATTN_SCALE * SEED_SCALE,
                                         in1=qks2[:, 1:2], op0=ALU.mult, op1=ALU.mult).then_inc(kscale_ready, 1)

            def split_wqk():
                steps.mark(dve.tensor_copy(wqk_hi[:], wqk_raw))
                steps.wait(dve)
                dve.tensor_tensor(wqk_lo[:], wqk_raw, wqk_hi[:].bitcast(F32), ALU.subtract).then_inc(wsplit_ready, 1)

            def norm_null_keys():
                dve.wait_ge(h_loaded, 16 * 7)
                steps.mark(dve.tensor_tensor(nksq[:], nkrow[:, 0:DH], nkrow[:, 0:DH], ALU.mult))
                steps.mark(dve.scalar_tensor_tensor(out=nksc[:, 0:DH], in0=nksc[:, 0:DH],
                                                    scalar=-ATTN_SCALE * SEED_SCALE, in1=nksc[:, DH:2 * DH],
                                                    op0=ALU.mult, op1=ALU.mult))
                steps.wait(dve)
                steps.mark(dve.tensor_reduce(nkst[:, 0:1], nksq[:], AX.X, ALU.add))
                steps.wait(dve)
                dve.tensor_scalar(nkst[:, 1:2], nkst[:, 0:1], 1e-24, None, ALU.max).then_inc(nkssq_ready, 1)
                dve.wait_ge(nkseed_ready, 1)
                steps.mark(newton(nkst[:, 3:4], nkst[:, 1:2], nkst[:, 4:5], nkst[:, 5:6], 0.5 * SEED_SCALE))
                steps.wait(dve)
                steps.mark(dve.scalar_tensor_tensor(out=nkrow[:, 0:DH], in0=nkrow[:, 0:DH], scalar=nkst[:, 5:6],
                                                    in1=nksc[:, 0:DH], op0=ALU.mult, op1=ALU.mult))
                steps.wait(dve)
                dve.tensor_copy(nkrow[:, DH:2 * DH], nkrow[:, 0:DH]).then_inc(nkrow_ready, 1)

            def split_wn():
                dve.wait_ge(wn_ready, 1)
                hi, lo = (w[:].rearrange("p (c r n) -> p c r n", r=2, n=NULLS) for w in (wn_hi, wn_lo))
                ps = [psJ[r][:, 0:NN // 2].rearrange("p (c n) -> p c n", n=NULLS) for r in range(2)]
                for r in range(2):
                    steps.mark(dve.tensor_copy(hi[:, :, r, :], ps[r]))
                steps.wait(dve)
                for r in range(2):
                    last = dve.tensor_tensor(lo[:, :, r, :], ps[r], hi[:, :, r, :].bitcast(F32), ALU.subtract)
                    if r == 0:
                        steps.mark(last)
                last.then_inc(wn_split, 1)

            def split_m():
                for c in range(H // 4):
                    dve.wait_ge(m_ready, c + 1)
                    hi, lo = (m[:].rearrange("p (c r d) -> p c r d", r=2, d=P)[:, 4 * (c // 2):4 * (c // 2) + 4, c % 2, :]
                              for m in (m_hi, m_lo))
                    ps = psJ[c % 2][:].rearrange("p (c d) -> p c d", d=P)
                    steps.mark(dve.tensor_copy(hi, ps))
                    steps.wait(dve)
                    dve.tensor_tensor(lo, ps, hi.bitcast(F32), ALU.subtract).then_inc(m_split, 1)
                dve.wait_ge(nullv_ready, 1)
                dve.tensor_copy(null_v[:], psJ[0][0:NN, 0:P]).then_inc(nullv_copied, 1)

            def make_alibi():
                dve.wait_ge(a_loaded, 32)
                for h, s in enumerate(slopes()):
                    dve.tensor_scalar(alibi[:, h, :], dist[:], float(s), None, ALU.mult).then_inc(alibi_ready, 1)

            def ln1_begin(n):
                dve.wait_ge(xin_loaded, 16 * (n + 1))
                ln_begin("ln1", xin, (0, 1), n + 1)

            def ln1_end(n):
                ln_end("ln1", xin, xn, (0, 1), n + 1).then_inc(xn_ready, 1)

            def split_xnT(n):
                dve.wait_ge(xnT_ready, n + 1)
                steps.mark(dve.tensor_scalar(xnT_hi[:], psJ[0][:, 0:SEQ], gam[:], None, ALU.mult))
                steps.wait(dve)
                dve.scalar_tensor_tensor(out=xnT_lo[:], in0=psJ[0][:, 0:SEQ], scalar=gam[:],
                                         in1=xnT_hi[:].bitcast(F32), op0=ALU.mult,
                                         op1=ALU.subtract).then_inc(xnT_split, 1)

            def sum_squares(n, t):
                dve.wait_ge(qk_squared, QK_CHUNKS * n + 4 * (t + 1))
                steps.mark(dve.tensor_reduce(ssq[:, t, :], sq[:].rearrange("p (h d) -> p h d", d=DH), AX.X, ALU.add))
                steps.wait(dve)
                dve.tensor_scalar(ssq[:, t, :], ssq[:, t, :], 1e-24, None, ALU.max).then_inc(ssq_ready, 1)

            def norms(n, t):
                dve.wait_ge(qkseed_ready, NT * n + t + 1)
                newton(seedq[:, t, :], ssq[:, t, :], newt[:, t, :], rn[:, t, :], 0.5 * SEED_SCALE).then_inc(rn_ready, 1)

            def null_scores(n):
                dve.wait_ge(nullraw_copied, n + 1)
                dve.wait_ge(rn_ready, NT * (n + 1))
                steps.mark(dve.tensor_tensor(nullmul[:].rearrange("p t (h n) -> p t h n", n=NULLS),
                                             nullraw[:].rearrange("p t (h n) -> p t h n", n=NULLS),
                                             rn[:, :, 0:H].unsqueeze(3).broadcast_to([P, NT, H, NULLS]), ALU.mult))
                steps.wait(dve)
                steps.mark(dve.tensor_tensor(nullneg[:], nullmul[:], nullbias[:], ALU.add))
                steps.wait(dve)
                steps.mark(dve.tensor_reduce(nullmin[:], nullneg[:].rearrange("p t (h n) -> p t h n", n=NULLS),
                                             AX.X, ALU.min))
                steps.wait(dve)

            def copy_qT(n):
                for k in range(2 * NT):
                    t, half = k // 2, k % 2
                    dve.wait_ge(qkT_ready, 4 * NT * n + 2 * k + 1)
                    dve.tensor_copy(qT[:, 4 * half:4 * half + 4, P * t:P * (t + 1)],
                                    psJ[0][:].rearrange("p (c k) -> p c k", c=4)).then_inc(qT_copied, 1)

            def mask_scores(b, t, chunks):
                keys = P if t == 0 else SEQ
                for c in chunks:
                    wait_apart(scores_ready, PC * b + (0 if t == 0 else TILE_PC[0]) + c + 1)
                    for j, h in enumerate(score_heads(t, c)):
                        dve.tensor_tensor_reduce(pr[t][:, h, :], psS[c % 2][:, keys * j:keys * (j + 1)],
                                                 alibi[:, h, SEQ - keys:SEQ], 1.0, nullmin[:, t, h:h + 1],
                                                 ALU.add, ALU.min, nmin[:, t, h:h + 1]).then_inc(scores_masked, 1)

            def null_shift(b, t):
                dve.wait_ge(scores_masked, NT * H * b + H * (t + 1))
                dve.tensor_tensor(nulld[:, t, :].rearrange("p (h n) -> p h n", n=NULLS),
                                  nmin[:, t, :].unsqueeze(2).broadcast_to([P, H, NULLS]),
                                  nullneg[:, t, :].rearrange("p (h n) -> p h n", n=NULLS),
                                  ALU.subtract).then_inc(nulld_ready, 1)

            def denominators(b, t):
                dve.wait_ge(pn_ready, NT * b + t + 1)
                steps.mark(dve.tensor_reduce(den[:, t, :], dparts[:, t], AX.X, ALU.add))
                steps.wait(dve)
                dve.reciprocal(rden[:, t, :], den[:, t, :]).then_inc(rden_ready, 1)
                dve.wait_ge(rden_ready, NT * b + t + 1)
                dve.tensor_tensor(pnn[:, t, :].rearrange("p (h n) -> p h n", n=NULLS), dparts[:, t, :, 1:1 + NULLS],
                                  rden[:, t, :].unsqueeze(2).broadcast_to([P, H, NULLS]),
                                  ALU.mult).then_inc(pnn_ready, 1)

            def copy_pT(b, c):
                dve.wait_ge(probsT_ready, PC * b + c + 1)
                need(dve, pv_done, PC * b + c - 3)
                dve.tensor_copy(pT[c % 4][:], psT[c % 2][:]).then_inc(pT_copied_dve, 1)

            def add_y(b, t):
                dve.wait_ge(y_ready, NT * b + t + 1)
                if t == 0:
                    dve.wait_ge(xres_loaded, 16 * (b + 1))
                dve.tensor_tensor(r1[:, t, :], psY[t][:, 0:P], xres[:, t, :], ALU.add).then_inc(y_added, 1)
                dve.wait_ge(y_added, NT * b + t + 1)
                ln_begin("ln2", r1, (t,), NT * b + t + 1)

            def ln2_end(b, t):
                ln_end("ln2", r1, x1, (t,), NT * b + t + 1).then_inc(x1_ready, 1)

            def x1_plus_bias(b):
                dve.wait_ge(x1_ready, NT * (b + 1))
                steps.mark(dve.tensor_tensor(x1b[:], x1[:], bo[:].unsqueeze(1).broadcast_to([P, NT, P]), ALU.add))

            def cross_shift(b):
                for k in range(XC):
                    t, half = k // 2, k % 2
                    hs = slice(8 * half, 8 * half + 8)
                    dve.wait_ge(xscores_ready, XC * b + k + 1)
                    s = psS[k % 2][:].rearrange("p (h k) -> p h k", h=8)
                    steps.mark(dve.tensor_reduce(xmax[:, t, hs], s, AX.X, ALU.max))
                    steps.wait(dve)
                    dve.tensor_tensor(xp[t][:, hs, :], s, xmax[:, t, hs].unsqueeze(2).broadcast_to([P, 8, CTX]),
                                      ALU.subtract).then_inc(xs_sub, 1)

            def cross_denominators(b):
                for t in range(NT):
                    dve.wait_ge(xexp_done, NT * b + t + 1)
                    steps.mark(dve.tensor_reduce(xden[:, t, :], xp[t][:], AX.X, ALU.add))
                    steps.wait(dve)
                    dve.reciprocal(xrden[:, t, :], xden[:, t, :]).then_inc(xrden_ready, 1)

            def add_y2(b):
                dve.wait_ge(xpv_done, XC * (b + 1))
                dve.tensor_tensor(r2[:], psY[0][:, 0:SEQ].rearrange("p (t d) -> p t d", t=NT), x1b[:],
                                  ALU.add).then_inc(y2_added, 1)
                dve.wait_ge(y2_added, b + 1)
                ln_begin("ln3", r2, (0, 1), b + 1)

            def ln3_end(b, g):
                ln_end("ln3", r2, x2, (0, 1), b + 1).then_inc(x2_ready, 1)
                dve.wait_ge(x2_ready, b + 1)
                dve.wait_ge(w12_copied, g + 1)
                steps.mark(dve.tensor_tensor(x2b[:], x2[:], w12[:, 1:2, :].broadcast_to([P, NT, P]), ALU.add))

            def add_h2(b):
                dve.wait_ge(h2_ready, b + 1)
                steps.wait(dve)
                dve.tensor_tensor(r3[:], psY[0][:, 0:SEQ].rearrange("p (t d) -> p t d", t=NT), x2b[:],
                                  ALU.add).then_inc(h2_added, 1)
                dve.wait_ge(h2_added, b + 1)
                ln_begin("ln4", r3, (0, 1), b + 1)

            def ln4_end(b):
                need(dve, stored, 16 * b)
                ln_end("ln4", r3, x3, (0, 1), b + 1).then_inc(x3_ready, 1)

            ln1_begin(0)
            scale_rows()
            ln1_end(0)
            split_wqk()
            norm_null_keys()
            split_wn()
            split_xnT(0)
            split_m()
            make_alibi()
            sum_squares(0, 0)
            norms(0, 0)
            sum_squares(0, 1)
            norms(0, 1)
            null_scores(0)
            copy_qT(0)
            dve.wait_ge(alibi_ready, H)

            def iteration(i, a, c, w, g):
                if a:
                    ln1_begin(i + 1)
                need(dve, probsT_ready, PC * (i - 1) + TILE_PC[0])
                mask_scores(i, 0, range(4))
                if a:
                    ln1_end(i + 1)
                null_shift(i, 0)
                need(dve, probsT_ready, PC * i)
                mask_scores(i, 1, range(0, 2))
                if a:
                    split_xnT(i + 1)
                mask_scores(i, 1, range(2, 5))
                denominators(i, 0)
                mask_scores(i, 1, range(5, 8))
                null_shift(i, 1)
                if c:
                    cross_shift(i - 1)
                if a:
                    sum_squares(i + 1, 0)
                denominators(i, 1)
                if c:
                    cross_denominators(i - 1)
                if a:
                    norms(i + 1, 0)
                    sum_squares(i + 1, 1)
                copy_pT(i, 0)
                copy_pT(i, 2)
                if a:
                    norms(i + 1, 1)
                    null_scores(i + 1)
                add_y(i, 0)
                if c:
                    add_y2(i - 1)
                ln2_end(i, 0)
                copy_pT(i, 4)
                if c:
                    ln3_end(i - 1, g)
                copy_pT(i, 6)
                copy_pT(i, 8)
                copy_pT(i, 10)
                if c:
                    add_h2(i - 1)
                add_y(i, 1)
                if c:
                    ln4_end(i - 1)
                ln2_end(i, 1)
                x1_plus_bias(i)
                if a:
                    copy_qT(i + 1)

            schedule(dve, iteration, steps, DVE_STEPS_A_TURN)
            b = NB - 1
            cross_shift(b)
            cross_denominators(b)
            add_y2(b)
            ln3_end(b, GROUPS - 1)
            add_h2(b)
            ln4_end(b)

        @block.scalar
        def _(act):
            steps = Steps(act_step)
            act.preload_act_table_set("natural_log_exp_and_others")

            def rsqrt_seed(v, tmp, res, scale):
                steps.mark(act.activation(tmp, v, ACT.Ln, scale=scale))
                steps.wait(act)
                return act.activation(res, tmp, ACT.Exp, scale=-0.5)

            def ln_seed(name, tiles, count):
                act.wait_ge(var_ready[name], count)
                a, z = tiles[0], tiles[-1] + 1
                rsqrt_seed(ve[name][:, a:z], lv[name][:, a:z], sd[name][:, a:z], 1.0).then_inc(seed_ready[name], 1)

            def null_keys():
                act.wait_ge(nkssq_ready, 1)
                rsqrt_seed(nkst[:, 1:2], nkst[:, 2:3], nkst[:, 3:4], SEED_SCALE).then_inc(nkseed_ready, 1)
                act.wait_ge(nkT_ready, 1)
                act.activation(nkT[:], psJ[0][:, 0:NN], ACT.Copy).then_inc(nkT_copied, 1)

            def context_kv():
                for k in range(4):
                    act.wait_ge(kvx_ready, k + 1)
                    dst = (kTx, vTx)[k // 2][:, 512 * (k % 2):512 * (k % 2) + 512]
                    act.activation(dst, psJ[(k + 1) % 2][:], ACT.Identity,
                                   bias=xb[:, 1 + k // 2:2 + k // 2]).then_inc(kvx_copied, 1)

            def copy_qk(n, t):
                for j in range(4):
                    c = 4 * t + j
                    act.wait_ge(qk_ready, QK_CHUNKS * n + c + 1)
                    if j == 0:
                        need(act, ssq_ready, NT * n + t)
                    col = slice(512 * j, 512 * (j + 1))
                    steps.mark(act.activation(qk[t][:, col], psJ[c % 2][:], ACT.Copy))
                    act.activation(sq[:, col], psJ[c % 2][:], ACT.Square).then_inc(qk_squared, 1)

            def qk_seed(n, t):
                act.wait_ge(ssq_ready, NT * n + t + 1)
                rsqrt_seed(ssq[:, t, :], lnq[:, t, :], seedq[:, t, :], SEED_SCALE).then_inc(qkseed_ready, 1)

            def copy_nullraw(n):
                act.wait_ge(nullraw_ready, n + 1)
                act.activation(nullraw[:].rearrange("p t n -> p (t n)"), psJ[0][:, 0:NT * NN],
                               ACT.Copy).then_inc(nullraw_copied, 1)

            def copy_v(n):
                for c in range(V_CHUNKS):
                    act.wait_ge(v_ready, V_CHUNKS * n + c + 1)
                    act.activation(val[:, c // 4, 512 * (c % 4):512 * (c % 4) + 512], psJ[c % 2][:],
                                   ACT.Copy).then_inc(v_copied, 1)

            def copy_kT(n):
                for k in range(2 * NT):
                    t, half = k // 2, k % 2
                    act.wait_ge(qkT_ready, 4 * NT * n + 2 * k + 2)
                    act.activation(kT[:, 4 * half:4 * half + 4, P * t:P * (t + 1)],
                                   psJ[1][:].rearrange("p (c k) -> p c k", c=4), ACT.Copy,
                                   scale=kscale[:]).then_inc(kT_copied, 1)

            def exponentials(b, t, chunks):
                for c in chunks:
                    for j, h in enumerate(score_heads(t, c)):
                        act.wait_ge(scores_masked, NT * H * b + H * t + len(score_heads(t, c)) * c + j + 1)
                        act.activation(pr[t][:, h, :], pr[t][:, h, :], ACT.Exp, bias=nmin[:, t, h:h + 1], scale=-1.0,
                                       accum_out=dparts[:, t, h, 0:1]).then_inc(exp_done, 1)

            def null_exponentials(b, t):
                act.wait_ge(nulld_ready, NT * b + t + 1)
                act.activation(dparts[:, t, :, 1:1 + NULLS], nulld[:, t, :].rearrange("p (h n) -> p h n", n=NULLS),
                               ACT.Exp).then_inc(pn_ready, 1)

            def copy_pnT(b, t):
                act.wait_ge(nullT_ready, NT * b + t + 1)
                act.activation(pnT[:, t, :], psJ[1][0:NN, 0:P], ACT.Copy).then_inc(pnT_copied, 1)

            def copy_pT(b, c):
                act.wait_ge(probsT_ready, PC * b + c + 1)
                need(act, pv_done, PC * b + c - 3)
                act.activation(pT[c % 4][:], psT[c % 2][:], ACT.Copy).then_inc(pT_copied_act, 1)

            def copy_x1T(b):
                act.wait_ge(x1T_ready, b + 1)
                act.activation(x1T[:], psJ[1][:, 0:SEQ], ACT.Copy).then_inc(x1T_copied, 1)

            def copy_xqT(b):
                act.wait_ge(xqT_ready, b + 1)
                act.activation(xqT[:], psJ[0][:, 0:SEQ], ACT.Identity, bias=xb[:, 0:1]).then_inc(xqT_copied, 1)

            def cross_exponentials(b):
                for t in range(NT):
                    act.wait_ge(xs_sub, XC * b + 2 * (t + 1))
                    act.activation(xp[t][:], xp[t][:], ACT.Exp, scale=float(XD) ** -0.5).then_inc(xexp_done, 1)

            def copy_xv(b):
                for c in range(2):
                    act.wait_ge(xv_ready, 2 * b + c + 1)
                    act.activation(xv[:, 4 * c:4 * c + 4, :].rearrange("p c d -> p (c d)"), psJ[c][:],
                                   ACT.Copy).then_inc(xv_copied, 1)

            def copy_w12(g):
                act.wait_ge(w12raw_ready, g + 1)
                act.activation(w12raw[:, 0, :], psJ[0][:, 0:P], ACT.Copy).then_inc(w12raw_copied, 1)
                act.activation(w12raw[:, 1, :], psJ[0][:, P:P + 1].broadcast_to([P, P]), ACT.Identity,
                               bias=b2s[:]).then_inc(w12raw_copied, 1)
                act.wait_ge(w12_ready, g + 1)
                act.activation(w12[:].rearrange("p a d -> p (a d)"), psJ[1][:, 0:2 * P], ACT.Copy).then_inc(w12_copied, 1)

            def copy_xpT(b):
                for k in range(XC):
                    act.wait_ge(xprobsT_ready, XC * b + k + 1)
                    need(act, xpv_done, XC * b + k - 1)
                    act.activation(xpT[k % 2][:], psT[k % 2][:], ACT.Copy).then_inc(xpT_copied, 1)

            def copy_x2T(b):
                act.wait_ge(x2T_ready, b + 1)
                act.activation(x2T[:], psJ[0][:, 0:SEQ], ACT.Copy).then_inc(x2T_copied, 1)

            ln_seed("ln1", (0, 1), 1)
            null_keys()
            act.wait_ge(c_loaded, 16 * 8)
            act.wait_ge(kscale_ready, 1)
            act.wait_ge(g_loaded, 16 * 10)
            context_kv()
            copy_qk(0, 0)
            qk_seed(0, 0)
            copy_qk(0, 1)
            copy_nullraw(0)
            copy_v(0)
            qk_seed(0, 1)
            copy_kT(0)

            def iteration(i, a, c, w, g):
                if a:
                    ln_seed("ln1", (0, 1), i + 2)
                exponentials(i, 0, range(4))
                if c:
                    copy_x1T(i - 1)
                null_exponentials(i, 0)
                exponentials(i, 1, range(0, 3))
                if c:
                    copy_xqT(i - 1)
                exponentials(i, 1, range(3, 8))
                null_exponentials(i, 1)
                if a:
                    copy_qk(i + 1, 0)
                if c:
                    cross_exponentials(i - 1)
                if a:
                    qk_seed(i + 1, 0)
                    copy_qk(i + 1, 1)
                    copy_nullraw(i + 1)
                if c:
                    copy_xv(i - 1)
                    if w:
                        copy_w12(g)
                copy_pnT(i, 0)
                copy_pT(i, 1)
                copy_pT(i, 3)
                if a:
                    qk_seed(i + 1, 1)
                ln_seed("ln2", (0,), NT * i + 1)
                if c:
                    copy_xpT(i - 1)
                    ln_seed("ln3", (0, 1), i)
                copy_pnT(i, 1)
                copy_pT(i, 5)
                copy_pT(i, 7)
                if c:
                    copy_x2T(i - 1)
                copy_pT(i, 9)
                copy_pT(i, 11)
                if c:
                    ln_seed("ln4", (0, 1), i)
                ln_seed("ln2", (1,), NT * i + 2)
                if a:
                    copy_v(i + 1)
                    copy_kT(i + 1)

            schedule(act, iteration, steps, ACT_STEPS_A_TURN)
            b = NB - 1
            copy_x1T(b)
            copy_xqT(b)
            cross_exponentials(b)
            copy_xv(b)
            copy_xpT(b)
            ln_seed("ln3", (0, 1), NB)
            copy_x2T(b)
            ln_seed("ln4", (0, 1), NB)

        @block.gpsimd
        def _(pool):
            def norm_qk(n, t):
                pool.wait_ge(rn_ready, NT * n + t + 1)
                for k in range(2):
                    v = qk[t][:, HD * k:HD * (k + 1)].rearrange("p (h d) -> p h d", d=DH)
                    pool.tensor_tensor(v, v, rn[:, t, H * k:H * (k + 1)].unsqueeze(2).broadcast_to([P, H, DH]),
                                       ALU.mult).then_inc(qk_normed, 1)

            def norm_probs(b, t):
                pool.wait_ge(exp_done, NT * H * b + H * (t + 1))
                pool.wait_ge(rden_ready, NT * b + t + 1)
                heads = 4 if t == 0 else 2
                for c in range(TILE_PC[t]):
                    hs = slice(heads * c, heads * (c + 1))
                    pool.tensor_tensor(pr[t][:, hs, :], pr[t][:, hs, :],
                                       rden[:, t, hs].unsqueeze(2).broadcast_to([P, heads, P * (t + 1)]),
                                       ALU.mult).then_inc(probs_normed, 1)

            def norm_cross(b):
                for t in range(NT):
                    pool.wait_ge(xrden_ready, NT * b + t + 1)
                    pool.tensor_tensor(xp[t][:], xp[t][:], xrden[:, t, :].unsqueeze(2).broadcast_to([P, XH, CTX]),
                                       ALU.mult).then_inc(xprobs_normed, 1)

            def spread_context(b):
                mask = hmask[:].unsqueeze(2).broadcast_to([P, XH, CTX])
                if isinstance(b, int):
                    col = slice(CTX * b, CTX * (b + 1))
                else:
                    col = bass.ds(CTX * b, CTX)
                need(pool, xscores_ready, XC * b)
                pool.tensor_tensor(kexp[:], mask, kTx[:, col].unsqueeze(1).broadcast_to([P, XH, CTX]),
                                   ALU.mult).then_inc(kexp_ready, 1)
                need(pool, xv_ready, 2 * b)
                pool.tensor_tensor(vexp[:], mask, vTx[:, col].unsqueeze(1).broadcast_to([P, XH, CTX]),
                                   ALU.mult).then_inc(vexp_ready, 1)

            pool.wait_ge(g_loaded, 16 * 10)
            pool.wait_ge(kvx_copied, 4)
            norm_qk(0, 0)
            norm_qk(0, 1)

            def iteration(i, a, c, w, g):
                norm_probs(i, 0)
                if c:
                    norm_cross(i - 1)
                norm_probs(i, 1)
                if a:
                    norm_qk(i + 1, 0)
                    norm_qk(i + 1, 1)
                spread_context(i)

            schedule(pool, iteration)
            norm_cross(NB - 1)


DVE_STEPS_A_TURN = 108
ACT_STEPS_A_TURN = 30


def kernel(x, ctx_1024, L0_attn_gamma, L0_attn_w_q, L0_attn_w_kv, L0_attn_null_kv, L0_attn_q_scale,
           L0_attn_k_scale, L0_attn_w_out, L0_xattn_wq, L0_xattn_bq, L0_xattn_wk, L0_xattn_bk, L0_xattn_wv,
           L0_xattn_bv, L0_xattn_wo, L0_xattn_bo, L0_ffn_W1, L0_ffn_b1, L0_ffn_W2, L0_ffn_b2):
    import concourse.bacc as bacc
    from concourse.bass_utils import run_bass_kernel_spmd

    def pairs(w):
        return w.reshape(HP, P, w.shape[1]).transpose(1, 0, 2)

    def block_diagonal(w):
        w = np.asarray(w)
        m = np.zeros((P, P), w.dtype)
        for h in range(XH):
            m[XD * h:XD * (h + 1), XD * h:XD * (h + 1)] = w[h].T
        return m

    w_q, w_kv, w_out = np.asarray(L0_attn_w_q), np.asarray(L0_attn_w_kv), np.asarray(L0_attn_w_out)
    nkv = np.asarray(L0_attn_null_kv).reshape(H, NULLS, 2, DH)
    nvT = np.zeros((HP, 2, DH, H, NULLS), nkv.dtype)
    for h in range(H):
        nvT[h // 2, h % 2, :, h, :] = nkv[h, :, 1].T
    q_pos, k_pos = np.arange(P)[:, None] + P, np.arange(SEQ)[None, :]
    dist = np.where(k_pos > q_pos, MASKED, q_pos - k_pos).astype(np.float32)
    null_dist = (np.arange(SEQ).reshape(NT, P, 1, 1) + NULLS - np.arange(NULLS)).astype(np.float32)
    nullbias = (null_dist * slopes()[None, None, :, None]).reshape(NT, P, NN).transpose(1, 0, 2)
    hmask = (np.arange(P)[:, None] // XD == np.arange(XH)[None, :]).astype(np.float32)
    arrays = {
        "x": x,
        "ctxT": np.asarray(ctx_1024).reshape(NB * CTX, P).T,
        "gamma": np.asarray(L0_attn_gamma).reshape(P, 1),
        "w_q": w_q,
        "w_kv": w_kv,
        "wqT": pairs(w_q.T),
        "wvT": pairs(w_kv[:, HD:].T),
        "wout": pairs(w_out),
        "nk": nkv[:, :, 0].reshape(NN, DH),
        "nvT": nvT.reshape(HP, P, NN).transpose(1, 0, 2),
        "q_scale": np.asarray(L0_attn_q_scale).reshape(DH, 1),
        "k_scale": np.asarray(L0_attn_k_scale).reshape(DH, 1),
        "xwq": block_diagonal(L0_xattn_wq),
        "xwk": block_diagonal(L0_xattn_wk),
        "xwv": block_diagonal(L0_xattn_wv),
        "xbq": np.asarray(L0_xattn_bq).reshape(P, 1),
        "xbk": np.asarray(L0_xattn_bk).reshape(P, 1),
        "xbv": np.asarray(L0_xattn_bv).reshape(P, 1),
        "xwoT": np.asarray(L0_xattn_wo).T,
        "xbo": np.asarray(L0_xattn_bo).reshape(1, P),
        "w1b": np.concatenate([np.asarray(L0_ffn_W1), np.asarray(L0_ffn_b1)[:, :, None]], axis=2),
        "w2T": np.asarray(L0_ffn_W2).transpose(0, 2, 1),
        "b2": np.asarray(L0_ffn_b2).reshape(GROUPS, P, 1),
        "ident_in": np.eye(P, dtype=np.float32),
        "dist_in": dist,
        "nullbias_in": nullbias,
        "hmask_in": hmask,
    }
    arrays = {n: np.ascontiguousarray(a) for n, a in arrays.items()}
    nc = bacc.Bacc("TRN2", target_bir_lowering=False, num_devices=1)
    args = {n: nc.dram_tensor(n, a.shape, mybir.dt.from_np(a.dtype), kind="ExternalInput").ap()
            for n, a in arrays.items()}
    out = nc.dram_tensor("out", (NB, SEQ, P), F32, kind="ExternalOutput").ap()
    program(nc, **args, out=out)
    r = run_bass_kernel_spmd(nc, [arrays], core_ids=[0])
    return r.results[0]["out"]
```

```python
import math
from contextlib import ExitStack

import numpy as np
import concourse.bass as bass
from concourse import mybir

F32 = mybir.dt.float32
F32R = mybir.dt.float32r
ALU = mybir.AluOpType
ACT = mybir.ActivationFunctionType
AX = mybir.AxisListType

P = 128
NB, SEQ = 16, 256
NT = SEQ // P
H, DH = 16, 64
HP = H // 2
HD = H * DH
NULLS = 2
NN = H * NULLS
CTX = 64
XH, XD = 16, 8
GROUPS = 8
INTER = 512
OC = INTER // P
EPS = 1e-5
ATTN_SCALE = 8.0
SEED_SCALE = 65536.0
MASKED = 1e30

QK_CHUNKS = 8
V_CHUNKS = 8
PC = 12
TILE_PC = (4, 8)
XC = 4


def slopes():
    start = 2.0 ** (-2.0 ** (-(math.log2(H) - 3.0)))
    return np.array([start * start ** i for i in range(H)], dtype=np.float32)


class Steps:

    def __init__(self, sem):
        self.sem, self.n, self.offset = sem, 0, 0

    def mark(self, ins):
        ins.then_inc(self.sem, 1)
        self.n += 1

    def value(self):
        return self.n + self.offset

    def wait(self, eng):
        eng.wait_ge(self.sem, self.value())

    def enter_loop(self, i, per_turn):
        self.offset, self.before, self.per_turn = i * per_turn, self.n, per_turn

    def leave_loop(self, turns):
        assert self.n - self.before == self.per_turn, ("steps of a turn", self.n - self.before)
        self.n, self.offset = self.before + turns * self.per_turn, 0


def score_heads(t, c):
    n = 4 if t == 0 else 2
    return [2 * (n * (c // 2) + j) + c % 2 for j in range(n)]


def need(eng, sem, value):
    if not (isinstance(value, int) and value <= 0):
        eng.wait_ge(sem, value)


def program(nc, x, ctxT, gamma, w_q, w_kv, wqT, wvT, wout, nk, nvT, q_scale, k_scale,
            xwq, xwk, xwv, xbq, xbk, xbv, xwoT, xbo, w1b, w2T, b2, ident_in, dist_in, nullbias_in,
            hmask_in, out):
    with ExitStack() as ctx:
        def sb(name, shape, dt=F32):
            return ctx.enter_context(nc.sbuf_tensor(name, shape, dt))

        def sem(name):
            return ctx.enter_context(nc.semaphore(name))

        psS = [ctx.enter_context(nc.psum_tensor(f"psS{k}", [P, 512], F32)) for k in range(2)]
        psT = [ctx.enter_context(nc.psum_tensor(f"psT{k}", [P, 512], F32)) for k in range(2)]
        psJ = [ctx.enter_context(nc.psum_tensor(f"psJ{k}", [P, 512], F32)) for k in range(2)]
        psY = [ctx.enter_context(nc.psum_tensor(f"psY{k}", [P, 512], F32)) for k in range(2)]

        ident = sb("ident", [P, P])
        dist = sb("dist", [P, SEQ])
        alibi = sb("alibi", [P, H, SEQ])
        nullbias = sb("nullbias", [P, NT, NN])
        hmask = sb("hmask", [P, XH])
        gam = sb("gam", [P, 1])
        qks2 = sb("qks2", [P, 2])
        kscale = sb("kscale", [P, 1])
        wqk_hi = sb("wqk_hi", [P, 2 * HD], F32R)
        wqk_lo = sb("wqk_lo", [P, 2 * HD], F32R)
        wn_hi = sb("wn_hi", [P, NN], F32R)
        wn_lo = sb("wn_lo", [P, NN], F32R)
        m_hi = sb("m_hi", [P, H * P], F32R)
        m_lo = sb("m_lo", [P, H * P], F32R)
        null_v = sb("null_v", [NN, P])
        nkrow = sb("nkrow", [NN, 2 * DH])
        nksc = sb("nksc", [NN, 2 * DH])
        nksq = sb("nksq", [NN, DH])
        nkst = sb("nkst", [NN, 8])
        nkT = sb("nkT", [P, NN])
        xw = sb("xw", [P, 3, P])
        xb = sb("xb", [P, 3])
        xwo = sb("xwo", [P, P])
        bo = sb("bo", [P, P])
        kTx = sb("kTx", [P, NB * CTX])
        vTx = sb("vTx", [P, NB * CTX])
        w1s = sb("w1s", [P, OC, P + 1])
        w2s = sb("w2s", [P, OC, P])
        b2s = sb("b2s", [P, 1])
        w12raw = sb("w12raw", [P, 2, P])
        w12 = sb("w12", [P, 2, P])
        xin = sb("xin", [P, NT, P])
        xn = sb("xn", [P, NT, P])
        xnT_hi = sb("xnT_hi", [P, SEQ], F32R)
        xnT_lo = sb("xnT_lo", [P, SEQ], F32R)
        qk = [sb(f"qk{t}", [P, 2 * HD]) for t in range(NT)]
        sq = sb("sq", [P, 2 * HD])
        ssq = sb("ssq", [P, NT, 2 * H])
        lnq = sb("lnq", [P, NT, 2 * H])
        seedq = sb("seedq", [P, NT, 2 * H])
        newt = sb("newt", [P, NT, 2 * H])
        rn = sb("rn", [P, NT, 2 * H])
        nullraw = sb("nullraw", [P, NT, NN])
        nullmul = sb("nullmul", [P, NT, NN])
        nullneg = sb("nullneg", [P, NT, NN])
        nullmin = sb("nullmin", [P, NT, H])
        qT = sb("qT", [P, HP, SEQ])
        kT = sb("kT", [P, HP, SEQ])
        val = sb("val", [P, NT, H * P])
        xres = sb("xres", [P, NT, P])
        pr = [sb(f"pr{t}", [P, H, P * (t + 1)]) for t in range(NT)]
        nmin = sb("nmin", [P, NT, H])
        nulld = sb("nulld", [P, NT, NN])
        dparts = sb("dparts", [P, NT, H, 1 + NULLS])
        den = sb("den", [P, NT, H])
        rden = sb("rden", [P, NT, H])
        pnn = sb("pnn", [P, NT, NN])
        pnT = sb("pnT", [NN, NT, P])
        pT = [sb(f"pT{k}", [P, 512]) for k in range(4)]
        r1 = sb("r1", [P, NT, P])
        x1 = sb("x1", [P, NT, P])
        x1b = sb("x1b", [P, NT, P])
        x1T = sb("x1T", [P, SEQ])
        xqT = sb("xqT", [P, SEQ])
        kexp = sb("kexp", [P, XH, CTX])
        vexp = sb("vexp", [P, XH, CTX])
        xv = sb("xv", [P, XH // 2, P])
        xmax = sb("xmax", [P, NT, XH])
        xp = [sb(f"xp{t}", [P, XH, CTX]) for t in range(NT)]
        xden = sb("xden", [P, NT, XH])
        xrden = sb("xrden", [P, NT, XH])
        xpT = [sb(f"xpT{k}", [P, 512]) for k in range(2)]
        r2 = sb("r2", [P, NT, P])
        x2 = sb("x2", [P, NT, P])
        x2b = sb("x2b", [P, NT, P])
        x2T = sb("x2T", [P, SEQ])
        r3 = sb("r3", [P, NT, P])
        x3 = sb("x3", [P, NT, P])
        LN = ("ln1", "ln2", "ln3", "ln4")
        st = {n: sb(f"{n}_st", [P, NT, 6]) for n in LN}
        mv = {n: sb(f"{n}_mv", [P, NT, 2]) for n in LN}
        ve = {n: sb(f"{n}_ve", [P, NT]) for n in LN}
        lv = {n: sb(f"{n}_lv", [P, NT]) for n in LN}
        sd = {n: sb(f"{n}_sd", [P, NT]) for n in LN}
        nw = {n: sb(f"{n}_nw", [P, NT]) for n in LN}
        rs = {n: sb(f"{n}_rs", [P, NT]) for n in LN}

        wqk_raw = pr[1][:, 0:8, :].rearrange("p h k -> p (h k)")
        wqT_s = qk[0][:, 0:HD].rearrange("p (c d) -> p c d", c=HP)
        wvT_s = qk[0][:, HD:2 * HD].rearrange("p (c d) -> p c d", c=HP)
        wout_s = qk[1][:, 0:HD].rearrange("p (c d) -> p c d", c=HP)
        nvT_s = qk[1][:, HD:HD + HP * NN].rearrange("p (c n) -> p c n", c=HP)
        ctxT_s = xp[0][:].rearrange("p h k -> p (h k)")

        c_loaded = sem("c_loaded")
        h_loaded = sem("h_loaded")
        a_loaded = sem("a_loaded")
        g_loaded = sem("g_loaded")
        xin_loaded = sem("xin_loaded")
        xres_loaded = sem("xres_loaded")
        ffn_loaded = sem("ffn_loaded")
        stored = sem("stored")
        nkT_ready = sem("nkT_ready")
        wn_ready = sem("wn_ready")
        m_ready = sem("m_ready")
        nullv_ready = sem("nullv_ready")
        kvx_ready = sem("kvx_ready")
        xnT_ready = sem("xnT_ready")
        qk_ready = sem("qk_ready")
        nullraw_ready = sem("nullraw_ready")
        qkT_ready = sem("qkT_ready")
        v_ready = sem("v_ready")
        scores_ready = sem("scores_ready")
        nullT_ready = sem("nullT_ready")
        probsT_ready = sem("probsT_ready")
        pv_done = sem("pv_done")
        y_ready = sem("y_ready")
        x1T_ready = sem("x1T_ready")
        xqT_ready = sem("xqT_ready")
        xscores_ready = sem("xscores_ready")
        xv_ready = sem("xv_ready")
        w12raw_ready = sem("w12raw_ready")
        w12_ready = sem("w12_ready")
        xprobsT_ready = sem("xprobsT_ready")
        xpv_done = sem("xpv_done")
        y2_ready = sem("y2_ready")
        x2T_ready = sem("x2T_ready")
        h2_ready = sem("h2_ready")
        dve_step = sem("dve_step")
        kscale_ready = sem("kscale_ready")
        nkssq_ready = sem("nkssq_ready")
        nkrow_ready = sem("nkrow_ready")
        wsplit_ready = sem("wsplit_ready")
        wn_split = sem("wn_split")
        m_split = sem("m_split")
        nullv_copied = sem("nullv_copied")
        alibi_ready = sem("alibi_ready")
        xn_ready = sem("xn_ready")
        xnT_split = sem("xnT_split")
        ssq_ready = sem("ssq_ready")
        rn_ready = sem("rn_ready")
        qT_copied = sem("qT_copied")
        qk_copied_dve = sem("qk_copied_dve")
        v_copied_dve = sem("v_copied_dve")
        scores_masked = sem("scores_masked")
        nulld_ready = sem("nulld_ready")
        rden_ready = sem("rden_ready")
        pnn_ready = sem("pnn_ready")
        pT_copied_dve = sem("pT_copied_dve")
        y_added = sem("y_added")
        x1_ready = sem("x1_ready")
        xs_sub = sem("xs_sub")
        xrden_ready = sem("xrden_ready")
        y2_added = sem("y2_added")
        x2_ready = sem("x2_ready")
        h2_added = sem("h2_added")
        x3_ready = sem("x3_ready")
        var_ready = {n: sem(f"{n}_var_ready") for n in LN}
        act_step = sem("act_step")
        nkseed_ready = sem("nkseed_ready")
        nkT_copied = sem("nkT_copied")
        kvx_copied = sem("kvx_copied")
        seed_ready = {n: sem(f"{n}_seed_ready") for n in LN}
        qk_squared = sem("qk_squared")
        qkseed_ready = sem("qkseed_ready")
        nullraw_copied = sem("nullraw_copied")
        kT_copied = sem("kT_copied")
        qk_copied_act = sem("qk_copied_act")
        v_copied_act = sem("v_copied_act")
        exp_done = sem("exp_done")
        pn_ready = sem("pn_ready")
        pnT_copied = sem("pnT_copied")
        pT_copied_act = sem("pT_copied_act")
        x1T_copied = sem("x1T_copied")
        xqT_copied = sem("xqT_copied")
        xexp_done = sem("xexp_done")
        xv_copied = sem("xv_copied")
        w12raw_copied = sem("w12raw_copied")
        w12_copied = sem("w12_copied")
        xpT_copied = sem("xpT_copied")
        x2T_copied = sem("x2T_copied")
        qk_normed = sem("qk_normed")
        probs_normed = sem("probs_normed")
        xprobs_normed = sem("xprobs_normed")
        kexp_ready = sem("kexp_ready")
        vexp_ready = sem("vexp_ready")

        x_dram = x.rearrange("b (t p) d -> p b t d", p=P)
        out_dram = out.rearrange("b (t p) d -> p b t d", p=P)
        w1_dram = w1b.rearrange("g (c p) h -> p g c h", p=P)
        w2_dram = w2T.rearrange("g (c p) h -> p g c h", p=P)

        FIRST = 3
        TURNS = (NB - 1 - FIRST) // 2

        def schedule(eng, iteration, steps=None, per_turn=0):
            for i in range(FIRST):
                iteration(i, True, i >= 1, i % 2 == 1, (i - 1) // 2)
            with eng.Fori(0, TURNS) as turn:
                if steps:
                    steps.enter_loop(turn, per_turn)
                for half in range(2):
                    iteration(2 * turn + (FIRST + half), True, True, half == 0, turn + (FIRST - 1) // 2)
            if steps:
                steps.leave_loop(TURNS)
            iteration(NB - 1, False, True, (NB - 1) % 2 == 1, (NB - 2) // 2)

        block = ctx.enter_context(nc.Block())

        @block.sync
        def _(sp):
            sp.dma_start(xin[:], x_dram[:, 0]).then_inc(xin_loaded, 16)
            sp.dma_start(ident[:], ident_in).then_inc(c_loaded, 16)
            sp.dma_start(gam[:], gamma).then_inc(c_loaded, 16)
            sp.dma_start(wqk_raw[:, 0:HD], w_q).then_inc(c_loaded, 16)
            sp.dma_start(wqk_raw[:, HD:2 * HD], w_kv[:, 0:HD]).then_inc(c_loaded, 16)
            for half in range(2):
                sp.dma_start(qks2[half * DH:(half + 1) * DH, 0:1], q_scale).then_inc(c_loaded, 16)
                sp.dma_start(qks2[half * DH:(half + 1) * DH, 1:2], k_scale).then_inc(c_loaded, 16)
            sp.dma_start(nkrow[:, 0:DH], nk).then_inc(h_loaded, 16)
            sp.dma_start(nksc[:, 0:DH], q_scale.rearrange("d a -> a d").broadcast_to([NN, DH])).then_inc(h_loaded, 16)
            sp.dma_start(nksc[:, DH:2 * DH], k_scale.rearrange("d a -> a d").broadcast_to([NN, DH])).then_inc(h_loaded, 16)
            sp.dma_start(wqT_s, wqT).then_inc(h_loaded, 16)
            sp.dma_start(wvT_s, wvT).then_inc(h_loaded, 16)
            sp.dma_start(wout_s, wout).then_inc(h_loaded, 16)
            sp.dma_start(nvT_s, nvT).then_inc(h_loaded, 16)
            sp.dma_start(dist[:], dist_in).then_inc(a_loaded, 16)
            sp.dma_start(nullbias[:], nullbias_in).then_inc(a_loaded, 16)
            sp.dma_start(xres[:], x_dram[:, 0]).then_inc(xres_loaded, 16)
            sp.dma_start(ctxT_s, ctxT).then_inc(g_loaded, 16)
            sp.dma_start(hmask[:], hmask_in).then_inc(g_loaded, 16)
            for k, (w, b) in enumerate(((xwq, xbq), (xwk, xbk), (xwv, xbv))):
                sp.dma_start(xw[:, k, :], w).then_inc(g_loaded, 16)
                sp.dma_start(xb[:, k:k + 1], b).then_inc(g_loaded, 16)
            sp.dma_start(xwo[:], xwoT).then_inc(g_loaded, 16)
            sp.dma_start(bo[:], xbo.broadcast_to([P, P])).then_inc(g_loaded, 16)

            def ffn_load(g):
                sp.dma_start(w1s[:], w1_dram[:, g]).then_inc(ffn_loaded, 16)
                sp.dma_start(w2s[:], w2_dram[:, g]).then_inc(ffn_loaded, 16)
                sp.dma_start(b2s[:], b2[g]).then_inc(ffn_loaded, 16)

            ffn_load(0)

            def iteration(i, a, c, w, g):
                if a:
                    sp.wait_ge(xn_ready, i + 1)
                    sp.dma_start(xin[:], x_dram[:, i + 1]).then_inc(xin_loaded, 16)
                if w and not (isinstance(g, int) and g + 1 >= GROUPS):
                    sp.wait_ge(w12raw_ready, g + 1)
                    sp.wait_ge(w12raw_copied, 2 * g + 2)
                    ffn_load(g + 1)
                if c:
                    sp.wait_ge(x3_ready, i)
                    sp.dma_start(out_dram[:, i - 1], x3[:]).then_inc(stored, 16)
                if a:
                    sp.wait_ge(y_added, NT * (i + 1))
                    sp.dma_start(xres[:], x_dram[:, i + 1]).then_inc(xres_loaded, 16)

            schedule(sp, iteration)
            sp.wait_ge(x3_ready, NB)
            sp.dma_start(out_dram[:, NB - 1], x3[:]).then_inc(stored, 16)
            sp.wait_ge(stored, 16 * NB)

        @block.tensor
        def _(pe):
            read = {}

            def take(bank, read_by, value):
                if bank in read:
                    need(pe, *read[bank])
                read[bank] = (read_by, value)

            def split_product(dst, hi, lo, whi, wlo):
                pe.matmul(dst, hi, whi, start=True, stop=False)
                pe.matmul(dst, hi, wlo, start=False, stop=False)
                return pe.matmul(dst, lo, whi, start=False, stop=True)

            def null_keys():
                pe.wait_ge(c_loaded, 16 * 8)
                pe.wait_ge(nkrow_ready, 1)
                take('J0', nkT_copied, 1)
                pe.transpose(psJ[0][:, 0:NN], nkrow[:], ident[0:NN, 0:NN]).then_inc(nkT_ready, 1)
                pe.wait_ge(h_loaded, 16 * 7)
                take('J0', wn_split, 1)
                take('J1', wn_split, 1)
                for h in list(range(0, H, 2)) + list(range(1, H, 2)):
                    r = slice(DH * (h % 2), DH * (h % 2) + DH)
                    mm = pe.matmul(psJ[h % 2][:, NULLS * (h // 2):NULLS * (h // 2 + 1)], wqT_s[r, h // 2, :],
                                   nkT[r, NULLS * h:NULLS * (h + 1)], start=True, stop=True)
                mm.then_inc(wn_ready, 1)

            def merged_values():
                for c in range(H // 4):
                    take(f'J{c % 2}', m_split, c + 1)
                    for j, h in enumerate(score_heads(0, c)):
                        r = slice(DH * (h % 2), DH * (h % 2) + DH)
                        mm = pe.matmul(psJ[c % 2][:, P * j:P * (j + 1)], wvT_s[r, h // 2, :],
                                       wout_s[r, h // 2, :], start=True, stop=True)
                    mm.then_inc(m_ready, 1)
                take('J0', nullv_copied, 1)
                for p in range(HP):
                    mm = pe.matmul(psJ[0][0:NN, 0:P], nvT_s[:, p, :], wout_s[:, p, :],
                                   start=(p == 0), stop=(p == HP - 1))
                mm.then_inc(nullv_ready, 1)

            def context_kv():
                pe.wait_ge(g_loaded, 16 * 10)
                for k in range(4):
                    take(f'J{(k + 1) % 2}', kvx_copied, k + 1)
                    pe.matmul(psJ[(k + 1) % 2][:], xw[:, 1 + k // 2, :], ctxT_s[:, 512 * (k % 2):512 * (k % 2) + 512],
                              start=True, stop=True).then_inc(kvx_ready, 1)

            def xn_turn(n):
                pe.wait_ge(xn_ready, n + 1)
                take('J0', xnT_split, n + 1)
                for t in range(NT):
                    mm = pe.transpose(psJ[0][:, P * t:P * (t + 1)], xn[:, t, :], ident[:])
                mm.then_inc(xnT_ready, 1)

            def project_qk(n, c):
                if c == 0:
                    pe.wait_ge(xnT_split, n + 1)
                t, j = c // 4, c % 4
                take(f'J{c % 2}', qk_copied_dve if c % 2 else qk_copied_act, QK_CHUNKS // 2 * n + c // 2 + 1)
                tok, col = slice(P * t, P * (t + 1)), slice(512 * j, 512 * (j + 1))
                split_product(psJ[c % 2][:], xnT_hi[:, tok], xnT_lo[:, tok],
                              wqk_hi[:, col], wqk_lo[:, col]).then_inc(qk_ready, 1)

            def project_nulls(n):
                take('J0', nullraw_copied, n + 1)
                for t in range(NT):
                    tok = slice(P * t, P * (t + 1))
                    mm = split_product(psJ[0][:, NN * t:NN * (t + 1)], xnT_hi[:, tok], xnT_lo[:, tok],
                                       wn_hi[:], wn_lo[:])
                mm.then_inc(nullraw_ready, 1)

            def project_v(n, c):
                t, j = c // 4, c % 4
                take(f'J{c % 2}', v_copied_act if c % 2 else v_copied_dve, V_CHUNKS // 2 * n + c // 2 + 1)
                tok, col = slice(P * t, P * (t + 1)), slice(512 * j, 512 * (j + 1))
                split_product(psJ[c % 2][:], xnT_hi[:, tok], xnT_lo[:, tok],
                              m_hi[:, col], m_lo[:, col]).then_inc(v_ready, 1)

            def turn_qk(n, c):
                t, half, isk = c // 4, (c // 2) % 2, c % 2
                if half == 0:
                    pe.wait_ge(qk_normed, 2 * NT * n + 2 * t + isk + 1)
                take(f'S{isk}', kT_copied if isk else qT_copied, 2 * NT * n + c // 2 + 1)
                for j in range(4):
                    col = HD * isk + P * (4 * half + j)
                    mm = pe.transpose(psS[isk][:, P * j:P * (j + 1)], qk[t][:, col:col + P], ident[:])
                mm.then_inc(qkT_ready, 1)

            def scores(b, t, c):
                heads, keys = (4, P) if t == 0 else (2, SEQ)
                if t == 0 and c == 0:
                    pe.wait_ge(kT_copied, 2 * NT * b + 1)
                before = 4 * c if t == 0 else H + 2 * c
                k = c % 2
                take(f'S{k}', scores_masked, NT * H * b + before + heads)
                for j, h in enumerate(score_heads(t, c)):
                    r = slice(DH * (h % 2), DH * (h % 2) + DH)
                    mm = pe.matmul(psS[k][:, keys * j:keys * (j + 1)], qT[r, h // 2, P * t:P * (t + 1)],
                                   kT[r, h // 2, 0:keys], start=True, stop=True)
                mm.then_inc(scores_ready, 1)

            def evacuated(b, c):
                if c % 2 == 0:
                    pe.wait_ge(pT_copied_dve, (PC // 2) * b + c // 2 + 1)
                else:
                    pe.wait_ge(pT_copied_act, (PC // 2) * b + c // 2 + 1)

            def turn_probs(b, c):
                t, first = (0, 0) if c < TILE_PC[0] else (1, TILE_PC[0])
                pe.wait_ge(probs_normed, PC * b + c + 1)
                if c >= 2:
                    evacuated(b, c - 2)
                for j in range(4):
                    blk = 4 * (c - first) + j
                    h, kt = blk // (t + 1), blk % (t + 1)
                    mm = pe.transpose(psT[c % 2][:, P * j:P * (j + 1)], pr[t][:, h, P * kt:P * (kt + 1)], ident[:])
                mm.then_inc(probsT_ready, 1)

            def weigh_values(b, c):
                t, first = (0, 0) if c < TILE_PC[0] else (1, TILE_PC[0])
                if c == 0:
                    pe.wait_ge(v_copied_dve, V_CHUNKS // 2 * (b + 1))
                    pe.wait_ge(v_copied_act, V_CHUNKS // 2 * (b + 1))
                evacuated(b, c)
                for j in range(4):
                    blk = 4 * (c - first) + j
                    h, kt = blk // (t + 1), blk % (t + 1)
                    mm = pe.matmul(psY[t][:, 0:P], pT[c % 4][:, P * j:P * (j + 1)], val[:, kt, P * h:P * (h + 1)],
                                   start=(blk == 0), stop=False)
                mm.then_inc(pv_done, 1)

            def turn_nulls(b, t):
                pe.wait_ge(pnn_ready, NT * b + t + 1)
                take('J1', pnT_copied, NT * b + t + 1)
                pe.transpose(psJ[1][0:NN, 0:P], pnn[:, t, :], ident[:]).then_inc(nullT_ready, 1)

            def weigh_nulls(b, t):
                pe.wait_ge(pnT_copied, NT * b + t + 1)
                pe.matmul(psY[t][:, 0:P], pnT[:, t, :], null_v[:], start=False, stop=True).then_inc(y_ready, 1)

            def x1_turn(b):
                pe.wait_ge(x1_ready, NT * (b + 1))
                take('J1', x1T_copied, b + 1)
                for t in range(NT):
                    mm = pe.transpose(psJ[1][:, P * t:P * (t + 1)], x1[:, t, :], ident[:])
                mm.then_inc(x1T_ready, 1)

            def cross_q(b):
                pe.wait_ge(x1T_copied, b + 1)
                take('J1', xqT_copied, b + 1)
                pe.matmul(psJ[1][:, 0:SEQ], xw[:, 0, :], x1T[:], start=True, stop=True).then_inc(xqT_ready, 1)

            def cross_scores(b, k):
                t, half = k // 2, k % 2
                if k == 0:
                    pe.wait_ge(xqT_copied, b + 1)
                    pe.wait_ge(kexp_ready, b + 1)
                take(f'S{half}', xs_sub, XC * b + k + 1)
                pe.matmul(psS[half][:], xqT[:, P * t:P * (t + 1)],
                          kexp[:, 8 * half:8 * half + 8, :].rearrange("p h k -> p (h k)"),
                          start=True, stop=True).then_inc(xscores_ready, 1)

            def cross_values(b, c):
                pe.wait_ge(vexp_ready, b + 1)
                take(f'J{c}', xv_copied, 2 * b + c + 1)
                for j in range(4):
                    p = 4 * c + j
                    mm = pe.matmul(psJ[c][:, P * j:P * (j + 1)],
                                   vexp[:, 2 * p:2 * p + 2, :].rearrange("p h k -> p (h k)"), xwo[:],
                                   start=True, stop=True)
                mm.then_inc(xv_ready, 1)

            def merge_ffn(g):
                pe.wait_ge(ffn_loaded, 48 * (g + 1))
                take('J0', w12raw_copied, 2 * g + 2)
                for c in range(OC):
                    mm = pe.matmul(psJ[0][:, 0:P + 1], w2s[:, c, :], w1s[:, c, :], start=(c == 0), stop=(c == OC - 1))
                mm.then_inc(w12raw_ready, 1)

            def turn_ffn(g):
                pe.wait_ge(w12raw_copied, 2 * g + 2)
                take('J1', w12_copied, g + 1)
                for k in range(2):
                    mm = pe.transpose(psJ[1][:, P * k:P * (k + 1)], w12raw[:, k, :], ident[:])
                mm.then_inc(w12_ready, 1)

            def turn_cross_probs(b, k):
                t, half = k // 2, k % 2
                pe.wait_ge(xprobs_normed, NT * b + t + 1)
                if k >= 2:
                    pe.wait_ge(xpT_copied, XC * b + k - 1)
                for j in range(4):
                    p = 4 * half + j
                    mm = pe.transpose(psT[half][:, P * j:P * (j + 1)],
                                      xp[t][:, 2 * p:2 * p + 2, :].rearrange("p h k -> p (h k)"), ident[:])
                mm.then_inc(xprobsT_ready, 1)

            def weigh_cross_values(b, k):
                t, half = k // 2, k % 2
                pe.wait_ge(xpT_copied, XC * b + k + 1)
                for j in range(4):
                    mm = pe.matmul(psY[0][:, P * t:P * (t + 1)], xpT[half][:, P * j:P * (j + 1)],
                                   xv[:, 4 * half + j, :], start=(half == 0 and j == 0),
                                   stop=(half == 1 and j == 3))
                mm.then_inc(xpv_done, 1)

            def x2_turn(b):
                pe.wait_ge(x2_ready, b + 1)
                take('J1', x2T_copied, b + 1)
                for t in range(NT):
                    mm = pe.transpose(psJ[1][:, P * t:P * (t + 1)], x2[:, t, :], ident[:])
                mm.then_inc(x2T_ready, 1)

            def feed_forward(b, g):
                pe.wait_ge(x2T_copied, b + 1)
                pe.wait_ge(w12_copied, g + 1)
                pe.wait_ge(y2_added, b + 1)
                for t in range(NT):
                    mm = pe.matmul(psY[0][:, P * t:P * (t + 1)], x2T[:, P * t:P * (t + 1)], w12[:, 0, :],
                                   start=True, stop=True)
                mm.then_inc(h2_ready, 1)

            null_keys()
            xn_turn(0)
            pe.wait_ge(wsplit_ready, 1)
            pe.wait_ge(wn_split, 1)
            merged_values()
            context_kv()
            for c in range(QK_CHUNKS):
                project_qk(0, c)
            project_nulls(0)
            for c in range(V_CHUNKS):
                project_v(0, c)
            for c in range(4 * NT):
                turn_qk(0, c)

            def iteration(i, a, c, w, g):
                read['J0'], read['J1'] = (v_copied_dve, V_CHUNKS // 2 * (i + 1)), (v_copied_act, V_CHUNKS // 2 * (i + 1))
                read['S0'], read['S1'] = (qT_copied, 2 * NT * (i + 1)), (kT_copied, 2 * NT * (i + 1))
                scores(i, 0, 0)
                scores(i, 0, 1)
                if c:
                    x1_turn(i - 1)
                if a:
                    xn_turn(i + 1)
                scores(i, 0, 2)
                if c:
                    cross_q(i - 1)
                scores(i, 0, 3)
                if a:
                    project_qk(i + 1, 0)
                for k in range(8):
                    scores(i, 1, k)
                    if a and k < 7:
                        project_qk(i + 1, k + 1)
                if a:
                    project_nulls(i + 1)
                turn_nulls(i, 0)
                turn_probs(i, 0)
                if c:
                    cross_scores(i - 1, 0)
                turn_probs(i, 1)
                if c:
                    cross_scores(i - 1, 1)
                for k in range(2):
                    weigh_values(i, k)
                    turn_probs(i, k + 2)
                    if c:
                        cross_scores(i - 1, k + 2)
                weigh_values(i, 2)
                if c:
                    cross_values(i - 1, 0)
                weigh_values(i, 3)
                weigh_nulls(i, 0)
                if c:
                    cross_values(i - 1, 1)
                if w:
                    merge_ffn(g)
                turn_nulls(i, 1)
                turn_probs(i, 4)
                turn_probs(i, 5)
                for k in range(4, PC):
                    weigh_values(i, k)
                    if k + 2 < PC:
                        turn_probs(i, k + 2)
                    if w and k == 5:
                        turn_ffn(g)
                weigh_nulls(i, 1)
                if c:
                    pe.wait_ge(y_added, NT * i + 1)
                    turn_cross_probs(i - 1, 0)
                    turn_cross_probs(i - 1, 1)
                for k in range(4):
                    if a:
                        project_v(i + 1, k)
                    if c:
                        weigh_cross_values(i - 1, k)
                        if k < 2:
                            turn_cross_probs(i - 1, k + 2)
                for k in range(4):
                    if a:
                        turn_qk(i + 1, 2 * k)
                        turn_qk(i + 1, 2 * k + 1)
                    if c and k == 2:
                        x2_turn(i - 1)
                    if c and k == 3:
                        feed_forward(i - 1, g)
                    if a:
                        project_v(i + 1, 4 + k)

            schedule(pe, iteration)
            b = NB - 1
            read.clear()
            x1_turn(b)
            cross_q(b)
            for k in range(2):
                cross_scores(b, k)
            for k in range(2):
                cross_values(b, k)
            for k in range(2):
                cross_scores(b, k + 2)
            turn_cross_probs(b, 0)
            turn_cross_probs(b, 1)
            for k in range(4):
                weigh_cross_values(b, k)
                if k < 2:
                    turn_cross_probs(b, k + 2)
            x2_turn(b)
            feed_forward(b, GROUPS - 1)

        @block.vector
        def _(dve):
            steps = Steps(dve_step)

            def wait_apart(semaphore, value):
                if not isinstance(value, int):
                    value = dve.to_reg(value)
                dve.wait_ge(xin_loaded, 16)
                dve.wait_ge(semaphore, value)

            def ln_begin(name, src, tiles, count):
                for t in tiles:
                    steps.mark(dve.bn_stats(st[name][:, t, :], src[:, t, :]))
                wait_apart(dve_step, steps.value())
                for t in tiles:
                    steps.mark(dve.bn_aggr(mv[name][:, t, :], st[name][:, t, :]))
                steps.wait(dve)
                a, z = tiles[0], tiles[-1] + 1
                dve.tensor_scalar(ve[name][:, a:z], mv[name][:, a:z, 1], EPS, None, ALU.add).then_inc(var_ready[name], 1)

            def newton(y0, v, tmp, res, half):
                steps.mark(dve.tensor_tensor(tmp, y0, y0, ALU.mult))
                steps.wait(dve)
                steps.mark(dve.scalar_tensor_tensor(out=tmp, in0=tmp, scalar=-half, in1=v, op0=ALU.mult, op1=ALU.mult))
                steps.wait(dve)
                return dve.scalar_tensor_tensor(out=res, in0=tmp, scalar=1.5, in1=y0, op0=ALU.add, op1=ALU.mult)

            def ln_end(name, src, dst, tiles, count):
                dve.wait_ge(seed_ready[name], count)
                a, z = tiles[0], tiles[-1] + 1
                steps.mark(newton(sd[name][:, a:z], ve[name][:, a:z], nw[name][:, a:z], rs[name][:, a:z], 0.5))
                steps.wait(dve)
                for t in tiles:
                    last = dve.tensor_scalar(dst[:, t, :], src[:, t, :], mv[name][:, t, 0:1], rs[name][:, t:t + 1],
                                             ALU.subtract, ALU.mult)
                    if t != tiles[-1]:
                        steps.mark(last)
                return last

            def scale_rows():
                dve.wait_ge(c_loaded, 16 * 8)
                dve.scalar_tensor_tensor(out=kscale[:], in0=qks2[:, 0:1], scalar=-ATTN_SCALE * SEED_SCALE,
                                         in1=qks2[:, 1:2], op0=ALU.mult, op1=ALU.mult).then_inc(kscale_ready, 1)

            def split_wqk():
                steps.mark(dve.tensor_copy(wqk_hi[:], wqk_raw))
                steps.wait(dve)
                dve.tensor_tensor(wqk_lo[:], wqk_raw, wqk_hi[:].bitcast(F32), ALU.subtract).then_inc(wsplit_ready, 1)

            def norm_null_keys():
                dve.wait_ge(h_loaded, 16 * 7)
                steps.mark(dve.tensor_tensor(nksq[:], nkrow[:, 0:DH], nkrow[:, 0:DH], ALU.mult))
                steps.mark(dve.scalar_tensor_tensor(out=nksc[:, 0:DH], in0=nksc[:, 0:DH],
                                                    scalar=-ATTN_SCALE * SEED_SCALE, in1=nksc[:, DH:2 * DH],
                                                    op0=ALU.mult, op1=ALU.mult))
                steps.wait(dve)
                steps.mark(dve.tensor_reduce(nkst[:, 0:1], nksq[:], AX.X, ALU.add))
                steps.wait(dve)
                dve.tensor_scalar(nkst[:, 1:2], nkst[:, 0:1], 1e-24, None, ALU.max).then_inc(nkssq_ready, 1)
                dve.wait_ge(nkseed_ready, 1)
                steps.mark(newton(nkst[:, 3:4], nkst[:, 1:2], nkst[:, 4:5], nkst[:, 5:6], 0.5 * SEED_SCALE))
                steps.wait(dve)
                steps.mark(dve.scalar_tensor_tensor(out=nkrow[:, 0:DH], in0=nkrow[:, 0:DH], scalar=nkst[:, 5:6],
                                                    in1=nksc[:, 0:DH], op0=ALU.mult, op1=ALU.mult))
                steps.wait(dve)
                dve.tensor_copy(nkrow[:, DH:2 * DH], nkrow[:, 0:DH]).then_inc(nkrow_ready, 1)

            def split_wn():
                dve.wait_ge(wn_ready, 1)
                hi, lo = (w[:].rearrange("p (c r n) -> p c r n", r=2, n=NULLS) for w in (wn_hi, wn_lo))
                ps = [psJ[r][:, 0:NN // 2].rearrange("p (c n) -> p c n", n=NULLS) for r in range(2)]
                for r in range(2):
                    steps.mark(dve.tensor_copy(hi[:, :, r, :], ps[r]))
                steps.wait(dve)
                for r in range(2):
                    last = dve.tensor_tensor(lo[:, :, r, :], ps[r], hi[:, :, r, :].bitcast(F32), ALU.subtract)
                    if r == 0:
                        steps.mark(last)
                last.then_inc(wn_split, 1)

            def split_m():
                for c in range(H // 4):
                    dve.wait_ge(m_ready, c + 1)
                    hi, lo = (m[:].rearrange("p (c r d) -> p c r d", r=2, d=P)[:, 4 * (c // 2):4 * (c // 2) + 4, c % 2, :]
                              for m in (m_hi, m_lo))
                    ps = psJ[c % 2][:].rearrange("p (c d) -> p c d", d=P)
                    steps.mark(dve.tensor_copy(hi, ps))
                    steps.wait(dve)
                    dve.tensor_tensor(lo, ps, hi.bitcast(F32), ALU.subtract).then_inc(m_split, 1)
                dve.wait_ge(nullv_ready, 1)
                dve.tensor_copy(null_v[:], psJ[0][0:NN, 0:P]).then_inc(nullv_copied, 1)

            def make_alibi():
                dve.wait_ge(a_loaded, 32)
                for h, s in enumerate(slopes()):
                    dve.tensor_scalar(alibi[:, h, :], dist[:], float(s), None, ALU.mult).then_inc(alibi_ready, 1)

            def ln1_begin(n):
                dve.wait_ge(xin_loaded, 16 * (n + 1))
                ln_begin("ln1", xin, (0, 1), n + 1)

            def ln1_end(n):
                ln_end("ln1", xin, xn, (0, 1), n + 1).then_inc(xn_ready, 1)

            def split_xnT(n):
                dve.wait_ge(xnT_ready, n + 1)
                steps.mark(dve.tensor_scalar(xnT_hi[:], psJ[0][:, 0:SEQ], gam[:], None, ALU.mult))
                steps.wait(dve)
                dve.scalar_tensor_tensor(out=xnT_lo[:], in0=psJ[0][:, 0:SEQ], scalar=gam[:],
                                         in1=xnT_hi[:].bitcast(F32), op0=ALU.mult,
                                         op1=ALU.subtract).then_inc(xnT_split, 1)

            def sum_squares(n, t):
                dve.wait_ge(qk_squared, 2 * (NT * n + t + 1))
                steps.mark(dve.tensor_reduce(ssq[:, t, :], sq[:].rearrange("p (h d) -> p h d", d=DH), AX.X, ALU.add))
                steps.wait(dve)
                dve.tensor_scalar(ssq[:, t, :], ssq[:, t, :], 1e-24, None, ALU.max).then_inc(ssq_ready, 1)

            def norms(n, t):
                dve.wait_ge(qkseed_ready, NT * n + t + 1)
                newton(seedq[:, t, :], ssq[:, t, :], newt[:, t, :], rn[:, t, :], 0.5 * SEED_SCALE).then_inc(rn_ready, 1)

            def null_scores(n):
                dve.wait_ge(nullraw_copied, n + 1)
                dve.wait_ge(rn_ready, NT * (n + 1))
                steps.mark(dve.tensor_tensor(nullmul[:].rearrange("p t (h n) -> p t h n", n=NULLS),
                                             nullraw[:].rearrange("p t (h n) -> p t h n", n=NULLS),
                                             rn[:, :, 0:H].unsqueeze(3).broadcast_to([P, NT, H, NULLS]), ALU.mult))
                steps.wait(dve)
                steps.mark(dve.tensor_tensor(nullneg[:], nullmul[:], nullbias[:], ALU.add))
                steps.wait(dve)
                steps.mark(dve.tensor_reduce(nullmin[:], nullneg[:].rearrange("p t (h n) -> p t h n", n=NULLS),
                                             AX.X, ALU.min))
                steps.wait(dve)

            def copy_qk(n, c):
                t, j = c // 4, c % 4
                dve.wait_ge(qk_ready, QK_CHUNKS * n + c + 1)
                dve.tensor_copy(qk[t][:, 512 * j:512 * (j + 1)], psJ[c % 2][:]).then_inc(qk_copied_dve, 1)

            def copy_v(n, c):
                dve.wait_ge(v_ready, V_CHUNKS * n + c + 1)
                dve.tensor_copy(val[:, c // 4, 512 * (c % 4):512 * (c % 4) + 512], psJ[c % 2][:]).then_inc(v_copied_dve, 1)

            def copy_qT(n, k):
                t, half = k // 2, k % 2
                dve.wait_ge(qkT_ready, 4 * NT * n + 2 * k + 1)
                dve.tensor_copy(qT[:, 4 * half:4 * half + 4, P * t:P * (t + 1)],
                                psS[0][:].rearrange("p (c k) -> p c k", c=4)).then_inc(qT_copied, 1)

            def mask_scores(b, t, chunks):
                keys = P if t == 0 else SEQ
                for c in chunks:
                    wait_apart(scores_ready, PC * b + (0 if t == 0 else TILE_PC[0]) + c + 1)
                    for j, h in enumerate(score_heads(t, c)):
                        dve.tensor_tensor_reduce(pr[t][:, h, :], psS[c % 2][:, keys * j:keys * (j + 1)],
                                                 alibi[:, h, SEQ - keys:SEQ], 1.0, nullmin[:, t, h:h + 1],
                                                 ALU.add, ALU.min, nmin[:, t, h:h + 1]).then_inc(scores_masked, 1)

            def null_shift(b, t):
                dve.wait_ge(scores_masked, NT * H * b + H * (t + 1))
                dve.tensor_tensor(nulld[:, t, :].rearrange("p (h n) -> p h n", n=NULLS),
                                  nmin[:, t, :].unsqueeze(2).broadcast_to([P, H, NULLS]),
                                  nullneg[:, t, :].rearrange("p (h n) -> p h n", n=NULLS),
                                  ALU.subtract).then_inc(nulld_ready, 1)

            def denominators(b, t):
                dve.wait_ge(pn_ready, NT * b + t + 1)
                steps.mark(dve.tensor_reduce(den[:, t, :], dparts[:, t], AX.X, ALU.add))
                steps.wait(dve)
                dve.reciprocal(rden[:, t, :], den[:, t, :]).then_inc(rden_ready, 1)
                dve.wait_ge(rden_ready, NT * b + t + 1)
                dve.tensor_tensor(pnn[:, t, :].rearrange("p (h n) -> p h n", n=NULLS), dparts[:, t, :, 1:1 + NULLS],
                                  rden[:, t, :].unsqueeze(2).broadcast_to([P, H, NULLS]),
                                  ALU.mult).then_inc(pnn_ready, 1)

            def copy_pT(b, c):
                dve.wait_ge(probsT_ready, PC * b + c + 1)
                need(dve, pv_done, PC * b + c - 3)
                dve.tensor_copy(pT[c % 4][:], psT[c % 2][:]).then_inc(pT_copied_dve, 1)

            def add_y(b, t):
                dve.wait_ge(y_ready, NT * b + t + 1)
                if t == 0:
                    dve.wait_ge(xres_loaded, 16 * (b + 1))
                dve.tensor_tensor(r1[:, t, :], psY[t][:, 0:P], xres[:, t, :], ALU.add).then_inc(y_added, 1)
                dve.wait_ge(y_added, NT * b + t + 1)
                ln_begin("ln2", r1, (t,), NT * b + t + 1)

            def ln2_end(b, t):
                ln_end("ln2", r1, x1, (t,), NT * b + t + 1).then_inc(x1_ready, 1)

            def x1_plus_bias(b):
                dve.wait_ge(x1_ready, NT * (b + 1))
                steps.mark(dve.tensor_tensor(x1b[:], x1[:], bo[:].unsqueeze(1).broadcast_to([P, NT, P]), ALU.add))

            def cross_shift(b, k):
                t, half = k // 2, k % 2
                hs = slice(8 * half, 8 * half + 8)
                dve.wait_ge(xscores_ready, XC * b + k + 1)
                s = psS[half][:].rearrange("p (h k) -> p h k", h=8)
                steps.mark(dve.tensor_reduce(xmax[:, t, hs], s, AX.X, ALU.max))
                steps.wait(dve)
                dve.tensor_tensor(xp[t][:, hs, :], s, xmax[:, t, hs].unsqueeze(2).broadcast_to([P, 8, CTX]),
                                  ALU.subtract).then_inc(xs_sub, 1)

            def cross_denominators(b, t):
                dve.wait_ge(xexp_done, NT * b + t + 1)
                steps.mark(dve.tensor_reduce(xden[:, t, :], xp[t][:], AX.X, ALU.add))
                steps.wait(dve)
                dve.reciprocal(xrden[:, t, :], xden[:, t, :]).then_inc(xrden_ready, 1)

            def add_y2(b):
                dve.wait_ge(xpv_done, XC * (b + 1))
                dve.tensor_tensor(r2[:], psY[0][:, 0:SEQ].rearrange("p (t d) -> p t d", t=NT), x1b[:],
                                  ALU.add).then_inc(y2_added, 1)
                dve.wait_ge(y2_added, b + 1)
                ln_begin("ln3", r2, (0, 1), b + 1)

            def ln3_end(b, g):
                ln_end("ln3", r2, x2, (0, 1), b + 1).then_inc(x2_ready, 1)
                dve.wait_ge(x2_ready, b + 1)
                dve.wait_ge(w12_copied, g + 1)
                steps.mark(dve.tensor_tensor(x2b[:], x2[:], w12[:, 1:2, :].broadcast_to([P, NT, P]), ALU.add))

            def add_h2(b):
                dve.wait_ge(h2_ready, b + 1)
                steps.wait(dve)
                dve.tensor_tensor(r3[:], psY[0][:, 0:SEQ].rearrange("p (t d) -> p t d", t=NT), x2b[:],
                                  ALU.add).then_inc(h2_added, 1)
                dve.wait_ge(h2_added, b + 1)
                ln_begin("ln4", r3, (0, 1), b + 1)

            def ln4_end(b):
                need(dve, stored, 16 * b)
                ln_end("ln4", r3, x3, (0, 1), b + 1).then_inc(x3_ready, 1)

            ln1_begin(0)
            scale_rows()
            ln1_end(0)
            split_wqk()
            norm_null_keys()
            split_wn()
            split_xnT(0)
            split_m()
            make_alibi()
            for c in range(1, QK_CHUNKS, 2):
                copy_qk(0, c)
            sum_squares(0, 0)
            for c in range(0, 4, 2):
                copy_v(0, c)
            norms(0, 0)
            sum_squares(0, 1)
            for c in range(4, V_CHUNKS, 2):
                copy_v(0, c)
            norms(0, 1)
            null_scores(0)
            for k in range(2 * NT):
                copy_qT(0, k)
            dve.wait_ge(alibi_ready, H)

            def iteration(i, a, c, w, g):
                if a:
                    ln1_begin(i + 1)
                need(dve, probsT_ready, PC * (i - 1) + TILE_PC[0])
                mask_scores(i, 0, (0,))
                if a:
                    ln1_end(i + 1)
                mask_scores(i, 0, (1, 2))
                if a:
                    split_xnT(i + 1)
                mask_scores(i, 0, (3,))
                null_shift(i, 0)
                need(dve, probsT_ready, PC * i)
                for k in range(8):
                    mask_scores(i, 1, (k,))
                    if a and k % 2 == 0:
                        copy_qk(i + 1, k + 1)
                    if k == 3:
                        denominators(i, 0)
                null_shift(i, 1)
                copy_pT(i, 0)
                if c:
                    cross_shift(i - 1, 0)
                    cross_shift(i - 1, 1)
                copy_pT(i, 2)
                denominators(i, 1)
                if c:
                    cross_shift(i - 1, 2)
                    cross_shift(i - 1, 3)
                if a:
                    sum_squares(i + 1, 0)
                if c:
                    cross_denominators(i - 1, 0)
                add_y(i, 0)
                copy_pT(i, 4)
                if c:
                    cross_denominators(i - 1, 1)
                ln2_end(i, 0)
                copy_pT(i, 6)
                if a:
                    norms(i + 1, 0)
                    sum_squares(i + 1, 1)
                copy_pT(i, 8)
                if a:
                    norms(i + 1, 1)
                copy_pT(i, 10)
                if a:
                    null_scores(i + 1)
                add_y(i, 1)
                if a:
                    copy_v(i + 1, 0)
                ln2_end(i, 1)
                if a:
                    copy_v(i + 1, 2)
                if c:
                    add_y2(i - 1)
                x1_plus_bias(i)
                if a:
                    copy_qT(i + 1, 0)
                    copy_v(i + 1, 4)
                if c:
                    ln3_end(i - 1, g)
                if a:
                    copy_qT(i + 1, 1)
                    copy_qT(i + 1, 2)
                    copy_v(i + 1, 6)
                    copy_qT(i + 1, 3)
                if c:
                    add_h2(i - 1)
                    ln4_end(i - 1)

            schedule(dve, iteration, steps, DVE_STEPS_A_TURN)
            b = NB - 1
            for k in range(XC):
                cross_shift(b, k)
            cross_denominators(b, 0)
            cross_denominators(b, 1)
            add_y2(b)
            ln3_end(b, GROUPS - 1)
            add_h2(b)
            ln4_end(b)

        @block.scalar
        def _(act):
            steps = Steps(act_step)
            act.preload_act_table_set("natural_log_exp_and_others")

            def rsqrt_seed(v, tmp, res, scale):
                steps.mark(act.activation(tmp, v, ACT.Ln, scale=scale))
                steps.wait(act)
                return act.activation(res, tmp, ACT.Exp, scale=-0.5)

            def ln_seed(name, tiles, count):
                act.wait_ge(var_ready[name], count)
                a, z = tiles[0], tiles[-1] + 1
                rsqrt_seed(ve[name][:, a:z], lv[name][:, a:z], sd[name][:, a:z], 1.0).then_inc(seed_ready[name], 1)

            def null_keys():
                act.wait_ge(nkssq_ready, 1)
                rsqrt_seed(nkst[:, 1:2], nkst[:, 2:3], nkst[:, 3:4], SEED_SCALE).then_inc(nkseed_ready, 1)
                act.wait_ge(nkT_ready, 1)
                act.activation(nkT[:], psJ[0][:, 0:NN], ACT.Copy).then_inc(nkT_copied, 1)

            def context_kv():
                for k in range(4):
                    act.wait_ge(kvx_ready, k + 1)
                    dst = (kTx, vTx)[k // 2][:, 512 * (k % 2):512 * (k % 2) + 512]
                    act.activation(dst, psJ[(k + 1) % 2][:], ACT.Identity,
                                   bias=xb[:, 1 + k // 2:2 + k // 2]).then_inc(kvx_copied, 1)

            def copy_qk(n, c):
                t, j = c // 4, c % 4
                act.wait_ge(qk_ready, QK_CHUNKS * n + c + 1)
                act.activation(qk[t][:, 512 * j:512 * (j + 1)], psJ[c % 2][:], ACT.Copy).then_inc(qk_copied_act, 1)

            def square_qk(n, t):
                act.wait_ge(qk_copied_act, QK_CHUNKS // 2 * n + 2 * (t + 1))
                act.wait_ge(qk_copied_dve, QK_CHUNKS // 2 * n + 2 * (t + 1))
                need(act, ssq_ready, NT * n + t)
                for half in range(2):
                    col = slice(HD * half, HD * (half + 1))
                    act.activation(sq[:, col], qk[t][:, col], ACT.Square).then_inc(qk_squared, 1)

            def qk_seed(n, t):
                act.wait_ge(ssq_ready, NT * n + t + 1)
                rsqrt_seed(ssq[:, t, :], lnq[:, t, :], seedq[:, t, :], SEED_SCALE).then_inc(qkseed_ready, 1)

            def copy_nullraw(n):
                act.wait_ge(nullraw_ready, n + 1)
                act.activation(nullraw[:].rearrange("p t n -> p (t n)"), psJ[0][:, 0:NT * NN],
                               ACT.Copy).then_inc(nullraw_copied, 1)

            def copy_v(n, c):
                act.wait_ge(v_ready, V_CHUNKS * n + c + 1)
                act.activation(val[:, c // 4, 512 * (c % 4):512 * (c % 4) + 512], psJ[c % 2][:],
                               ACT.Copy).then_inc(v_copied_act, 1)

            def copy_kT(n, k):
                t, half = k // 2, k % 2
                act.wait_ge(qkT_ready, 4 * NT * n + 2 * k + 2)
                act.activation(kT[:, 4 * half:4 * half + 4, P * t:P * (t + 1)],
                               psS[1][:].rearrange("p (c k) -> p c k", c=4), ACT.Copy,
                               scale=kscale[:]).then_inc(kT_copied, 1)

            def exponentials(b, t, chunks):
                for c in chunks:
                    for j, h in enumerate(score_heads(t, c)):
                        act.wait_ge(scores_masked, NT * H * b + H * t + len(score_heads(t, c)) * c + j + 1)
                        act.activation(pr[t][:, h, :], pr[t][:, h, :], ACT.Exp, bias=nmin[:, t, h:h + 1], scale=-1.0,
                                       accum_out=dparts[:, t, h, 0:1]).then_inc(exp_done, 1)

            def null_exponentials(b, t):
                act.wait_ge(nulld_ready, NT * b + t + 1)
                act.activation(dparts[:, t, :, 1:1 + NULLS], nulld[:, t, :].rearrange("p (h n) -> p h n", n=NULLS),
                               ACT.Exp).then_inc(pn_ready, 1)

            def copy_pnT(b, t):
                act.wait_ge(nullT_ready, NT * b + t + 1)
                act.activation(pnT[:, t, :], psJ[1][0:NN, 0:P], ACT.Copy).then_inc(pnT_copied, 1)

            def copy_pT(b, c):
                act.wait_ge(probsT_ready, PC * b + c + 1)
                need(act, pv_done, PC * b + c - 3)
                act.activation(pT[c % 4][:], psT[c % 2][:], ACT.Copy).then_inc(pT_copied_act, 1)

            def copy_x1T(b):
                act.wait_ge(x1T_ready, b + 1)
                act.activation(x1T[:], psJ[1][:, 0:SEQ], ACT.Copy).then_inc(x1T_copied, 1)

            def copy_xqT(b):
                act.wait_ge(xqT_ready, b + 1)
                act.activation(xqT[:], psJ[1][:, 0:SEQ], ACT.Identity, bias=xb[:, 0:1]).then_inc(xqT_copied, 1)

            def cross_exponentials(b, t):
                act.wait_ge(xs_sub, XC * b + 2 * (t + 1))
                act.activation(xp[t][:], xp[t][:], ACT.Exp, scale=float(XD) ** -0.5).then_inc(xexp_done, 1)

            def copy_xv(b, c):
                act.wait_ge(xv_ready, 2 * b + c + 1)
                act.activation(xv[:, 4 * c:4 * c + 4, :].rearrange("p c d -> p (c d)"), psJ[c][:],
                               ACT.Copy).then_inc(xv_copied, 1)

            def copy_w12raw(g):
                act.wait_ge(w12raw_ready, g + 1)
                act.activation(w12raw[:, 0, :], psJ[0][:, 0:P], ACT.Copy).then_inc(w12raw_copied, 1)
                act.activation(w12raw[:, 1, :], psJ[0][:, P:P + 1].broadcast_to([P, P]), ACT.Identity,
                               bias=b2s[:]).then_inc(w12raw_copied, 1)

            def copy_w12(g):
                act.wait_ge(w12_ready, g + 1)
                act.activation(w12[:].rearrange("p a d -> p (a d)"), psJ[1][:, 0:2 * P], ACT.Copy).then_inc(w12_copied, 1)

            def copy_xpT(b, k):
                act.wait_ge(xprobsT_ready, XC * b + k + 1)
                need(act, xpv_done, XC * b + k - 1)
                act.activation(xpT[k % 2][:], psT[k % 2][:], ACT.Copy).then_inc(xpT_copied, 1)

            def copy_x2T(b):
                act.wait_ge(x2T_ready, b + 1)
                act.activation(x2T[:], psJ[1][:, 0:SEQ], ACT.Copy).then_inc(x2T_copied, 1)

            ln_seed("ln1", (0, 1), 1)
            null_keys()
            act.wait_ge(c_loaded, 16 * 8)
            act.wait_ge(kscale_ready, 1)
            act.wait_ge(g_loaded, 16 * 10)
            context_kv()
            copy_qk(0, 0)
            copy_qk(0, 2)
            copy_qk(0, 4)
            copy_qk(0, 6)
            copy_nullraw(0)
            square_qk(0, 0)
            copy_v(0, 1)
            qk_seed(0, 0)
            copy_v(0, 3)
            square_qk(0, 1)
            copy_v(0, 5)
            qk_seed(0, 1)
            copy_v(0, 7)
            for k in range(2 * NT):
                copy_kT(0, k)

            def iteration(i, a, c, w, g):
                if a:
                    ln_seed("ln1", (0, 1), i + 2)
                exponentials(i, 0, (0,))
                if c:
                    copy_x1T(i - 1)
                exponentials(i, 0, (1,))
                if c:
                    copy_xqT(i - 1)
                exponentials(i, 0, (2, 3))
                if a:
                    copy_qk(i + 1, 0)
                null_exponentials(i, 0)
                for k in range(8):
                    exponentials(i, 1, (k,))
                    if a and k % 2 and k < 7:
                        copy_qk(i + 1, k + 1)
                null_exponentials(i, 1)
                if a:
                    copy_nullraw(i + 1)
                copy_pnT(i, 0)
                copy_pT(i, 1)
                if c:
                    cross_exponentials(i - 1, 0)
                if a:
                    square_qk(i + 1, 0)
                copy_pT(i, 3)
                if c:
                    copy_xv(i - 1, 0)
                    cross_exponentials(i - 1, 1)
                    copy_xv(i - 1, 1)
                if a:
                    qk_seed(i + 1, 0)
                ln_seed("ln2", (0,), NT * i + 1)
                if w:
                    copy_w12raw(g)
                copy_pnT(i, 1)
                copy_pT(i, 5)
                if a:
                    square_qk(i + 1, 1)
                copy_pT(i, 7)
                if w:
                    copy_w12(g)
                if a:
                    qk_seed(i + 1, 1)
                copy_pT(i, 9)
                copy_pT(i, 11)
                if c:
                    copy_xpT(i - 1, 0)
                    copy_xpT(i - 1, 1)
                ln_seed("ln2", (1,), NT * i + 2)
                if c:
                    copy_xpT(i - 1, 2)
                if a:
                    copy_v(i + 1, 1)
                if c:
                    copy_xpT(i - 1, 3)
                if a:
                    copy_v(i + 1, 3)
                    copy_kT(i + 1, 0)
                if c:
                    ln_seed("ln3", (0, 1), i)
                if a:
                    copy_kT(i + 1, 1)
                    copy_v(i + 1, 5)
                    copy_kT(i + 1, 2)
                if c:
                    copy_x2T(i - 1)
                if a:
                    copy_kT(i + 1, 3)
                    copy_v(i + 1, 7)
                if c:
                    ln_seed("ln4", (0, 1), i)

            schedule(act, iteration, steps, ACT_STEPS_A_TURN)
            b = NB - 1
            copy_x1T(b)
            copy_xqT(b)
            cross_exponentials(b, 0)
            copy_xv(b, 0)
            copy_xv(b, 1)
            cross_exponentials(b, 1)
            for k in range(XC):
                copy_xpT(b, k)
            ln_seed("ln3", (0, 1), NB)
            copy_x2T(b)
            ln_seed("ln4", (0, 1), NB)

        @block.gpsimd
        def _(pool):
            def norm_qk(n, t):
                pool.wait_ge(rn_ready, NT * n + t + 1)
                for k in range(2):
                    v = qk[t][:, HD * k:HD * (k + 1)].rearrange("p (h d) -> p h d", d=DH)
                    pool.tensor_tensor(v, v, rn[:, t, H * k:H * (k + 1)].unsqueeze(2).broadcast_to([P, H, DH]),
                                       ALU.mult).then_inc(qk_normed, 1)

            def norm_probs(b, t):
                pool.wait_ge(exp_done, NT * H * b + H * (t + 1))
                pool.wait_ge(rden_ready, NT * b + t + 1)
                heads = 4 if t == 0 else 2
                for c in range(TILE_PC[t]):
                    hs = slice(heads * c, heads * (c + 1))
                    pool.tensor_tensor(pr[t][:, hs, :], pr[t][:, hs, :],
                                       rden[:, t, hs].unsqueeze(2).broadcast_to([P, heads, P * (t + 1)]),
                                       ALU.mult).then_inc(probs_normed, 1)

            def norm_cross(b):
                for t in range(NT):
                    pool.wait_ge(xrden_ready, NT * b + t + 1)
                    pool.tensor_tensor(xp[t][:], xp[t][:], xrden[:, t, :].unsqueeze(2).broadcast_to([P, XH, CTX]),
                                       ALU.mult).then_inc(xprobs_normed, 1)

            def spread_context(b):
                mask = hmask[:].unsqueeze(2).broadcast_to([P, XH, CTX])
                if isinstance(b, int):
                    col = slice(CTX * b, CTX * (b + 1))
                else:
                    col = bass.ds(CTX * b, CTX)
                need(pool, xscores_ready, XC * b)
                pool.tensor_tensor(kexp[:], mask, kTx[:, col].unsqueeze(1).broadcast_to([P, XH, CTX]),
                                   ALU.mult).then_inc(kexp_ready, 1)
                need(pool, xv_ready, 2 * b)
                pool.tensor_tensor(vexp[:], mask, vTx[:, col].unsqueeze(1).broadcast_to([P, XH, CTX]),
                                   ALU.mult).then_inc(vexp_ready, 1)

            pool.wait_ge(g_loaded, 16 * 10)
            pool.wait_ge(kvx_copied, 4)
            norm_qk(0, 0)
            norm_qk(0, 1)

            def iteration(i, a, c, w, g):
                norm_probs(i, 0)
                norm_probs(i, 1)
                if c:
                    norm_cross(i - 1)
                if a:
                    norm_qk(i + 1, 0)
                    norm_qk(i + 1, 1)
                spread_context(i)

            schedule(pool, iteration)
            norm_cross(NB - 1)


DVE_STEPS_A_TURN = 108
ACT_STEPS_A_TURN = 14


def kernel(x, ctx_1024, L0_attn_gamma, L0_attn_w_q, L0_attn_w_kv, L0_attn_null_kv, L0_attn_q_scale,
           L0_attn_k_scale, L0_attn_w_out, L0_xattn_wq, L0_xattn_bq, L0_xattn_wk, L0_xattn_bk, L0_xattn_wv,
           L0_xattn_bv, L0_xattn_wo, L0_xattn_bo, L0_ffn_W1, L0_ffn_b1, L0_ffn_W2, L0_ffn_b2):
    import concourse.bacc as bacc
    from concourse.bass_utils import run_bass_kernel_spmd

    def pairs(w):
        return w.reshape(HP, P, w.shape[1]).transpose(1, 0, 2)

    def block_diagonal(w):
        w = np.asarray(w)
        m = np.zeros((P, P), w.dtype)
        for h in range(XH):
            m[XD * h:XD * (h + 1), XD * h:XD * (h + 1)] = w[h].T
        return m

    w_q, w_kv, w_out = np.asarray(L0_attn_w_q), np.asarray(L0_attn_w_kv), np.asarray(L0_attn_w_out)
    nkv = np.asarray(L0_attn_null_kv).reshape(H, NULLS, 2, DH)
    nvT = np.zeros((HP, 2, DH, H, NULLS), nkv.dtype)
    for h in range(H):
        nvT[h // 2, h % 2, :, h, :] = nkv[h, :, 1].T
    q_pos, k_pos = np.arange(P)[:, None] + P, np.arange(SEQ)[None, :]
    dist = np.where(k_pos > q_pos, MASKED, q_pos - k_pos).astype(np.float32)
    null_dist = (np.arange(SEQ).reshape(NT, P, 1, 1) + NULLS - np.arange(NULLS)).astype(np.float32)
    nullbias = (null_dist * slopes()[None, None, :, None]).reshape(NT, P, NN).transpose(1, 0, 2)
    hmask = (np.arange(P)[:, None] // XD == np.arange(XH)[None, :]).astype(np.float32)
    arrays = {
        "x": x,
        "ctxT": np.asarray(ctx_1024).reshape(NB * CTX, P).T,
        "gamma": np.asarray(L0_attn_gamma).reshape(P, 1),
        "w_q": w_q,
        "w_kv": w_kv,
        "wqT": pairs(w_q.T),
        "wvT": pairs(w_kv[:, HD:].T),
        "wout": pairs(w_out),
        "nk": nkv[:, :, 0].reshape(NN, DH),
        "nvT": nvT.reshape(HP, P, NN).transpose(1, 0, 2),
        "q_scale": np.asarray(L0_attn_q_scale).reshape(DH, 1),
        "k_scale": np.asarray(L0_attn_k_scale).reshape(DH, 1),
        "xwq": block_diagonal(L0_xattn_wq),
        "xwk": block_diagonal(L0_xattn_wk),
        "xwv": block_diagonal(L0_xattn_wv),
        "xbq": np.asarray(L0_xattn_bq).reshape(P, 1),
        "xbk": np.asarray(L0_xattn_bk).reshape(P, 1),
        "xbv": np.asarray(L0_xattn_bv).reshape(P, 1),
        "xwoT": np.asarray(L0_xattn_wo).T,
        "xbo": np.asarray(L0_xattn_bo).reshape(1, P),
        "w1b": np.concatenate([np.asarray(L0_ffn_W1), np.asarray(L0_ffn_b1)[:, :, None]], axis=2),
        "w2T": np.asarray(L0_ffn_W2).transpose(0, 2, 1),
        "b2": np.asarray(L0_ffn_b2).reshape(GROUPS, P, 1),
        "ident_in": np.eye(P, dtype=np.float32),
        "dist_in": dist,
        "nullbias_in": nullbias,
        "hmask_in": hmask,
    }
    arrays = {n: np.ascontiguousarray(a) for n, a in arrays.items()}
    nc = bacc.Bacc("TRN2", target_bir_lowering=False, num_devices=1)
    args = {n: nc.dram_tensor(n, a.shape, mybir.dt.from_np(a.dtype), kind="ExternalInput").ap()
            for n, a in arrays.items()}
    out = nc.dram_tensor("out", (NB, SEQ, P), F32, kind="ExternalOutput").ap()
    program(nc, **args, out=out)
    r = run_bass_kernel_spmd(nc, [arrays], core_ids=[0])
    return r.results[0]["out"]
```

```python
import math
from contextlib import ExitStack

import numpy as np
import concourse.bass as bass
from concourse import mybir

F32 = mybir.dt.float32
F32R = mybir.dt.float32r
ALU = mybir.AluOpType
ACT = mybir.ActivationFunctionType
AX = mybir.AxisListType

P = 128
NB, SEQ = 16, 256
NT = SEQ // P
H, DH = 16, 64
HP = H // 2
HD = H * DH
NULLS = 2
NN = H * NULLS
CTX = 64
XH, XD = 16, 8
XHALF = 8
GROUPS = 8
INTER = 512
OC = INTER // P
EPS = 1e-5
ATTN_SCALE = 8.0
SEED_SCALE = 65536.0
MASKED = 1e30

QK_CHUNKS = 8
V_CHUNKS = 8
QK_DVE, QK_ACT = (0, 1, 3), (2, 4, 5, 6, 7)
V_DVE, V_ACT = (2,), (0, 1, 3, 4, 5, 6, 7)
PT_DVE, PT_ACT = (0, 2, 6, 8, 10), (1, 3, 4, 5, 7, 9, 11)
PC = 12
TILE_PC = (4, 8)
XC = 4


def slopes():
    start = 2.0 ** (-2.0 ** (-(math.log2(H) - 3.0)))
    return np.array([start * start ** i for i in range(H)], dtype=np.float32)


class Steps:

    def __init__(self, sem):
        self.sem, self.n, self.offset = sem, 0, 0

    def mark(self, ins):
        ins.then_inc(self.sem, 1)
        self.n += 1

    def value(self):
        return self.n + self.offset

    def wait(self, eng):
        eng.wait_ge(self.sem, self.value())

    def enter_loop(self, i, per_turn):
        self.offset, self.before, self.per_turn = i * per_turn, self.n, per_turn

    def leave_loop(self, turns):
        assert self.n - self.before == self.per_turn, ("steps of a turn", self.n - self.before)
        self.n, self.offset = self.before + turns * self.per_turn, 0


def chunks_to(chunks, n, c):
    return len(chunks) * n + sum(k <= c for k in chunks)


def score_heads(t, c):
    n = 4 if t == 0 else 2
    return [2 * (n * (c // 2) + j) + c % 2 for j in range(n)]


def need(eng, sem, value):
    if not (isinstance(value, int) and value <= 0):
        eng.wait_ge(sem, value)


def program(nc, x, ctxT, gamma, w_q, w_kv, wqT, wvT, wout, nk, nvT, q_scale, k_scale,
            xwq, xwk, xwv, xbq, xbk, xbv, xwoT, xbo, w1b, w2T, b2, ident_in, dist_in, nullbias_in,
            hmask_in, hmask2_in, out):
    with ExitStack() as ctx:
        def sb(name, shape, dt=F32):
            return ctx.enter_context(nc.sbuf_tensor(name, shape, dt))

        def sem(name):
            return ctx.enter_context(nc.semaphore(name))

        psS = [ctx.enter_context(nc.psum_tensor(f"psS{k}", [P, 512], F32)) for k in range(2)]
        psT = [ctx.enter_context(nc.psum_tensor(f"psT{k}", [P, 512], F32)) for k in range(2)]
        psJ = [ctx.enter_context(nc.psum_tensor(f"psJ{k}", [P, 512], F32)) for k in range(2)]
        psY = [ctx.enter_context(nc.psum_tensor(f"psY{k}", [P, 512], F32)) for k in range(2)]

        ident = sb("ident", [P, P])
        alibi = sb("alibi", [P, H, SEQ])
        nullbias = sb("nullbias", [P, NT, NN])
        hmask = sb("hmask", [P, XH])
        hmask2 = sb("hmask2", [P, XHALF])
        gam = sb("gam", [P, 1])
        qks2 = sb("qks2", [P, 2])
        kscale = sb("kscale", [P, 1])
        wqk_hi = sb("wqk_hi", [P, 2 * HD], F32R)
        wqk_lo = sb("wqk_lo", [P, 2 * HD], F32R)
        wn_hi = sb("wn_hi", [P, NN], F32R)
        wn_lo = sb("wn_lo", [P, NN], F32R)
        m_hi = sb("m_hi", [P, H * P], F32R)
        m_lo = sb("m_lo", [P, H * P], F32R)
        null_v = sb("null_v", [NN, P])
        nkst = sb("nkst", [NN, 8])
        nkT = sb("nkT", [P, NN])
        xw = sb("xw", [P, 5, P])
        xb = sb("xb", [P, 5])
        xwo = sb("xwo", [P, P])
        bo = sb("bo", [P, P])
        kTx = sb("kTx", [P, 2, NB * CTX], F32R)
        vTx = sb("vTx", [P, NB * CTX])
        w1s = sb("w1s", [P, OC, P + 1])
        w2s = sb("w2s", [P, OC, P])
        b2s = sb("b2s", [P, 1])
        w12raw = sb("w12raw", [P, 2, P])
        w12 = sb("w12", [P, 2, P])
        xin = sb("xin", [P, NT, P])
        xn = sb("xn", [P, NT, P])
        xnT_hi = sb("xnT_hi", [P, SEQ], F32R)
        xnT_lo = sb("xnT_lo", [P, SEQ], F32R)
        qk = [sb(f"qk{t}", [P, 2 * HD]) for t in range(NT)]
        sq = sb("sq", [P, 2 * HD])
        ssq = sb("ssq", [P, NT, 2 * H])
        lnq = sb("lnq", [P, NT, 2 * H])
        seedq = sb("seedq", [P, NT, 2 * H])
        newt = sb("newt", [P, NT, 2 * H])
        rn = sb("rn", [P, NT, 2 * H])
        nullraw = sb("nullraw", [P, NT, NN])
        nullmul = sb("nullmul", [P, NT, NN])
        nullneg = sb("nullneg", [P, NT, NN])
        nullmin = sb("nullmin", [P, NT, H])
        qT = sb("qT", [P, HP, SEQ])
        kT = sb("kT", [P, HP, SEQ])
        val = sb("val", [P, NT, H * P])
        xres = sb("xres", [P, NT, P])
        pr = [sb(f"pr{t}", [P, H, P * (t + 1)]) for t in range(NT)]
        nmin = sb("nmin", [P, NT, H])
        nulld = sb("nulld", [P, NT, NN])
        dparts = sb("dparts", [P, NT, H, 1 + NULLS])
        den = sb("den", [P, NT, H])
        rden = sb("rden", [P, NT, H])
        pnn = sb("pnn", [P, NT, NN])
        pnT = sb("pnT", [NN, NT, P])
        pT = [sb(f"pT{k}", [P, 512]) for k in range(4)]
        r1 = sb("r1", [P, NT, P])
        x1 = sb("x1", [P, NT, P])
        x1b = sb("x1b", [P, NT, P])
        x1T = sb("x1T", [P, SEQ])
        xqT_hi = sb("xqT_hi", [P, 2, SEQ], F32R)
        xqT_lo = sb("xqT_lo", [DH, 2, SEQ], F32R)
        kexp = sb("kexp", [P, 2, XHALF, CTX], F32R)
        vexp = sb("vexp", [P, XH, CTX])
        xv = sb("xv", [P, XH // 2, P])
        xmax = sb("xmax", [P, NT, XH])
        xp = [sb(f"xp{t}", [P, XH, CTX]) for t in range(NT)]
        xden = sb("xden", [P, NT, XH])
        xrden = sb("xrden", [P, NT, XH])
        xpT = [sb(f"xpT{k}", [P, 512]) for k in range(2)]
        r2 = sb("r2", [P, NT, P])
        x2 = sb("x2", [P, NT, P])
        x2b = sb("x2b", [P, NT, P])
        x2T = sb("x2T", [P, SEQ])
        r3 = r2
        x3 = sb("x3", [P, NT, P])
        LN = ("ln1", "ln2", "ln3", "ln4")
        st = {n: sb(f"{n}_st", [P, NT, 6]) for n in LN}
        mv = {n: sb(f"{n}_mv", [P, NT, 2]) for n in LN}
        ve = {n: sb(f"{n}_ve", [P, NT]) for n in LN}
        lv = {n: sb(f"{n}_lv", [P, NT]) for n in LN}
        sd = {n: sb(f"{n}_sd", [P, NT]) for n in LN}
        nw = {n: sb(f"{n}_nw", [P, NT]) for n in LN}
        rs = {n: sb(f"{n}_rs", [P, NT]) for n in LN}

        wqk_raw = pr[1][:, 0:8, :].rearrange("p h k -> p (h k)")
        wvT_s, wout_s = (pr[1][:, 8 + 4 * k:12 + 4 * k, :].rearrange("p h k -> p (h k)")
                         .rearrange("p (c d) -> p c d", c=HP) for k in range(2))
        wqT_s = pr[0][:, 0:8, :]
        nvT_s = pr[0][:, 8:10, :].rearrange("p h k -> p (h k)").rearrange("p (c n) -> p c n", c=HP)
        dist = x3[:].rearrange("p t d -> p (t d)")
        nkrow, nksc = (xp[1][0:NN, 2 * k:2 * k + 2, :].rearrange("p h k -> p (h k)") for k in range(2))
        nksq = xp[1][0:NN, 4, :]
        ctxT_s = xp[0][:].rearrange("p h k -> p (h k)")

        wq_loaded = sem("wq_loaded")
        wk_loaded = sem("wk_loaded")
        c_loaded = sem("c_loaded")
        s_loaded = sem("s_loaded")
        n_loaded = sem("n_loaded")
        h_loaded = sem("h_loaded")
        vo_loaded = sem("vo_loaded")
        a_loaded = sem("a_loaded")
        b_loaded = sem("b_loaded")
        g_loaded = sem("g_loaded")
        xin_loaded = sem("xin_loaded")
        xres_loaded = sem("xres_loaded")
        ffn_loaded = sem("ffn_loaded")
        stored = sem("stored")
        nkT_ready = sem("nkT_ready")
        wn_ready = sem("wn_ready")
        m_ready = sem("m_ready")
        nullv_ready = sem("nullv_ready")
        kvx_ready = sem("kvx_ready")
        xnT_ready = sem("xnT_ready")
        qk_ready = sem("qk_ready")
        nullraw_ready = sem("nullraw_ready")
        qkT_ready = sem("qkT_ready")
        v_ready = sem("v_ready")
        scores_ready = sem("scores_ready")
        nullT_ready = sem("nullT_ready")
        probsT_ready = sem("probsT_ready")
        pv_done = sem("pv_done")
        y_ready = sem("y_ready")
        x1T_ready = sem("x1T_ready")
        xqT_ready = sem("xqT_ready")
        xscores_ready = sem("xscores_ready")
        xv_ready = sem("xv_ready")
        w12raw_ready = sem("w12raw_ready")
        w12_ready = sem("w12_ready")
        xprobsT_ready = sem("xprobsT_ready")
        xpv_done = sem("xpv_done")
        y2_ready = sem("y2_ready")
        x2T_ready = sem("x2T_ready")
        h2_ready = sem("h2_ready")
        dve_step = sem("dve_step")
        kscale_ready = sem("kscale_ready")
        nkssq_ready = sem("nkssq_ready")
        nkrow_ready = sem("nkrow_ready")
        wsplit_ready = sem("wsplit_ready")
        wn_split = sem("wn_split")
        m_split = sem("m_split")
        nullv_copied = sem("nullv_copied")
        xn_ready = sem("xn_ready")
        xnT_split = sem("xnT_split")
        ssq_ready = sem("ssq_ready")
        rn_ready = sem("rn_ready")
        qT_copied = sem("qT_copied")
        qk_copied_dve = sem("qk_copied_dve")
        v_copied_dve = sem("v_copied_dve")
        scores_masked = sem("scores_masked")
        nulld_ready = sem("nulld_ready")
        rden_ready = sem("rden_ready")
        pnn_ready = sem("pnn_ready")
        pT_copied_dve = sem("pT_copied_dve")
        y_added = sem("y_added")
        xqT_split = sem("xqT_split")
        kx_split = sem("kx_split")
        x1_ready = sem("x1_ready")
        xs_sub = sem("xs_sub")
        xrden_ready = sem("xrden_ready")
        y2_added = sem("y2_added")
        x2_ready = sem("x2_ready")
        h2_added = sem("h2_added")
        x3_ready = sem("x3_ready")
        var_ready = {n: sem(f"{n}_var_ready") for n in LN}
        alibi_ready = sem("alibi_ready")
        act_step = sem("act_step")
        nkseed_ready = sem("nkseed_ready")
        nkT_copied = sem("nkT_copied")
        kvx_copied = sem("kvx_copied")
        seed_ready = {n: sem(f"{n}_seed_ready") for n in LN}
        qk_squared = sem("qk_squared")
        qkseed_ready = sem("qkseed_ready")
        nullraw_copied = sem("nullraw_copied")
        kT_copied = sem("kT_copied")
        qk_copied_act = sem("qk_copied_act")
        v_copied_act = sem("v_copied_act")
        exp_done = sem("exp_done")
        pn_ready = sem("pn_ready")
        pnT_copied = sem("pnT_copied")
        pT_copied_act = sem("pT_copied_act")
        x1T_copied = sem("x1T_copied")
        xqT_copied = sem("xqT_copied")
        xexp_done = sem("xexp_done")
        xv_copied = sem("xv_copied")
        w12raw_copied = sem("w12raw_copied")
        w12_copied = sem("w12_copied")
        xpT_copied = sem("xpT_copied")
        x2T_copied = sem("x2T_copied")
        qk_normed = sem("qk_normed")
        probs_normed = sem("probs_normed")
        xprobs_normed = sem("xprobs_normed")
        kexp_ready = sem("kexp_ready")
        vexp_ready = sem("vexp_ready")
        x1b_ready = sem("x1b_ready")
        x2b_ready = sem("x2b_ready")

        x_dram = x.rearrange("b (t p) d -> p b t d", p=P)
        out_dram = out.rearrange("b (t p) d -> p b t d", p=P)
        w1_dram = w1b.rearrange("g (c p) h -> p g c h", p=P)
        w2_dram = w2T.rearrange("g (c p) h -> p g c h", p=P)

        FIRST = 2
        TURNS = (NB - 2 - FIRST) // 2

        def schedule(eng, iteration, steps=None, per_turn=0):
            for i in range(FIRST):
                iteration(i, i % 2 == 1, (i - 1) // 2)
            with eng.Fori(0, TURNS) as turn:
                if steps:
                    steps.enter_loop(turn, per_turn)
                for half in range(2):
                    iteration(2 * turn + (FIRST + half), half == 1, turn + half)
            if steps:
                steps.leave_loop(TURNS)
            for i in range(NB - 2, NB):
                iteration(i, i % 2 == 1, (i - 1) // 2)

        def stages(i):
            if isinstance(i, int):
                return i + 2 < NB, i + 1 < NB, i >= 1, i >= 2
            return True, True, True, True

        block = ctx.enter_context(nc.Block())

        @block.sync
        def _(sp):
            sp.dma_start(xin[:], x_dram[:, 0]).then_inc(xin_loaded, 16)
            sp.dma_start(ident[:], ident_in).then_inc(c_loaded, 16)
            sp.dma_start(wqk_raw[:, 0:HD], w_q).then_inc(wq_loaded, 16)
            sp.dma_start(gam[:], gamma).then_inc(c_loaded, 16)
            sp.dma_start(dist, dist_in).then_inc(a_loaded, 16)
            sp.dma_start(wqk_raw[:, HD:2 * HD], w_kv[:, 0:HD]).then_inc(wk_loaded, 16)
            sp.dma_start(nkrow[:, 0:DH], nk).then_inc(n_loaded, 16)
            sp.dma_start(nksc[:, 0:DH], q_scale.rearrange("d a -> a d").broadcast_to([NN, DH])).then_inc(n_loaded, 16)
            sp.dma_start(nksc[:, DH:2 * DH], k_scale.rearrange("d a -> a d").broadcast_to([NN, DH])).then_inc(n_loaded, 16)
            sp.dma_start(wvT_s, wvT).then_inc(vo_loaded, 16)
            sp.dma_start(wout_s, wout).then_inc(vo_loaded, 16)
            sp.dma_start(wqT_s, wqT).then_inc(h_loaded, 16)
            sp.dma_start(nvT_s, nvT).then_inc(h_loaded, 16)
            for half in range(2):
                sp.dma_start(qks2[half * DH:(half + 1) * DH, 0:1], q_scale).then_inc(s_loaded, 16)
                sp.dma_start(qks2[half * DH:(half + 1) * DH, 1:2], k_scale).then_inc(s_loaded, 16)
            sp.dma_start(nullbias[:], nullbias_in).then_inc(b_loaded, 16)
            sp.dma_start(xres[:], x_dram[:, 0]).then_inc(xres_loaded, 16)
            sp.dma_start(ctxT_s, ctxT).then_inc(g_loaded, 16)
            sp.dma_start(hmask[:], hmask_in).then_inc(g_loaded, 16)
            for k, (w, b) in enumerate(((xwq, xbq), (xwk, xbk))):
                sp.dma_start(xw[:, 2 * k:2 * k + 2, :], w).then_inc(g_loaded, 16)
                sp.dma_start(xb[:, 2 * k:2 * k + 2], b).then_inc(g_loaded, 16)
            sp.dma_start(xw[:, 4, :], xwv).then_inc(g_loaded, 16)
            sp.dma_start(xb[:, 4:5], xbv).then_inc(g_loaded, 16)
            sp.dma_start(hmask2[:], hmask2_in).then_inc(g_loaded, 16)
            sp.dma_start(xwo[:], xwoT).then_inc(g_loaded, 16)
            sp.dma_start(bo[:], xbo.broadcast_to([P, P])).then_inc(g_loaded, 16)

            def ffn_load(g):
                sp.dma_start(w1s[:], w1_dram[:, g]).then_inc(ffn_loaded, 16)
                sp.dma_start(w2s[:], w2_dram[:, g]).then_inc(ffn_loaded, 16)
                sp.dma_start(b2s[:], b2[g]).then_inc(ffn_loaded, 16)

            ffn_load(0)

            def iteration(i, w, g):
                d, a, c, e = stages(i)
                if d:
                    sp.wait_ge(xn_ready, i + 2)
                    sp.dma_start(xin[:], x_dram[:, i + 2]).then_inc(xin_loaded, 16)
                if e:
                    sp.wait_ge(x3_ready, i - 1)
                    sp.dma_start(out_dram[:, i - 2], x3[:]).then_inc(stored, 16)
                if w and not (isinstance(g, int) and g + 1 >= GROUPS):
                    sp.wait_ge(w12raw_ready, g + 1)
                    sp.wait_ge(w12raw_copied, 2 * g + 2)
                    ffn_load(g + 1)
                if a:
                    sp.wait_ge(y_added, NT * (i + 1))
                    sp.dma_start(xres[:], x_dram[:, i + 1]).then_inc(xres_loaded, 16)

            sp.wait_ge(xn_ready, 1)
            sp.dma_start(xin[:], x_dram[:, 1]).then_inc(xin_loaded, 16)
            schedule(sp, iteration)
            sp.wait_ge(x3_ready, NB - 1)
            sp.dma_start(out_dram[:, NB - 2], x3[:]).then_inc(stored, 16)
            sp.wait_ge(x3_ready, NB)
            sp.dma_start(out_dram[:, NB - 1], x3[:]).then_inc(stored, 16)
            sp.wait_ge(stored, 16 * NB)

        @block.tensor
        def _(pe):
            read = {}

            def take(bank, read_by, value):
                if bank in read:
                    need(pe, *read[bank])
                read[bank] = (read_by, value)

            def split_product(dst, hi, lo, whi, wlo):
                pe.matmul(dst, hi, whi, start=True, stop=False)
                pe.matmul(dst, hi, wlo, start=False, stop=False)
                return pe.matmul(dst, lo, whi, start=False, stop=True)

            def turn_null_keys():
                pe.wait_ge(nkrow_ready, 1)
                take('T0', nkT_copied, 1)
                pe.transpose(psT[0][:, 0:NN], nkrow, ident[0:NN, 0:NN]).then_inc(nkT_ready, 1)

            def merged_nulls():
                pe.wait_ge(h_loaded, 16 * 2)
                take('T0', wn_split, 1)
                take('T1', wn_split, 1)
                for h in list(range(0, H, 2)) + list(range(1, H, 2)):
                    r = slice(DH * (h % 2), DH * (h % 2) + DH)
                    mm = pe.matmul(psT[h % 2][:, NULLS * (h // 2):NULLS * (h // 2 + 1)], wqT_s[r, h // 2, :],
                                   nkT[r, NULLS * h:NULLS * (h + 1)], start=True, stop=True)
                mm.then_inc(wn_ready, 1)

            def merged_values(c):
                if c == 0:
                    pe.wait_ge(vo_loaded, 16 * 2)
                take(f'S{c % 2}', m_split, c + 1)
                for j, h in enumerate(score_heads(0, c)):
                    r = slice(DH * (h % 2), DH * (h % 2) + DH)
                    mm = pe.matmul(psS[c % 2][:, P * j:P * (j + 1)], wvT_s[r, h // 2, :],
                                   wout_s[r, h // 2, :], start=True, stop=True)
                mm.then_inc(m_ready, 1)

            def null_values():
                take('T0', nullv_copied, 1)
                for p in range(HP):
                    mm = pe.matmul(psT[0][0:NN, 0:P], nvT_s[:, p, :], wout_s[:, p, :],
                                   start=(p == 0), stop=(p == HP - 1))
                mm.then_inc(nullv_ready, 1)

            def context_kv():
                pe.wait_ge(g_loaded, 16 * 11)
                for k in range(6):
                    take(f'J{k % 2}', *((kx_split, k + 1) if k < 4 else (kvx_copied, k + 1)))
                    pe.matmul(psJ[k % 2][:], xw[:, 2 + k // 2, :], ctxT_s[:, 512 * (k % 2):512 * (k % 2) + 512],
                              start=True, stop=True).then_inc(kvx_ready, 1)

            def xn_turn(n):
                pe.wait_ge(xn_ready, n + 1)
                take('J0', xnT_split, n + 1)
                for t in range(NT):
                    mm = pe.transpose(psJ[0][:, P * t:P * (t + 1)], xn[:, t, :], ident[:])
                mm.then_inc(xnT_ready, 1)

            def project_qk(n, c):
                if c == 0:
                    pe.wait_ge(xnT_split, n + 1)
                if isinstance(n, int) and n == 0 and c < 4:
                    pe.wait_ge(wsplit_ready, c + 1)
                t, j = c // 4, c % 4
                if c in QK_ACT:
                    take(f'J{c % 2}', qk_copied_act, chunks_to(QK_ACT, n, c))
                else:
                    take(f'J{c % 2}', qk_copied_dve, chunks_to(QK_DVE, n, c))
                tok, col = slice(P * t, P * (t + 1)), slice(512 * j, 512 * (j + 1))
                split_product(psJ[c % 2][:], xnT_hi[:, tok], xnT_lo[:, tok],
                              wqk_hi[:, col], wqk_lo[:, col]).then_inc(qk_ready, 1)

            def project_nulls(n):
                if isinstance(n, int) and n == 0:
                    pe.wait_ge(wn_split, 1)
                take('J0', nullraw_copied, n + 1)
                for t in range(NT):
                    tok = slice(P * t, P * (t + 1))
                    mm = split_product(psJ[0][:, NN * t:NN * (t + 1)], xnT_hi[:, tok], xnT_lo[:, tok],
                                       wn_hi[:], wn_lo[:])
                mm.then_inc(nullraw_ready, 1)

            def project_v(n, c):
                t, j = c // 4, c % 4
                if isinstance(n, int) and n == 0 and c < 4:
                    pe.wait_ge(m_split, 2 * (c // 2) + 2)
                if c in V_ACT:
                    take(f'J{c % 2}', v_copied_act, chunks_to(V_ACT, n, c))
                else:
                    take(f'J{c % 2}', v_copied_dve, chunks_to(V_DVE, n, c))
                tok, col = slice(P * t, P * (t + 1)), slice(512 * j, 512 * (j + 1))
                split_product(psJ[c % 2][:], xnT_hi[:, tok], xnT_lo[:, tok],
                              m_hi[:, col], m_lo[:, col]).then_inc(v_ready, 1)

            def turn_qk(n, c):
                t, half, isk = c // 4, (c // 2) % 2, c % 2
                if half == 0:
                    pe.wait_ge(qk_normed, 2 * NT * n + 2 * t + isk + 1)
                take(f'S{isk}', kT_copied if isk else qT_copied, 2 * NT * n + c // 2 + 1)
                for j in range(4):
                    col = HD * isk + P * (4 * half + j)
                    mm = pe.transpose(psS[isk][:, P * j:P * (j + 1)], qk[t][:, col:col + P], ident[:])
                mm.then_inc(qkT_ready, 1)

            def scores(b, t, c):
                heads, keys = (4, P) if t == 0 else (2, SEQ)
                if t == 0 and c == 0:
                    pe.wait_ge(kT_copied, 2 * NT * b + 1)
                before = 4 * c if t == 0 else H + 2 * c
                k = c % 2
                take(f'S{k}', scores_masked, NT * H * b + before + heads)
                for j, h in enumerate(score_heads(t, c)):
                    r = slice(DH * (h % 2), DH * (h % 2) + DH)
                    mm = pe.matmul(psS[k][:, keys * j:keys * (j + 1)], qT[r, h // 2, P * t:P * (t + 1)],
                                   kT[r, h // 2, 0:keys], start=True, stop=True)
                mm.then_inc(scores_ready, 1)

            def evacuated(b, c):
                if c in PT_DVE:
                    pe.wait_ge(pT_copied_dve, chunks_to(PT_DVE, b, c))
                else:
                    pe.wait_ge(pT_copied_act, chunks_to(PT_ACT, b, c))

            def turn_probs(b, c):
                t, first = (0, 0) if c < TILE_PC[0] else (1, TILE_PC[0])
                pe.wait_ge(probs_normed, PC * b + c + 1)
                if c >= 2:
                    evacuated(b, c - 2)
                for j in range(4):
                    blk = 4 * (c - first) + j
                    h, kt = blk // (t + 1), blk % (t + 1)
                    mm = pe.transpose(psT[c % 2][:, P * j:P * (j + 1)], pr[t][:, h, P * kt:P * (kt + 1)], ident[:])
                mm.then_inc(probsT_ready, 1)

            def weigh_values(b, c):
                t, first = (0, 0) if c < TILE_PC[0] else (1, TILE_PC[0])
                if c == 0:
                    pe.wait_ge(v_copied_dve, len(V_DVE) * (b + 1))
                    pe.wait_ge(v_copied_act, len(V_ACT) * (b + 1))
                    need(pe, h2_added, b - 1)
                evacuated(b, c)
                for j in range(4):
                    blk = 4 * (c - first) + j
                    h, kt = blk // (t + 1), blk % (t + 1)
                    mm = pe.matmul(psY[t][:, 0:P], pT[c % 4][:, P * j:P * (j + 1)], val[:, kt, P * h:P * (h + 1)],
                                   start=(blk == 0), stop=False)
                mm.then_inc(pv_done, 1)

            def turn_nulls(b, t):
                pe.wait_ge(pnn_ready, NT * b + t + 1)
                take('J1', pnT_copied, NT * b + t + 1)
                pe.transpose(psJ[1][0:NN, 0:P], pnn[:, t, :], ident[:]).then_inc(nullT_ready, 1)

            def weigh_nulls(b, t):
                pe.wait_ge(pnT_copied, NT * b + t + 1)
                pe.matmul(psY[t][:, 0:P], pnT[:, t, :], null_v[:], start=False, stop=True).then_inc(y_ready, 1)

            def x1_turn(b):
                pe.wait_ge(x1_ready, b + 1)
                take('J1', x1T_copied, b + 1)
                for t in range(NT):
                    mm = pe.transpose(psJ[1][:, P * t:P * (t + 1)], x1[:, t, :], ident[:])
                mm.then_inc(x1T_ready, 1)

            def cross_q(b):
                pe.wait_ge(x1T_copied, b + 1)
                take('J1', xqT_split, b + 1)
                for half in range(2):
                    mm = pe.matmul(psJ[1][:, SEQ * half:SEQ * (half + 1)], xw[:, half, :], x1T[:], start=True, stop=True)
                mm.then_inc(xqT_ready, 1)

            def cross_scores(b, k):
                t, half = k // 2, k % 2
                if k == 0:
                    pe.wait_ge(xqT_split, b + 1)
                    pe.wait_ge(kexp_ready, b + 1)
                take(f'S{half}', xs_sub, XC * b + k + 1)
                tok = slice(P * t, P * (t + 1))
                pe.matmul(psS[half][:], xqT_hi[:, half, tok],
                          kexp[:, half, :, :].rearrange("p h k -> p (h k)"), start=True, stop=False)
                pe.matmul(psS[half][:], xqT_lo[:, half, tok],
                          kexp[0:DH, half, :, :].rearrange("p h k -> p (h k)"),
                          start=False, stop=True).then_inc(xscores_ready, 1)

            def cross_values(b, c):
                pe.wait_ge(vexp_ready, b + 1)
                take(f'J{c}', xv_copied, 2 * b + c + 1)
                for j in range(4):
                    p = 4 * c + j
                    mm = pe.matmul(psJ[c][:, P * j:P * (j + 1)],
                                   vexp[:, 2 * p:2 * p + 2, :].rearrange("p h k -> p (h k)"), xwo[:],
                                   start=True, stop=True)
                mm.then_inc(xv_ready, 1)

            def merge_ffn(g):
                pe.wait_ge(ffn_loaded, 48 * (g + 1))
                take('J0', w12raw_copied, 2 * g + 2)
                for c in range(OC):
                    mm = pe.matmul(psJ[0][:, 0:P + 1], w2s[:, c, :], w1s[:, c, :], start=(c == 0), stop=(c == OC - 1))
                mm.then_inc(w12raw_ready, 1)

            def turn_ffn(g):
                pe.wait_ge(w12raw_copied, 2 * g + 2)
                take('J1', w12_copied, g + 1)
                for k in range(2):
                    mm = pe.transpose(psJ[1][:, P * k:P * (k + 1)], w12raw[:, k, :], ident[:])
                mm.then_inc(w12_ready, 1)

            def turn_cross_probs(b, k):
                t, half = k // 2, k % 2
                pe.wait_ge(xprobs_normed, NT * b + t + 1)
                if k >= 2:
                    pe.wait_ge(xpT_copied, XC * b + k - 1)
                for j in range(4):
                    p = 4 * half + j
                    mm = pe.transpose(psT[half][:, P * j:P * (j + 1)],
                                      xp[t][:, 2 * p:2 * p + 2, :].rearrange("p h k -> p (h k)"), ident[:])
                mm.then_inc(xprobsT_ready, 1)

            def weigh_cross_values(b, k):
                t, half = k // 2, k % 2
                pe.wait_ge(xpT_copied, XC * b + k + 1)
                for j in range(4):
                    mm = pe.matmul(psY[0][:, P * t:P * (t + 1)], xpT[half][:, P * j:P * (j + 1)],
                                   xv[:, 4 * half + j, :], start=(half == 0 and j == 0),
                                   stop=(half == 1 and j == 3))
                mm.then_inc(xpv_done, 1)

            def x2_turn(b):
                pe.wait_ge(x2_ready, b + 1)
                take('J0', x2T_copied, b + 1)
                for t in range(NT):
                    mm = pe.transpose(psJ[0][:, P * t:P * (t + 1)], x2[:, t, :], ident[:])
                mm.then_inc(x2T_ready, 1)

            def feed_forward(b, g):
                pe.wait_ge(x2T_copied, b + 1)
                pe.wait_ge(w12_copied, g + 1)
                pe.wait_ge(y2_added, b + 1)
                for t in range(NT):
                    mm = pe.matmul(psY[0][:, P * t:P * (t + 1)], x2T[:, P * t:P * (t + 1)], w12[:, 0, :],
                                   start=True, stop=True)
                mm.then_inc(h2_ready, 1)

            pe.wait_ge(c_loaded, 16 * 2)
            xn_turn(0)
            for c in range(4):
                project_qk(0, c)
            for c in range(4, QK_CHUNKS):
                project_qk(0, c)
            turn_null_keys()
            merged_values(0)
            merged_values(1)
            merged_nulls()
            merged_values(2)
            merged_values(3)
            null_values()
            project_nulls(0)
            project_v(0, 0)
            project_v(0, 1)
            for k in range(4):
                turn_qk(0, 2 * k)
                turn_qk(0, 2 * k + 1)
                project_v(0, 2 + k)

            def iteration(i, w, g):
                d, a, c, e = stages(i)
                read['J0'] = (x2T_copied, i - 1) if e else (v_copied_act, chunks_to(V_ACT, i, 4))
                read['J1'] = (v_copied_act, chunks_to(V_ACT, i, 5))
                read['S0'], read['S1'] = (qT_copied, 2 * NT * (i + 1)), (kT_copied, 2 * NT * (i + 1))
                scores(i, 0, 0)
                project_v(i, 6)
                scores(i, 0, 1)
                project_v(i, 7)
                if a:
                    xn_turn(i + 1)
                scores(i, 0, 2)
                scores(i, 0, 3)
                if a:
                    project_qk(i + 1, 0)
                for k in range(3):
                    scores(i, 1, k)
                    if a:
                        project_qk(i + 1, k + 1)
                scores(i, 1, 3)
                turn_probs(i, 0)
                scores(i, 1, 4)
                turn_probs(i, 1)
                turn_nulls(i, 0)
                for k in range(4):
                    weigh_values(i, k)
                    if k < 3:
                        scores(i, 1, 5 + k)
                    if k < 2:
                        turn_probs(i, k + 2)
                weigh_nulls(i, 0)
                if c:
                    cross_scores(i - 1, 0)
                if a:
                    project_qk(i + 1, 4)
                if c:
                    cross_scores(i - 1, 1)
                if a:
                    project_qk(i + 1, 5)
                    project_qk(i + 1, 6)
                if c:
                    cross_scores(i - 1, 2)
                if a:
                    project_qk(i + 1, 7)
                if c:
                    cross_values(i - 1, 0)
                    cross_scores(i - 1, 3)
                else:
                    context_kv()
                turn_probs(i, 4)
                if c:
                    cross_values(i - 1, 1)
                turn_probs(i, 5)
                for k in range(4, PC):
                    weigh_values(i, k)
                    if k + 2 < PC:
                        turn_probs(i, k + 2)
                    if a and k == 5:
                        project_nulls(i + 1)
                    if w and k == 6:
                        merge_ffn(g)
                    if w and k == 8:
                        turn_ffn(g)
                    if k == 9:
                        turn_nulls(i, 1)
                weigh_nulls(i, 1)
                if c:
                    pe.wait_ge(y_added, NT * i + 1)
                    turn_cross_probs(i - 1, 0)
                    turn_cross_probs(i - 1, 1)
                for k in range(4):
                    if a and k < 3:
                        project_v(i + 1, k)
                    if k == 2:
                        cross_q(i)
                    if c:
                        weigh_cross_values(i - 1, k)
                        if k < 2:
                            turn_cross_probs(i - 1, k + 2)
                    if k == 1:
                        x1_turn(i)
                for k in range(4):
                    if a:
                        turn_qk(i + 1, 2 * k)
                        turn_qk(i + 1, 2 * k + 1)
                    if a and k < 3:
                        project_v(i + 1, 3 + k)
                    if a and c and k == 2:
                        x2_turn(i - 1)
                    if a and c and k == 3:
                        feed_forward(i - 1, g)

            schedule(pe, iteration)
            b = NB - 1
            for k in range(XC):
                cross_scores(b, k)
            cross_values(b, 0)
            x2_turn(b - 1)
            cross_values(b, 1)
            feed_forward(b - 1, GROUPS - 1)
            turn_cross_probs(b, 0)
            turn_cross_probs(b, 1)
            pe.wait_ge(h2_added, b)
            for k in range(4):
                weigh_cross_values(b, k)
                if k < 2:
                    turn_cross_probs(b, k + 2)
            x2_turn(b)
            feed_forward(b, GROUPS - 1)

        @block.vector
        def _(dve):
            steps = Steps(dve_step)

            def wait_apart(semaphore, value):
                if not isinstance(value, int):
                    value = dve.to_reg(value)
                dve.wait_ge(xin_loaded, 16)
                dve.wait_ge(semaphore, value)

            def ln_begin(name, src, tiles, count):
                for t in tiles:
                    steps.mark(dve.bn_stats(st[name][:, t, :], src[:, t, :]))
                wait_apart(dve_step, steps.value())
                for t in tiles:
                    steps.mark(dve.bn_aggr(mv[name][:, t, :], st[name][:, t, :]))
                steps.wait(dve)
                a, z = tiles[0], tiles[-1] + 1
                dve.tensor_scalar(ve[name][:, a:z], mv[name][:, a:z, 1], EPS, None, ALU.add).then_inc(var_ready[name], 1)

            def newton(y0, v, tmp, res, half):
                steps.mark(dve.tensor_tensor(tmp, y0, y0, ALU.mult))
                steps.wait(dve)
                steps.mark(dve.scalar_tensor_tensor(out=tmp, in0=tmp, scalar=-half, in1=v, op0=ALU.mult, op1=ALU.mult))
                steps.wait(dve)
                return dve.scalar_tensor_tensor(out=res, in0=tmp, scalar=1.5, in1=y0, op0=ALU.add, op1=ALU.mult)

            def ln_end(name, src, dst, tiles, count):
                dve.wait_ge(seed_ready[name], count)
                a, z = tiles[0], tiles[-1] + 1
                steps.mark(newton(sd[name][:, a:z], ve[name][:, a:z], nw[name][:, a:z], rs[name][:, a:z], 0.5))
                steps.wait(dve)
                for t in tiles:
                    last = dve.tensor_scalar(dst[:, t, :], src[:, t, :], mv[name][:, t, 0:1], rs[name][:, t:t + 1],
                                             ALU.subtract, ALU.mult)
                    if t != tiles[-1]:
                        steps.mark(last)
                return last

            def scale_rows():
                dve.wait_ge(s_loaded, 16 * 4)
                dve.scalar_tensor_tensor(out=kscale[:], in0=qks2[:, 0:1], scalar=-ATTN_SCALE * SEED_SCALE,
                                         in1=qks2[:, 1:2], op0=ALU.mult, op1=ALU.mult).then_inc(kscale_ready, 1)

            def split_wqk(c):
                dve.wait_ge(wq_loaded if c < 2 else wk_loaded, 16)
                col = slice(512 * c, 512 * (c + 1))
                steps.mark(dve.tensor_copy(wqk_hi[:, col], wqk_raw[:, col]))
                steps.wait(dve)
                dve.tensor_tensor(wqk_lo[:, col], wqk_raw[:, col], wqk_hi[:, col].bitcast(F32),
                                  ALU.subtract).then_inc(wsplit_ready, 1)

            def null_squares():
                dve.wait_ge(n_loaded, 16 * 3)
                steps.mark(dve.tensor_tensor(nksq, nkrow[:, 0:DH], nkrow[:, 0:DH], ALU.mult))
                steps.mark(dve.scalar_tensor_tensor(out=nksc[:, 0:DH], in0=nksc[:, 0:DH],
                                                    scalar=-ATTN_SCALE * SEED_SCALE, in1=nksc[:, DH:2 * DH],
                                                    op0=ALU.mult, op1=ALU.mult))
                steps.wait(dve)
                steps.mark(dve.tensor_reduce(nkst[:, 0:1], nksq, AX.X, ALU.add))
                steps.wait(dve)
                dve.tensor_scalar(nkst[:, 1:2], nkst[:, 0:1], 1e-24, None, ALU.max).then_inc(nkssq_ready, 1)

            def norm_null_keys():
                dve.wait_ge(nkseed_ready, 1)
                steps.mark(newton(nkst[:, 3:4], nkst[:, 1:2], nkst[:, 4:5], nkst[:, 5:6], 0.5 * SEED_SCALE))
                steps.wait(dve)
                steps.mark(dve.scalar_tensor_tensor(out=nkrow[:, 0:DH], in0=nkrow[:, 0:DH], scalar=nkst[:, 5:6],
                                                    in1=nksc[:, 0:DH], op0=ALU.mult, op1=ALU.mult))
                steps.wait(dve)
                dve.tensor_copy(nkrow[:, DH:2 * DH], nkrow[:, 0:DH]).then_inc(nkrow_ready, 1)

            def split_wn():
                dve.wait_ge(wn_ready, 1)
                hi, lo = (w[:].rearrange("p (c r n) -> p c r n", r=2, n=NULLS) for w in (wn_hi, wn_lo))
                ps = [psT[r][:, 0:NN // 2].rearrange("p (c n) -> p c n", n=NULLS) for r in range(2)]
                for r in range(2):
                    steps.mark(dve.tensor_copy(hi[:, :, r, :], ps[r]))
                steps.wait(dve)
                for r in range(2):
                    last = dve.tensor_tensor(lo[:, :, r, :], ps[r], hi[:, :, r, :].bitcast(F32), ALU.subtract)
                    if r == 0:
                        steps.mark(last)
                last.then_inc(wn_split, 1)

            def split_m(c):
                dve.wait_ge(m_ready, c + 1)
                hi, lo = (m[:].rearrange("p (c r d) -> p c r d", r=2, d=P)[:, 4 * (c // 2):4 * (c // 2) + 4, c % 2, :]
                          for m in (m_hi, m_lo))
                ps = psS[c % 2][:].rearrange("p (c d) -> p c d", d=P)
                steps.mark(dve.tensor_copy(hi, ps))
                steps.wait(dve)
                dve.tensor_tensor(lo, ps, hi.bitcast(F32), ALU.subtract).then_inc(m_split, 1)

            def copy_null_v():
                dve.wait_ge(nullv_ready, 1)
                dve.tensor_copy(null_v[:], psT[0][0:NN, 0:P]).then_inc(nullv_copied, 1)

            def ln1_begin(n):
                dve.wait_ge(xin_loaded, 16 * (n + 1))
                ln_begin("ln1", xin, (0, 1), n + 1)

            def ln1_end(n):
                ln_end("ln1", xin, xn, (0, 1), n + 1).then_inc(xn_ready, 1)

            def split_xnT(n):
                dve.wait_ge(xnT_ready, n + 1)
                steps.mark(dve.tensor_scalar(xnT_hi[:], psJ[0][:, 0:SEQ], gam[:], None, ALU.mult))
                steps.wait(dve)
                dve.scalar_tensor_tensor(out=xnT_lo[:], in0=psJ[0][:, 0:SEQ], scalar=gam[:],
                                         in1=xnT_hi[:].bitcast(F32), op0=ALU.mult,
                                         op1=ALU.subtract).then_inc(xnT_split, 1)

            def sum_squares(n, t, half):
                dve.wait_ge(qk_squared, 2 * (NT * n + t) + half + 1)
                steps.mark(dve.tensor_reduce(ssq[:, t, H * half:H * (half + 1)],
                                             sq[:, HD * half:HD * (half + 1)].rearrange("p (h d) -> p h d", d=DH),
                                             AX.X, ALU.add))

            def floor_squares(t):
                steps.wait(dve)
                dve.tensor_scalar(ssq[:, t, :], ssq[:, t, :], 1e-24, None, ALU.max).then_inc(ssq_ready, 1)

            def norms(n, t):
                dve.wait_ge(qkseed_ready, NT * n + t + 1)
                newton(seedq[:, t, :], ssq[:, t, :], newt[:, t, :], rn[:, t, :], 0.5 * SEED_SCALE).then_inc(rn_ready, 1)

            def null_scores(n):
                dve.wait_ge(nullraw_copied, n + 1)
                dve.wait_ge(rn_ready, NT * (n + 1))
                steps.mark(dve.tensor_tensor(nullmul[:].rearrange("p t (h n) -> p t h n", n=NULLS),
                                             nullraw[:].rearrange("p t (h n) -> p t h n", n=NULLS),
                                             rn[:, :, 0:H].unsqueeze(3).broadcast_to([P, NT, H, NULLS]), ALU.mult))
                steps.wait(dve)
                steps.mark(dve.tensor_tensor(nullneg[:], nullmul[:], nullbias[:], ALU.add))
                steps.wait(dve)
                steps.mark(dve.tensor_reduce(nullmin[:], nullneg[:].rearrange("p t (h n) -> p t h n", n=NULLS),
                                             AX.X, ALU.min))
                steps.wait(dve)

            def copy_qk(n, c):
                t, j = c // 4, c % 4
                dve.wait_ge(qk_ready, QK_CHUNKS * n + c + 1)
                dve.tensor_copy(qk[t][:, 512 * j:512 * (j + 1)], psJ[c % 2][:]).then_inc(qk_copied_dve, 1)

            def copy_v(n, c):
                dve.wait_ge(v_ready, V_CHUNKS * n + c + 1)
                dve.tensor_copy(val[:, c // 4, 512 * (c % 4):512 * (c % 4) + 512], psJ[c % 2][:]).then_inc(v_copied_dve, 1)

            def copy_qT(n, k):
                t, half = k // 2, k % 2
                dve.wait_ge(qkT_ready, 4 * NT * n + 2 * k + 1)
                dve.tensor_copy(qT[:, 4 * half:4 * half + 4, P * t:P * (t + 1)],
                                psS[0][:].rearrange("p (c k) -> p c k", c=4)).then_inc(qT_copied, 1)

            def mask_scores(b, t, chunks):
                keys = P if t == 0 else SEQ
                for c in chunks:
                    wait_apart(scores_ready, PC * b + (0 if t == 0 else TILE_PC[0]) + c + 1)
                    for j, h in enumerate(score_heads(t, c)):
                        dve.tensor_tensor_reduce(pr[t][:, h, :], psS[c % 2][:, keys * j:keys * (j + 1)],
                                                 alibi[:, h, SEQ - keys:SEQ], 1.0, nullmin[:, t, h:h + 1],
                                                 ALU.add, ALU.min, nmin[:, t, h:h + 1]).then_inc(scores_masked, 1)

            def null_shift(b, t):
                dve.wait_ge(scores_masked, NT * H * b + H * (t + 1))
                dve.tensor_tensor(nulld[:, t, :].rearrange("p (h n) -> p h n", n=NULLS),
                                  nmin[:, t, :].unsqueeze(2).broadcast_to([P, H, NULLS]),
                                  nullneg[:, t, :].rearrange("p (h n) -> p h n", n=NULLS),
                                  ALU.subtract).then_inc(nulld_ready, 1)

            def denominators(b, t):
                dve.wait_ge(pn_ready, NT * b + t + 1)
                steps.mark(dve.tensor_reduce(den[:, t, :], dparts[:, t], AX.X, ALU.add))
                steps.wait(dve)
                dve.reciprocal(rden[:, t, :], den[:, t, :]).then_inc(rden_ready, 1)
                dve.wait_ge(rden_ready, NT * b + t + 1)
                dve.tensor_tensor(pnn[:, t, :].rearrange("p (h n) -> p h n", n=NULLS), dparts[:, t, :, 1:1 + NULLS],
                                  rden[:, t, :].unsqueeze(2).broadcast_to([P, H, NULLS]),
                                  ALU.mult).then_inc(pnn_ready, 1)

            def copy_pT(b, c):
                dve.wait_ge(probsT_ready, PC * b + c + 1)
                need(dve, pv_done, PC * b + c - 3)
                dve.tensor_copy(pT[c % 4][:], psT[c % 2][:]).then_inc(pT_copied_dve, 1)

            def add_y(b, t):
                dve.wait_ge(y_ready, NT * b + t + 1)
                if t == 0:
                    dve.wait_ge(xres_loaded, 16 * (b + 1))
                dve.tensor_tensor(r1[:, t, :], psY[t][:, 0:P], xres[:, t, :], ALU.add).then_inc(y_added, 1)

            def ln2_begin(b):
                dve.wait_ge(y_added, NT * (b + 1))
                ln_begin("ln2", r1, (0, 1), b + 1)

            def ln2_end(b):
                ln_end("ln2", r1, x1, (0, 1), b + 1).then_inc(x1_ready, 1)

            def split_context_k():
                for k in range(4):
                    dve.wait_ge(kvx_copied, k + 1)
                    low = kTx[DH:P, k // 2, 512 * (k % 2):512 * (k % 2) + 512]
                    dve.scalar_tensor_tensor(out=low, in0=psJ[k % 2][DH:P, :], scalar=xb[DH:P, 2 + k // 2:3 + k // 2],
                                             in1=low.bitcast(F32), op0=ALU.add, op1=ALU.subtract).then_inc(kx_split, 1)

            def split_xqT(b):
                dve.wait_ge(xqT_copied, 2 * (b + 1))
                for half in range(2):
                    last = dve.scalar_tensor_tensor(out=xqT_lo[:, half, :], in0=psJ[1][0:DH, SEQ * half:SEQ * (half + 1)],
                                                    scalar=xb[0:DH, half:half + 1],
                                                    in1=xqT_hi[0:DH, half, :].bitcast(F32), op0=ALU.add, op1=ALU.subtract)
                    if half == 0:
                        steps.mark(last)
                last.then_inc(xqT_split, 1)

            def cross_shift(b, k):
                t, half = k // 2, k % 2
                hs = slice(8 * half, 8 * half + 8)
                dve.wait_ge(xscores_ready, XC * b + k + 1)
                s = psS[half][:].rearrange("p (h k) -> p h k", h=8)
                steps.mark(dve.tensor_reduce(xmax[:, t, hs], s, AX.X, ALU.max))
                steps.wait(dve)
                dve.tensor_tensor(xp[t][:, hs, :], s, xmax[:, t, hs].unsqueeze(2).broadcast_to([P, 8, CTX]),
                                  ALU.subtract).then_inc(xs_sub, 1)

            def cross_denominators(b, t):
                dve.wait_ge(xexp_done, NT * b + t + 1)
                steps.mark(dve.tensor_reduce(xden[:, t, :], xp[t][:], AX.X, ALU.add))
                steps.wait(dve)
                dve.reciprocal(xrden[:, t, :], xden[:, t, :]).then_inc(xrden_ready, 1)

            def add_y2(b):
                dve.wait_ge(xpv_done, XC * (b + 1))
                dve.wait_ge(x1b_ready, b + 1)
                dve.tensor_tensor(r2[:], psY[0][:, 0:SEQ].rearrange("p (t d) -> p t d", t=NT), x1b[:],
                                  ALU.add).then_inc(y2_added, 1)

            def ln3_begin(b):
                dve.wait_ge(y2_added, b + 1)
                ln_begin("ln3", r2, (0, 1), b + 1)

            def ln3_end(b):
                ln_end("ln3", r2, x2, (0, 1), b + 1).then_inc(x2_ready, 1)

            def add_h2(b):
                dve.wait_ge(h2_ready, b + 1)
                dve.wait_ge(x2b_ready, b + 1)
                dve.tensor_tensor(r3[:], psY[0][:, 0:SEQ].rearrange("p (t d) -> p t d", t=NT), x2b[:],
                                  ALU.add).then_inc(h2_added, 1)
                dve.wait_ge(h2_added, b + 1)
                ln_begin("ln4", r3, (0, 1), b + 1)

            def ln4_end(b):
                need(dve, stored, 16 * b)
                ln_end("ln4", r3, x3, (0, 1), b + 1).then_inc(x3_ready, 1)

            ln1_begin(0)
            ln1_end(0)
            split_wqk(0)
            split_xnT(0)
            split_wqk(1)
            copy_qk(0, 0)
            split_wqk(2)
            copy_qk(0, 1)
            split_wqk(3)
            null_squares()
            copy_qk(0, 3)
            norm_null_keys()
            sum_squares(0, 0, 0)
            split_m(0)
            sum_squares(0, 0, 1)
            floor_squares(0)
            split_m(1)
            norms(0, 0)
            sum_squares(0, 1, 0)
            split_wn()
            sum_squares(0, 1, 1)
            floor_squares(1)
            split_m(2)
            norms(0, 1)
            split_m(3)
            copy_null_v()
            scale_rows()
            copy_qT(0, 0)
            copy_v(0, 2)
            copy_qT(0, 1)
            dve.wait_ge(b_loaded, 16)
            null_scores(0)
            copy_qT(0, 2)
            copy_qT(0, 3)
            dve.wait_ge(alibi_ready, H)
            ln1_begin(1)
            ln1_end(1)

            def iteration(i, w, g):
                d, a, c, e = stages(i)
                need(dve, probsT_ready, PC * (i - 1) + TILE_PC[0])
                mask_scores(i, 0, (0, 1))
                if a:
                    split_xnT(i + 1)
                mask_scores(i, 0, (2, 3))
                if a:
                    copy_qk(i + 1, 0)
                null_shift(i, 0)
                need(dve, probsT_ready, PC * i)
                for k in range(8):
                    mask_scores(i, 1, (k,))
                    if k == 0 and a:
                        copy_qk(i + 1, 1)
                    if k == 1:
                        denominators(i, 0)
                    if k == 2 and a:
                        copy_qk(i + 1, 3)
                    if k == 3:
                        copy_pT(i, 0)
                    if k == 4 and e:
                        ln4_end(i - 2)
                    if k == 5:
                        copy_pT(i, 2)
                null_shift(i, 1)
                if c:
                    cross_shift(i - 1, 0)
                denominators(i, 1)
                if c:
                    cross_shift(i - 1, 1)
                if c:
                    cross_shift(i - 1, 2)
                add_y(i, 0)
                if c:
                    cross_shift(i - 1, 3)
                else:
                    split_context_k()
                if a:
                    sum_squares(i + 1, 0, 0)
                copy_pT(i, 6)
                if a:
                    sum_squares(i + 1, 0, 1)
                    floor_squares(0)
                if c:
                    cross_denominators(i - 1, 0)
                copy_pT(i, 8)
                if c:
                    cross_denominators(i - 1, 1)
                if a:
                    norms(i + 1, 0)
                copy_pT(i, 10)
                if a:
                    sum_squares(i + 1, 1, 0)
                    sum_squares(i + 1, 1, 1)
                    floor_squares(1)
                add_y(i, 1)
                ln2_begin(i)
                if a:
                    norms(i + 1, 1)
                ln2_end(i)
                if d:
                    ln1_begin(i + 2)
                if a:
                    null_scores(i + 1)
                if a:
                    copy_v(i + 1, 2)
                split_xqT(i)
                if c:
                    add_y2(i - 1)
                if a:
                    copy_qT(i + 1, 0)
                if c:
                    ln3_begin(i - 1)
                if a:
                    copy_qT(i + 1, 1)
                if a and c:
                    ln3_end(i - 1)
                if a:
                    copy_qT(i + 1, 2)
                if d:
                    ln1_end(i + 2)
                if a:
                    copy_qT(i + 1, 3)
                if a and c:
                    add_h2(i - 1)

            schedule(dve, iteration, steps, DVE_STEPS_A_TURN)
            b = NB - 1
            cross_shift(b, 0)
            cross_shift(b, 1)
            ln3_end(b - 1)
            cross_shift(b, 2)
            cross_denominators(b, 0)
            cross_shift(b, 3)
            add_h2(b - 1)
            cross_denominators(b, 1)
            ln4_end(b - 1)
            dve.wait_ge(x3_ready, b)
            add_y2(b)
            ln3_begin(b)
            ln3_end(b)
            add_h2(b)
            ln4_end(b)

        @block.scalar
        def _(act):
            steps = Steps(act_step)
            act.preload_act_table_set("natural_log_exp_and_others")

            def rsqrt_seed(v, tmp, res, scale):
                steps.mark(act.activation(tmp, v, ACT.Ln, scale=scale))
                steps.wait(act)
                return act.activation(res, tmp, ACT.Exp, scale=-0.5)

            def ln_seed(name, tiles, count):
                act.wait_ge(var_ready[name], count)
                a, z = tiles[0], tiles[-1] + 1
                rsqrt_seed(ve[name][:, a:z], lv[name][:, a:z], sd[name][:, a:z], 1.0).then_inc(seed_ready[name], 1)

            def null_keys_seed():
                act.wait_ge(nkssq_ready, 1)
                rsqrt_seed(nkst[:, 1:2], nkst[:, 2:3], nkst[:, 3:4], SEED_SCALE).then_inc(nkseed_ready, 1)

            def make_alibi(heads):
                act.wait_ge(a_loaded, 16)
                for h in heads:
                    act.activation(alibi[:, h, :], dist, ACT.Copy, scale=float(slopes()[h])).then_inc(alibi_ready, 1)

            def copy_nkT():
                act.wait_ge(nkT_ready, 1)
                act.activation(nkT[:], psT[0][:, 0:NN], ACT.Copy).then_inc(nkT_copied, 1)

            def context_kv():
                act.wait_ge(g_loaded, 16 * 11)
                for k in range(6):
                    act.wait_ge(kvx_ready, k + 1)
                    col = slice(512 * (k % 2), 512 * (k % 2) + 512)
                    dst = kTx[:, k // 2, col] if k < 4 else vTx[:, col]
                    act.activation(dst, psJ[k % 2][:], ACT.Identity,
                                   bias=xb[:, 2 + k // 2:3 + k // 2]).then_inc(kvx_copied, 1)

            def copy_qk(n, c):
                t, j = c // 4, c % 4
                act.wait_ge(qk_ready, QK_CHUNKS * n + c + 1)
                act.activation(qk[t][:, 512 * j:512 * (j + 1)], psJ[c % 2][:], ACT.Copy).then_inc(qk_copied_act, 1)

            def square_qk(n, t, half):
                act.wait_ge(qk_copied_act, chunks_to(QK_ACT, n, 4 * t + 2 * half + 1))
                act.wait_ge(qk_copied_dve, chunks_to(QK_DVE, n, 4 * t + 2 * half + 1))
                if half == 0:
                    need(act, ssq_ready, NT * n + t)
                col = slice(HD * half, HD * (half + 1))
                act.activation(sq[:, col], qk[t][:, col], ACT.Square).then_inc(qk_squared, 1)

            def qk_seed(n, t):
                act.wait_ge(ssq_ready, NT * n + t + 1)
                rsqrt_seed(ssq[:, t, :], lnq[:, t, :], seedq[:, t, :], SEED_SCALE).then_inc(qkseed_ready, 1)

            def copy_nullraw(n):
                act.wait_ge(nullraw_ready, n + 1)
                act.activation(nullraw[:].rearrange("p t n -> p (t n)"), psJ[0][:, 0:NT * NN],
                               ACT.Copy).then_inc(nullraw_copied, 1)

            def copy_v(n, c):
                act.wait_ge(v_ready, V_CHUNKS * n + c + 1)
                act.activation(val[:, c // 4, 512 * (c % 4):512 * (c % 4) + 512], psJ[c % 2][:],
                               ACT.Copy).then_inc(v_copied_act, 1)

            def copy_kT(n, k):
                t, half = k // 2, k % 2
                act.wait_ge(qkT_ready, 4 * NT * n + 2 * k + 2)
                act.activation(kT[:, 4 * half:4 * half + 4, P * t:P * (t + 1)],
                               psS[1][:].rearrange("p (c k) -> p c k", c=4), ACT.Copy,
                               scale=kscale[:]).then_inc(kT_copied, 1)

            def exponentials(b, t, chunks):
                for c in chunks:
                    for j, h in enumerate(score_heads(t, c)):
                        act.wait_ge(scores_masked, NT * H * b + H * t + len(score_heads(t, c)) * c + j + 1)
                        act.activation(pr[t][:, h, :], pr[t][:, h, :], ACT.Exp, bias=nmin[:, t, h:h + 1], scale=-1.0,
                                       accum_out=dparts[:, t, h, 0:1]).then_inc(exp_done, 1)

            def null_exponentials(b, t):
                act.wait_ge(nulld_ready, NT * b + t + 1)
                act.activation(dparts[:, t, :, 1:1 + NULLS], nulld[:, t, :].rearrange("p (h n) -> p h n", n=NULLS),
                               ACT.Exp).then_inc(pn_ready, 1)

            def copy_pnT(b, t):
                act.wait_ge(nullT_ready, NT * b + t + 1)
                act.activation(pnT[:, t, :], psJ[1][0:NN, 0:P], ACT.Copy).then_inc(pnT_copied, 1)

            def copy_pT(b, c):
                act.wait_ge(probsT_ready, PC * b + c + 1)
                need(act, pv_done, PC * b + c - 3)
                act.activation(pT[c % 4][:], psT[c % 2][:], ACT.Copy).then_inc(pT_copied_act, 1)

            def copy_x1T(b):
                act.wait_ge(x1T_ready, b + 1)
                act.activation(x1T[:], psJ[1][:, 0:SEQ], ACT.Copy).then_inc(x1T_copied, 1)

            def copy_xqT(b):
                act.wait_ge(xqT_ready, b + 1)
                for half in range(2):
                    act.activation(xqT_hi[:, half, :], psJ[1][:, SEQ * half:SEQ * (half + 1)], ACT.Identity,
                                   bias=xb[:, half:half + 1]).then_inc(xqT_copied, 1)

            def cross_exponentials(b, t):
                act.wait_ge(xs_sub, XC * b + 2 * (t + 1))
                act.activation(xp[t][:], xp[t][:], ACT.Exp, scale=float(XD) ** -0.5).then_inc(xexp_done, 1)

            def copy_xv(b, c):
                act.wait_ge(xv_ready, 2 * b + c + 1)
                act.activation(xv[:, 4 * c:4 * c + 4, :].rearrange("p c d -> p (c d)"), psJ[c][:],
                               ACT.Copy).then_inc(xv_copied, 1)

            def copy_w12raw(g):
                act.wait_ge(w12raw_ready, g + 1)
                act.activation(w12raw[:, 0, :], psJ[0][:, 0:P], ACT.Copy).then_inc(w12raw_copied, 1)
                act.activation(w12raw[:, 1, :], psJ[0][:, P:P + 1].broadcast_to([P, P]), ACT.Identity,
                               bias=b2s[:]).then_inc(w12raw_copied, 1)

            def copy_w12(g):
                act.wait_ge(w12_ready, g + 1)
                act.activation(w12[:].rearrange("p a d -> p (a d)"), psJ[1][:, 0:2 * P], ACT.Copy).then_inc(w12_copied, 1)

            def copy_xpT(b, k):
                act.wait_ge(xprobsT_ready, XC * b + k + 1)
                need(act, xpv_done, XC * b + k - 1)
                act.activation(xpT[k % 2][:], psT[k % 2][:], ACT.Copy).then_inc(xpT_copied, 1)

            def copy_x2T(b):
                act.wait_ge(x2T_ready, b + 1)
                act.activation(x2T[:], psJ[0][:, 0:SEQ], ACT.Copy).then_inc(x2T_copied, 1)

            ln_seed("ln1", (0, 1), 1)
            make_alibi(range(8))
            copy_qk(0, 2)
            null_keys_seed()
            copy_qk(0, 4)
            copy_qk(0, 5)
            square_qk(0, 0, 0)
            copy_qk(0, 6)
            square_qk(0, 0, 1)
            copy_qk(0, 7)
            copy_nkT()
            qk_seed(0, 0)
            square_qk(0, 1, 0)
            square_qk(0, 1, 1)
            qk_seed(0, 1)
            copy_nullraw(0)
            make_alibi(range(8, H))
            copy_v(0, 0)
            copy_v(0, 1)
            act.wait_ge(kscale_ready, 1)
            for k in range(2 * NT):
                copy_kT(0, k)
                if k > 0:
                    copy_v(0, 2 + k)
            ln_seed("ln1", (0, 1), 2)

            def iteration(i, w, g):
                d, a, c, e = stages(i)
                copy_v(i, 6)
                exponentials(i, 0, (0,))
                copy_v(i, 7)
                exponentials(i, 0, (1,))
                exponentials(i, 0, (2,))
                exponentials(i, 0, (3,))
                null_exponentials(i, 0)
                exponentials(i, 1, (0,))
                exponentials(i, 1, (1,))
                if a:
                    copy_qk(i + 1, 2)
                exponentials(i, 1, (2, 3))
                copy_pnT(i, 0)
                copy_pT(i, 1)
                exponentials(i, 1, (4, 5))
                copy_pT(i, 3)
                exponentials(i, 1, (6, 7))
                null_exponentials(i, 1)
                if a:
                    copy_qk(i + 1, 4)
                    copy_qk(i + 1, 5)
                    copy_qk(i + 1, 6)
                if c:
                    cross_exponentials(i - 1, 0)
                if a:
                    copy_qk(i + 1, 7)
                    square_qk(i + 1, 0, 0)
                if not c:
                    context_kv()
                copy_pT(i, 4)
                if c:
                    cross_exponentials(i - 1, 1)
                copy_pT(i, 5)
                if a:
                    square_qk(i + 1, 0, 1)
                if c:
                    copy_xv(i - 1, 0)
                    copy_xv(i - 1, 1)
                copy_pT(i, 7)
                if a:
                    copy_nullraw(i + 1)
                if w:
                    copy_w12raw(g)
                if a:
                    square_qk(i + 1, 1, 0)
                    square_qk(i + 1, 1, 1)
                if a:
                    qk_seed(i + 1, 0)
                copy_pT(i, 9)
                if w:
                    copy_w12(g)
                copy_pnT(i, 1)
                copy_pT(i, 11)
                if c:
                    copy_xpT(i - 1, 0)
                if a:
                    qk_seed(i + 1, 1)
                if c:
                    copy_xpT(i - 1, 1)
                ln_seed("ln2", (0, 1), i + 1)
                if a:
                    copy_v(i + 1, 0)
                if c:
                    copy_xpT(i - 1, 2)
                if a:
                    copy_v(i + 1, 1)
                if c:
                    copy_xpT(i - 1, 3)
                copy_x1T(i)
                copy_xqT(i)
                if d:
                    ln_seed("ln1", (0, 1), i + 3)
                if a:
                    copy_kT(i + 1, 0)
                    copy_v(i + 1, 3)
                if c:
                    ln_seed("ln3", (0, 1), i)
                if a:
                    copy_kT(i + 1, 1)
                    copy_v(i + 1, 4)
                    copy_kT(i + 1, 2)
                    copy_v(i + 1, 5)
                if a and c:
                    copy_x2T(i - 1)
                if a:
                    copy_kT(i + 1, 3)
                if a and c:
                    ln_seed("ln4", (0, 1), i)

            schedule(act, iteration, steps, ACT_STEPS_A_TURN)
            b = NB - 1
            cross_exponentials(b, 0)
            copy_xv(b, 0)
            copy_x2T(b - 1)
            copy_xv(b, 1)
            cross_exponentials(b, 1)
            ln_seed("ln4", (0, 1), b)
            for k in range(XC):
                copy_xpT(b, k)
            ln_seed("ln3", (0, 1), NB)
            copy_x2T(b)
            ln_seed("ln4", (0, 1), NB)

        @block.gpsimd
        def _(pool):
            def norm_qk(n, t):
                pool.wait_ge(rn_ready, NT * n + t + 1)
                for k in range(2):
                    v = qk[t][:, HD * k:HD * (k + 1)].rearrange("p (h d) -> p h d", d=DH)
                    pool.tensor_tensor(v, v, rn[:, t, H * k:H * (k + 1)].unsqueeze(2).broadcast_to([P, H, DH]),
                                       ALU.mult).then_inc(qk_normed, 1)

            def norm_probs(b, t):
                pool.wait_ge(exp_done, NT * H * b + H * (t + 1))
                pool.wait_ge(rden_ready, NT * b + t + 1)
                heads = 4 if t == 0 else 2
                for c in range(TILE_PC[t]):
                    hs = slice(heads * c, heads * (c + 1))
                    pool.tensor_tensor(pr[t][:, hs, :], pr[t][:, hs, :],
                                       rden[:, t, hs].unsqueeze(2).broadcast_to([P, heads, P * (t + 1)]),
                                       ALU.mult).then_inc(probs_normed, 1)

            def norm_cross(b):
                for t in range(NT):
                    pool.wait_ge(xrden_ready, NT * b + t + 1)
                    pool.tensor_tensor(xp[t][:], xp[t][:], xrden[:, t, :].unsqueeze(2).broadcast_to([P, XH, CTX]),
                                       ALU.mult).then_inc(xprobs_normed, 1)

            def spread_context(b):
                mask = hmask[:].unsqueeze(2).broadcast_to([P, XH, CTX])
                if isinstance(b, int):
                    col = slice(CTX * b, CTX * (b + 1))
                else:
                    col = bass.ds(CTX * b, CTX)
                if isinstance(b, int) and b == 0:
                    pool.wait_ge(kx_split, 4)
                    pool.wait_ge(kvx_copied, 6)
                need(pool, xscores_ready, XC * b)
                pool.tensor_tensor(kexp[:], hmask2[:].unsqueeze(1).unsqueeze(3).broadcast_to([P, 2, XHALF, CTX]),
                                   kTx[:, :, col].bitcast(F32).unsqueeze(2).broadcast_to([P, 2, XHALF, CTX]),
                                   ALU.mult).then_inc(kexp_ready, 1)
                need(pool, xv_ready, 2 * b)
                pool.tensor_tensor(vexp[:], mask, vTx[:, col].unsqueeze(1).broadcast_to([P, XH, CTX]),
                                   ALU.mult).then_inc(vexp_ready, 1)

            def x1_plus_bias(b):
                pool.wait_ge(x1_ready, b + 1)
                need(pool, y2_added, b)
                pool.tensor_tensor(x1b[:], x1[:], bo[:].unsqueeze(1).broadcast_to([P, NT, P]),
                                   ALU.add).then_inc(x1b_ready, 1)

            def x2_plus_bias(b, g):
                pool.wait_ge(x2_ready, b + 1)
                pool.wait_ge(w12_copied, g + 1)
                need(pool, h2_added, b)
                pool.tensor_tensor(x2b[:], x2[:], w12[:, 1:2, :].broadcast_to([P, NT, P]),
                                   ALU.add).then_inc(x2b_ready, 1)

            norm_qk(0, 0)
            norm_qk(0, 1)

            def iteration(i, w, g):
                d, a, c, e = stages(i)
                norm_probs(i, 0)
                norm_probs(i, 1)
                if c:
                    norm_cross(i - 1)
                if a:
                    norm_qk(i + 1, 0)
                    norm_qk(i + 1, 1)
                spread_context(i)
                x1_plus_bias(i)
                if a and c:
                    x2_plus_bias(i - 1, g)

            schedule(pool, iteration)
            x2_plus_bias(NB - 2, GROUPS - 1)
            norm_cross(NB - 1)
            x2_plus_bias(NB - 1, GROUPS - 1)


DVE_STEPS_A_TURN = 106
ACT_STEPS_A_TURN = 12


def kernel(x, ctx_1024, L0_attn_gamma, L0_attn_w_q, L0_attn_w_kv, L0_attn_null_kv, L0_attn_q_scale,
           L0_attn_k_scale, L0_attn_w_out, L0_xattn_wq, L0_xattn_bq, L0_xattn_wk, L0_xattn_bk, L0_xattn_wv,
           L0_xattn_bv, L0_xattn_wo, L0_xattn_bo, L0_ffn_W1, L0_ffn_b1, L0_ffn_W2, L0_ffn_b2):
    import concourse.bacc as bacc
    from concourse.bass_utils import run_bass_kernel_spmd

    def pairs(w):
        return w.reshape(HP, P, w.shape[1]).transpose(1, 0, 2)

    def block_diagonal(w):
        w = np.asarray(w)
        m = np.zeros((P, P), w.dtype)
        for h in range(XH):
            m[XD * h:XD * (h + 1), XD * h:XD * (h + 1)] = w[h].T
        return m

    def halves_twice(m):
        m = m.reshape(m.shape[0], 2, DH)
        return np.concatenate([m, m], axis=2)

    w_q, w_kv, w_out = np.asarray(L0_attn_w_q), np.asarray(L0_attn_w_kv), np.asarray(L0_attn_w_out)
    nkv = np.asarray(L0_attn_null_kv).reshape(H, NULLS, 2, DH)
    nvT = np.zeros((HP, 2, DH, H, NULLS), nkv.dtype)
    for h in range(H):
        nvT[h // 2, h % 2, :, h, :] = nkv[h, :, 1].T
    q_pos, k_pos = np.arange(P)[:, None] + P, np.arange(SEQ)[None, :]
    dist = np.where(k_pos > q_pos, MASKED, q_pos - k_pos).astype(np.float32)
    null_dist = (np.arange(SEQ).reshape(NT, P, 1, 1) + NULLS - np.arange(NULLS)).astype(np.float32)
    nullbias = (null_dist * slopes()[None, None, :, None]).reshape(NT, P, NN).transpose(1, 0, 2)
    hmask = (np.arange(P)[:, None] // XD == np.arange(XH)[None, :]).astype(np.float32)
    hmask2 = (np.arange(P)[:, None] % DH // XD == np.arange(XHALF)[None, :]).astype(np.float32)
    arrays = {
        "x": x,
        "ctxT": np.asarray(ctx_1024).reshape(NB * CTX, P).T,
        "gamma": np.asarray(L0_attn_gamma).reshape(P, 1),
        "w_q": w_q,
        "w_kv": w_kv,
        "wqT": pairs(w_q.T),
        "wvT": pairs(w_kv[:, HD:].T),
        "wout": pairs(w_out),
        "nk": nkv[:, :, 0].reshape(NN, DH),
        "nvT": nvT.reshape(HP, P, NN).transpose(1, 0, 2),
        "q_scale": np.asarray(L0_attn_q_scale).reshape(DH, 1),
        "k_scale": np.asarray(L0_attn_k_scale).reshape(DH, 1),
        "xwq": halves_twice(block_diagonal(L0_xattn_wq)),
        "xwk": halves_twice(block_diagonal(L0_xattn_wk)),
        "xwv": block_diagonal(L0_xattn_wv),
        "xbq": halves_twice(np.asarray(L0_xattn_bq).reshape(1, P))[0].T,
        "xbk": halves_twice(np.asarray(L0_xattn_bk).reshape(1, P))[0].T,
        "xbv": np.asarray(L0_xattn_bv).reshape(P, 1),
        "xwoT": np.asarray(L0_xattn_wo).T,
        "xbo": np.asarray(L0_xattn_bo).reshape(1, P),
        "w1b": np.concatenate([np.asarray(L0_ffn_W1), np.asarray(L0_ffn_b1)[:, :, None]], axis=2),
        "w2T": np.asarray(L0_ffn_W2).transpose(0, 2, 1),
        "b2": np.asarray(L0_ffn_b2).reshape(GROUPS, P, 1),
        "ident_in": np.eye(P, dtype=np.float32),
        "dist_in": dist,
        "nullbias_in": nullbias,
        "hmask_in": hmask,
        "hmask2_in": hmask2,
    }
    arrays = {n: np.ascontiguousarray(a) for n, a in arrays.items()}
    nc = bacc.Bacc("TRN2", target_bir_lowering=False, num_devices=1)
    args = {n: nc.dram_tensor(n, a.shape, mybir.dt.from_np(a.dtype), kind="ExternalInput").ap()
            for n, a in arrays.items()}
    out = nc.dram_tensor("out", (NB, SEQ, P), F32, kind="ExternalOutput").ap()
    program(nc, **args, out=out)
    r = run_bass_kernel_spmd(nc, [arrays], core_ids=[0])
    return r.results[0]["out"]
```
